# Optimizing a Trainium2 kernel written in Bass

```python
import numpy as np
import jax
import jax.numpy as jnp

def _softmax(x, axis=-1):
    return jax.nn.softmax(x, axis=axis)

def _gelu(x):
    return jax.nn.gelu(x, approximate=True)

def _silu(x):
    return jax.nn.silu(x)

def _sigmoid(x):
    return jax.nn.sigmoid(x)

def _layernorm(x, axis=-1, eps=1e-05):
    m = jnp.mean(x, axis=axis, keepdims=True)
    v = jnp.var(x, axis=axis, keepdims=True)
    return (x - m) / jnp.sqrt(v + eps)

def _scatter_add(tgt, idx, src, axis=0):
    return tgt.at[idx].add(src)

def _segment_sum(src, seg, n):
    return jax.ops.segment_sum(src, seg, n)
kernel_name = 'mk_xattn_ffn_d1_seqx_r2_2a2aad'

def setup_inputs(seed: int=0):
    np.random.seed(seed)
    _w = jnp.asarray

    def _rec_inputs():
        import jax
        import jax.numpy as jnp
        _rk = jax.random.key(seed)
        x = 7.22e-05 + 1 * jax.random.normal(jax.random.fold_in(_rk, 1), (4, 2048, 512), jnp.float32)
        _lenS = 2048 - jax.random.randint(jax.random.fold_in(_rk, 7), (4,), 0, max(1, 2048 // 4) + 1, jnp.int32)
        _lenS2 = 128 - jax.random.randint(jax.random.fold_in(_rk, 8), (4,), 0, max(1, 128 // 4) + 1, jnp.int32)
        _ctx_1024P = jax.random.normal(jax.random.fold_in(_rk, 11), (4, 16, 512), jnp.float32)
        _ctx_1024c = jax.random.dirichlet(jax.random.fold_in(_rk, 511), 0.3 * jnp.ones((16,), jnp.float32), (4, 128))
        _ctx_1024t = jnp.einsum('bsk,bkd->bsd', _ctx_1024c, _ctx_1024P)
        _ctx_1024t = _ctx_1024t * jax.lax.rsqrt(jnp.mean(jnp.square(_ctx_1024t)) + 1e-12) * 0.953939
        ctx_1024 = 4.13588e-05 + 0.999923 * (_ctx_1024t + 0.3 * jax.random.normal(jax.random.fold_in(_rk, 611), (4, 128, 512), jnp.float32))
        _validS = jnp.arange(2048)[None, :] < _lenS[:, None]
        _validS2 = jnp.arange(128)[None, :] < _lenS2[:, None]
        _causal = jnp.tril(jnp.ones((2048, 2048), dtype=bool))
        mask_BxS2_bf1 = jnp.ones((4, 128), dtype=bool)
        return (x, ctx_1024, mask_BxS2_bf1)
    x, ctx_1024, mask_BxS2_bf1 = _rec_inputs()

    def _L0_xattn_setup():
        import jax, jax.numpy as jnp
        import numpy as np
        HEADS, QSIZE, KSIZE = (16, 64, 64)
        key = jax.random.key(seed)
        ks = jax.random.split(key, 8)
        B, S, D = (4, 1024, 512)
        sd = 1.0 / np.sqrt(D)
        return {'q_in': jax.random.normal(ks[0], (B, S, D), jnp.float32), 'k_in': jax.random.normal(ks[1], (B, S, D), jnp.float32), 'v_in': jax.random.normal(ks[2], (B, S, D), jnp.float32), 'key_mask': jnp.ones((B, S), dtype=bool), 'Wq': jax.random.normal(ks[3], (D, HEADS * QSIZE), jnp.float32) * sd, 'bq': jnp.zeros((HEADS * QSIZE,), jnp.float32), 'Wk': jax.random.normal(ks[4], (D, HEADS * QSIZE), jnp.float32) * sd, 'bk': jnp.zeros((HEADS * QSIZE,), jnp.float32), 'Wv': jax.random.normal(ks[5], (D, HEADS * KSIZE), jnp.float32) * sd, 'bv': jnp.zeros((HEADS * KSIZE,), jnp.float32), 'Wo': jax.random.normal(ks[6], (HEADS * KSIZE, D), jnp.float32) * sd, 'bo': jnp.zeros((D,), jnp.float32)}
    _L0_xattn_all = _L0_xattn_setup()
    _L0_xattn_in = {k: v for k, v in _L0_xattn_all.items() if k in ('Wq', 'bq', 'Wk', 'bk', 'Wv', 'bv', 'Wo', 'bo')}
    del _L0_xattn_all

    def _L0_ffn_setup():
        import jax, jax.numpy as jnp
        import numpy as np
        DIM = 512

        def _reference_tuple_inner(x, W_r, W_k, W_v, mu_r, mu_k):
            B, T, C = x.shape
            x_prev = jnp.concatenate([jnp.zeros((B, 1, C), x.dtype), x[:, :-1, :]], axis=1)
            xr = mu_r * x + (1.0 - mu_r) * x_prev
            xk = mu_k * x + (1.0 - mu_k) * x_prev
            r = jax.nn.sigmoid(jnp.einsum('btc,dc->btd', xr, W_r))
            k = jnp.einsum('btc,dc->btd', xk, W_k)
            k_act = jnp.square(jax.nn.relu(k))
            out = r * jnp.einsum('btc,dc->btd', k_act, W_v)
            new_state = x[:, -1, :]
            return (out, new_state)
        key = jax.random.key(seed)
        ks = jax.random.split(key, 6)
        B, T, C = (8, 1024, DIM)
        x = jax.random.normal(ks[0], (B, T, C), dtype=jnp.float32)
        s = 1.0 / np.sqrt(C)
        W_r = jax.random.uniform(ks[1], (C, C), jnp.float32, -s, s)
        W_k = jax.random.uniform(ks[2], (C, C), jnp.float32, -s, s)
        W_v = jax.random.uniform(ks[3], (C, C), jnp.float32, -s, s)
        mu_r = jax.random.uniform(ks[4], (C,), jnp.float32)
        mu_k = jax.random.uniform(ks[5], (C,), jnp.float32)
        return {'x': x, 'W_r': W_r, 'W_k': W_k, 'W_v': W_v, 'mu_r': mu_r, 'mu_k': mu_k}
    _L0_ffn_all = _L0_ffn_setup()
    _L0_ffn_in = {k: v for k, v in _L0_ffn_all.items() if k in ('W_r', 'W_k', 'W_v', 'mu_r', 'mu_k')}
    del _L0_ffn_all
    return {'x': x, 'ctx_1024': ctx_1024, 'mask_BxS2_bf1': mask_BxS2_bf1, 'L0_xattn_Wq': _L0_xattn_in['Wq'], 'L0_xattn_bq': _L0_xattn_in['bq'], 'L0_xattn_Wk': _L0_xattn_in['Wk'], 'L0_xattn_bk': _L0_xattn_in['bk'], 'L0_xattn_Wv': _L0_xattn_in['Wv'], 'L0_xattn_bv': _L0_xattn_in['bv'], 'L0_xattn_Wo': _L0_xattn_in['Wo'], 'L0_xattn_bo': _L0_xattn_in['bo'], 'L0_ffn_W_r': _L0_ffn_in['W_r'], 'L0_ffn_W_k': _L0_ffn_in['W_k'], 'L0_ffn_W_v': _L0_ffn_in['W_v'], 'L0_ffn_mu_r': _L0_ffn_in['mu_r'], 'L0_ffn_mu_k': _L0_ffn_in['mu_k']}

def reference(x, ctx_1024, mask_BxS2_bf1, L0_xattn_Wq, L0_xattn_bq, L0_xattn_Wk, L0_xattn_bk, L0_xattn_Wv, L0_xattn_bv, L0_xattn_Wo, L0_xattn_bo, L0_ffn_W_r, L0_ffn_W_k, L0_ffn_W_v, L0_ffn_mu_r, L0_ffn_mu_k):
    import jax
    import jax.numpy as jnp

    def _L0_xattn_ref(q_in, k_in, v_in, key_mask, Wq, bq, Wk, bk, Wv, bv, Wo, bo):
        import jax, jax.numpy as jnp
        import numpy as np
        HEADS, QSIZE, KSIZE = (16, 64, 64)
        B, M, _ = q_in.shape
        N = k_in.shape[1]
        qw = (q_in @ Wq + bq).reshape(B, M, HEADS, QSIZE)
        kw = (k_in @ Wk + bk).reshape(B, N, HEADS, QSIZE)
        vw = (v_in @ Wv + bv).reshape(B, N, HEADS, KSIZE)
        a = jnp.einsum('bmhd,bnhd->bhmn', qw, kw) / jnp.sqrt(jnp.float32(QSIZE))
        a = jnp.where(key_mask[:, None, None, :], a, -jnp.inf)
        a = jax.nn.softmax(a, axis=-1)
        o = jnp.einsum('bhmn,bnhd->bmhd', a, vw).reshape(B, M, HEADS * KSIZE)
        return o @ Wo + bo

    def _L0_ffn_ref(x, W_r, W_k, W_v, mu_r, mu_k):
        import jax, jax.numpy as jnp
        import numpy as np
        DIM = 512

        def _reference_tuple_inner(x, W_r, W_k, W_v, mu_r, mu_k):
            B, T, C = x.shape
            x_prev = jnp.concatenate([jnp.zeros((B, 1, C), x.dtype), x[:, :-1, :]], axis=1)
            xr = mu_r * x + (1.0 - mu_r) * x_prev
            xk = mu_k * x + (1.0 - mu_k) * x_prev
            r = jax.nn.sigmoid(jnp.einsum('btc,dc->btd', xr, W_r))
            k = jnp.einsum('btc,dc->btd', xk, W_k)
            k_act = jnp.square(jax.nn.relu(k))
            out = r * jnp.einsum('btc,dc->btd', k_act, W_v)
            new_state = x[:, -1, :]
            return (out, new_state)
        return _reference_tuple_inner(x, W_r, W_k, W_v, mu_r, mu_k)[0]
    x = x + _L0_xattn_ref(_layernorm(x, axis=-1), ctx_1024, ctx_1024, mask_BxS2_bf1, L0_xattn_Wq, L0_xattn_bq, L0_xattn_Wk, L0_xattn_bk, L0_xattn_Wv, L0_xattn_bv, L0_xattn_Wo, L0_xattn_bo)
    x = x + _L0_ffn_ref(_layernorm(x, axis=-1), L0_ffn_W_r, L0_ffn_W_k, L0_ffn_W_v, L0_ffn_mu_r, L0_ffn_mu_k)
    return x

_drawn_inputs = setup_inputs


def setup_inputs(seed=0):
    import zlib

    import numpy as np

    out = dict(_drawn_inputs(seed))
    spreads = {'L0_xattn_bq': (0.0, 0.286),
     'L0_xattn_bk': (0.0, 0.8),
     'L0_xattn_bv': (0.0, 0.1),
     'L0_xattn_bo': (0.0, 0.1)}
    factors = {'L0_ffn_W_r': 3.321, 'L0_ffn_mu_r': 8.0}
    for name, (base, spread) in spreads.items():
        noise = np.random.default_rng([zlib.crc32(name.encode()), seed]).standard_normal(out[name].shape)
        drawn = base * np.exp(spread * noise) if base else spread * noise
        out[name] = jnp.asarray(drawn.astype(out[name].dtype))
    for name, factor in factors.items():
        out[name] = (out[name] * factor).astype(out[name].dtype)
    return out
```

```python
import numpy as np
import concourse.bass as bass
from concourse import mybir
from contextlib import ExitStack

F32, F32R, U8 = mybir.dt.float32, mybir.dt.float32r, mybir.dt.uint8
ALU, ACT, AX = mybir.AluOpType, mybir.ActivationFunctionType, mybir.AxisListType

P = 128
B, S, D = 4, 2048, 512
KEYS, HEADS, DH = 128, 16, 64
HD = HEADS * DH
DC = D // P
PAIRS = HEADS // 2
TOK = 256
TT = TOK // P
TPB = S // TOK
TILES = B * TPB
N3 = 512
T3 = N3 // P
TPB3 = S // N3
SCALE = float(DH) ** -0.5
EPS = 1e-5
BIG = 3e38
ONE = 1


def split_passes(nc, out, w_h, w_l, x_h, x_l, first, last):
    nc.tensor.matmul(out, w_h, x_h, start=first, stop=False)
    nc.tensor.matmul(out, w_h, x_l, start=False, stop=False)
    return nc.tensor.matmul(out, w_l, x_h, start=False, stop=last)


def part1(nc, t, d):
    with ExitStack() as ctx:
        def sb(name, shape, dt=F32):
            return ctx.enter_context(nc.sbuf_tensor(name, shape, dt))

        def sem(name):
            return ctx.enter_context(nc.semaphore(name))

        raw = [sb(f"raw{i}", [P, 2, HD]) for i in range(2)]
        wk_h, wk_l = sb("wk_h", [P, DC, HD], F32R), sb("wk_l", [P, DC, HD], F32R)
        wv_h, wv_l = sb("wv_h", [P, DC, HD], F32R), sb("wv_l", [P, DC, HD], F32R)
        ctxn = sb("ctxn", [P, B, D])
        c_h, c_l = sb("c_h", [P, DC, B * KEYS], F32R), sb("c_l", [P, DC, B * KEYS], F32R)
        kout_h, kout_l = sb("kout_h", [P, 2, B * KEYS], F32R), sb("kout_l", [P, 2, B * KEYS], F32R)
        v32 = sb("v32", [P, 2, 512])
        bv_row = sb("bv_row", [P, HD])
        bk_col = sb("bk_col", [P, PAIRS])
        ident, ramp, ramp_col = sb("ident1", [P, P]), sb("ramp", [P, P]), sb("ramp_col", [P, 1])
        mask8 = sb("mask8", [P, B, KEYS], U8)
        mask = sb("mask", [P, B, KEYS])
        diag = sb("diag", [P, B, KEYS])
        ranked = sb("ranked", [P, B, KEYS])
        sel = sb("sel", [P, B, KEYS])
        best, mcol, nfirst, first = (sb(n, [P, B]) for n in ("best", "mcol", "nfirst", "first_valid"))
        ps = [ctx.enter_context(nc.psum_tensor(f"p1_{i}", [P, 512], F32)) for i in range(4)]

        small_in, mask_in, ctx_in = sem("small_in"), sem("mask_in"), sem("ctx_in")
        raw_in = [sem("raw_in0"), sem("raw_in1")]
        w_hi, w_lo = sem("w_hi"), sem("w_lo")
        dve_step = sem("p1_dve_step")
        sel_ready = sem("sel_ready")
        ctx_t, c_hi, c_lo = sem("ctx_t"), sem("c_hi"), sem("c_lo")
        k_mm, k_hi, k_lo = sem("k_mm"), sem("k_hi"), sem("k_lo")
        v_mm, v_f, v_hi, v_lo = sem("v_mm"), sem("v_f"), sem("v_hi"), sem("v_lo")
        out_h = [sem("kv_out0"), sem("kv_out1")]

        jobs = []
        for w, th, tl in ((d["Wk"], wk_h, wk_l), (d["Wv"], wv_h, wv_l), (d["Wq"], t["wq_h"], t["wq_l"])):
            v = w.rearrange("(c p) n -> p c n", p=P)
            jobs += [(v[:, 2 * i:2 * i + 2, :], th[:, 2 * i:2 * i + 2, :], tl[:, 2 * i:2 * i + 2, :]) for i in range(2)]
        v = d["Wo"].rearrange("(c p) n -> p c n", p=P)
        jobs += [(v[:, 4 * i:4 * i + 4, :], t["wo_h"][:, 4 * i:4 * i + 4, :], t["wo_l"][:, 4 * i:4 * i + 4, :]) for i in range(2)]

        def raw_of(i):
            r = raw[i % 2]
            return r[:, :, :] if i < 6 else r[:, :, :].rearrange("p a (b n) -> p (a b) n", n=D)

        with nc.Block() as block:
            @block.sync
            def _(sp):
                sp.dma_start(mask8[:, :, :], d["mask"].partition_broadcast(P)).then_inc(mask_in, 16)
                sp.dma_start(ident[:, :], d["ident"]).then_inc(mask_in, 16)
                sp.dma_start(ramp[:, :], d["ramp"]).then_inc(mask_in, 16)
                sp.dma_start(ramp_col[:, :], d["ramp_col"]).then_inc(mask_in, 16)
                sp.dma_start(ctxn[:, :, :], d["ctx"].rearrange("b k d -> k b d")).then_inc(ctx_in, 16)
                for i, (src, _, _) in enumerate(jobs):
                    if i >= 2:
                        sp.wait_ge(w_lo, i - 1)
                    sp.dma_start(raw_of(i), src).then_inc(raw_in[i % 2], 16)
                    if i == 1:
                        sp.dma_start(bk_col[:, :], d["bk"].rearrange("(c p) -> p c", p=P), allow_slow_non_contiguous=True).then_inc(small_in, 16)
                        sp.dma_start(t["bq_col"][:, :], d["bq"].rearrange("(c p) -> p c", p=P), allow_slow_non_contiguous=True).then_inc(small_in, 16)
                        sp.dma_start(bv_row[:, :], d["bv"].partition_broadcast(P)).then_inc(small_in, 16)
                        sp.dma_start(t["bo_row"][:, :], d["bo"].partition_broadcast(P)).then_inc(small_in, 16)
                sp.wait_ge(small_in, 64)

            @block.scalar
            def _(act):
                for c in range(DC):
                    act.wait_ge(ctx_t, c + 1)
                    nc.scalar.activation(c_h[:, c, :], ps[c % 2][:, :], ACT.Identity).then_inc(c_hi, 1)
                act.wait_ge(small_in, 64)
                for c in range(PAIRS):
                    act.wait_ge(k_mm, c + 1)
                    if c >= 2:
                        act.wait_ge(out_h[c % 2], 32 * (c // 2))
                    nc.scalar.activation(kout_h[:, c % 2, :], ps[c % 2][:, :], ACT.Identity,
                                         bias=bk_col[:, c:c + 1]).then_inc(k_hi, 1)
                    act.wait_ge(k_lo, c + 1)
                    act.wait_ge(k_hi, c + 1)
                    act.dma_start(d["k_h"][:, c, :], kout_h[:, c % 2, :].bitcast(F32)).then_inc(out_h[c % 2], 16)
                    act.dma_start(d["k_l"][:, c, :], kout_l[:, c % 2, :].bitcast(F32)).then_inc(out_h[c % 2], 16)
                for i in range(2 * B):
                    b, half = i // 2, i % 2
                    act.wait_ge(v_f, i + 1)
                    act.wait_ge(out_h[i % 2], 32 * (PAIRS // 2 + i // 2))
                    nc.scalar.activation(kout_h[:, i % 2, :], v32[:, i % 2, :], ACT.Identity).then_inc(v_hi, 1)
                    act.wait_ge(v_lo, i + 1)
                    act.wait_ge(v_hi, i + 1)
                    act.dma_start(d["v_h"][:, b, half * 512:half * 512 + 512], kout_h[:, i % 2, :].bitcast(F32)).then_inc(out_h[i % 2], 16)
                    act.dma_start(d["v_l"][:, b, half * 512:half * 512 + 512], kout_l[:, i % 2, :].bitcast(F32)).then_inc(out_h[i % 2], 16)
                for i in range(2):
                    act.wait_ge(out_h[i], 32 * (PAIRS // 2 + B))

            @block.gpsimd
            def _(pool):
                for i, (_, th, tl) in enumerate(jobs):
                    pool.wait_ge(w_hi, i + 1)
                    nc.gpsimd.tensor_tensor(tl, raw_of(i), th, ALU.subtract).then_inc(w_lo, 1)

            @block.vector
            def _(dve):
                steps = [0]

                def chained(ins):
                    steps[0] += 1
                    ins.then_inc(dve_step, 1)
                    dve.wait_ge(dve_step, steps[0])

                bcast = lambda x: x.unsqueeze(1).broadcast_to([P, B, KEYS])
                dve.wait_ge(mask_in, 64)
                chained(nc.vector.tensor_copy(mask[:, :, :], mask8[:, :, :]))
                chained(nc.vector.tensor_tensor(diag[:, :, :], mask[:, :, :], bcast(ident[:, :]), ALU.mult))
                chained(nc.vector.tensor_tensor(ranked[:, :, :], mask[:, :, :], bcast(ramp[:, :]), ALU.mult))
                chained(nc.vector.tensor_reduce(best[:, :], ranked[:, :, :], axis=AX.X, op=ALU.max))
                chained(nc.vector.tensor_reduce(mcol[:, :], diag[:, :, :], axis=AX.X, op=ALU.add))
                chained(nc.vector.tensor_scalar(first[:, :], best[:, :], ramp_col[:, 0:1], None, ALU.is_equal))
                chained(nc.vector.tensor_tensor(first[:, :], first[:, :], mcol[:, :], ALU.mult))
                chained(nc.vector.tensor_scalar(nfirst[:, :], first[:, :], -1.0, None, ALU.mult))
                for b in range(B):
                    chained(nc.vector.tensor_scalar(ranked[:, b, :], mask[:, b, :], nfirst[:, b:b + 1], first[:, b:b + 1], ALU.mult, ALU.add))
                nc.vector.tensor_tensor(sel[:, :, :], ranked[:, :, :], diag[:, :, :], ALU.add).then_inc(sel_ready, 1)
                chained(nc.vector.tensor_scalar(mcol[:, :], mcol[:, :], 1.0, BIG, ALU.subtract, ALU.mult))
                chained(nc.vector.tensor_scalar(t["mask_bias"][:, :], mcol[:, :], 10.0, None, ALU.mult))

                def hi(i):
                    dve.wait_ge(raw_in[i % 2], 16 * (i // 2 + 1))
                    nc.vector.tensor_copy(jobs[i][1], raw_of(i)).then_inc(w_hi, 1)

                hi(0)
                hi(1)
                for c in range(DC):
                    dve.wait_ge(c_hi, c + 1)
                    nc.vector.tensor_tensor(c_l[:, c, :], ps[c % 2][:, :], c_h[:, c, :], ALU.subtract).then_inc(c_lo, 1)
                hi(2)
                hi(3)
                dve.wait_ge(small_in, 64)
                for c in range(PAIRS):
                    dve.wait_ge(k_hi, c + 1)
                    nc.vector.scalar_tensor_tensor(kout_l[:, c % 2, :], ps[c % 2][:, :], bk_col[:, c:c + 1],
                                                   kout_h[:, c % 2, :], ALU.add, ALU.subtract).then_inc(k_lo, 1)
                    if c in (3, 5):
                        hi(4 + (c - 3) // 2)
                for i in range(2 * B):
                    dve.wait_ge(v_mm, i + 1)
                    nc.vector.tensor_tensor(v32[:, i % 2, :], ps[i % 2][:, :],
                                            bv_row[:, (i % 2) * 512:(i % 2) * 512 + 512], ALU.add).then_inc(v_f, 1)
                    dve.wait_ge(v_hi, i + 1)
                    nc.vector.tensor_tensor(kout_l[:, i % 2, :], v32[:, i % 2, :], kout_h[:, i % 2, :], ALU.subtract).then_inc(v_lo, 1)
                    if i in (2, 4):
                        hi(6 + (i - 2) // 2)

            @block.tensor
            def _(pe):
                pe.wait_ge(ctx_in, 16)
                pe.wait_ge(sel_ready, 1)
                for c in range(DC):
                    if c >= 2:
                        pe.wait_ge(c_lo, c - 1)
                    for b in range(B):
                        last = nc.tensor.matmul(ps[c % 2][:, b * KEYS:(b + 1) * KEYS], ctxn[:, b, c * P:(c + 1) * P],
                                                sel[:, b, :], start=True, stop=True)
                    last.then_inc(ctx_t, 1)
                pe.wait_ge(c_lo, DC)
                pe.wait_ge(w_lo, 2)
                for c in range(PAIRS):
                    if c >= 2:
                        pe.wait_ge(k_lo, c - 1)
                    for k in range(DC):
                        last = split_passes(nc, ps[c % 2][:, :], wk_h[:, k, c * P:(c + 1) * P], wk_l[:, k, c * P:(c + 1) * P],
                                            c_h[:, k, :], c_l[:, k, :], k == 0, k == DC - 1)
                    last.then_inc(k_mm, 1)
                pe.wait_ge(w_lo, 4)
                for i in range(2 * B):
                    b, n = i // 2, slice((i % 2) * 512, (i % 2) * 512 + 512)
                    if i < 2:
                        pe.wait_ge(k_lo, PAIRS - 1 + i)
                    else:
                        pe.wait_ge(v_f, i - 1)
                    for k in range(DC):
                        key = slice(b * KEYS, (b + 1) * KEYS)
                        last = split_passes(nc, ps[i % 2][:, :], c_h[:, k, key], c_l[:, k, key],
                                            wv_h[:, k, n], wv_l[:, k, n], k == 0, k == DC - 1)
                    last.then_inc(v_mm, 1)


def part2(nc, t, d):
    with ExitStack() as ctx:
        def sb(name, shape, dt=F32):
            return ctx.enter_context(nc.sbuf_tensor(name, shape, dt))

        def sem(name):
            return ctx.enter_context(nc.semaphore(name))

        def bank(name):
            return ctx.enter_context(nc.psum_tensor(name, [P, 512], F32))

        kz_h = sb("kz_h", [P, PAIRS, 2, KEYS], F32R)
        kz_l = sb("kz_l", [P, PAIRS, 2, KEYS], F32R)
        kg = sb("kg", [P, PAIRS, 2, KEYS], F32R)
        kb = sb("kb", [DH + 1, PAIRS, 2, KEYS], F32R)
        v1_h = sb("v1_h", [P, HEADS, P], F32R)
        vz_l = sb("vz_l", [P, HEADS, P], F32R)
        mb = sb("mb", [P, 1])
        ident = sb("ident2", [P, P])
        xa, xn = sb("xa", [P, TT, D]), sb("xn", [P, TT, D])
        x_h, x_l = sb("x_h", [P, DC, TOK], F32R), sb("x_l", [P, DC, TOK], F32R)
        q_h = sb("q_h", [P, PAIRS, TOK], F32R)
        q_l = sb("q_l", [DH + 1, HEADS, TOK], F32R)
        e32, e_h, e_l = sb("e32", [P, 2, 512]), sb("e_h", [P, 2, 512], F32R), sb("e_l", [P, 2, 512], F32R)
        lnz, inv0, res0, ninv = sb("lnz", [P, 512]), sb("inv0", [P, 2, 512]), sb("res0", [P, 512]), sb("ninv", [DH, 512])
        o32 = sb("o32", [P, 2, TOK])
        o_h, o_l = sb("o_h", [P, PAIRS, TOK], F32R), sb("o_l", [P, PAIRS, TOK], F32R)
        nmax, nmax_t = sb("nmax", [P, TT, HEADS]), sb("nmax_t", [HEADS, TOK], F32R)
        xr = sb("xr", [P, TT, D])
        st, mv = sb("st", [P, TT, 6]), sb("mv", [P, TT, 2])
        st1, mv1 = sb("st1", [P, 6]), sb("mv1", [P, 2])
        ve, y0, ya, rstd, nmr = (sb(n, [P, TT]) for n in ("ve", "y0", "ya", "rstd", "nmr"))
        pq, psc, px = [bank("pq0"), bank("pq1")], [bank("ps0"), bank("ps1")], [bank("px0"), bank("px1")]
        pg, py = bank("pg"), bank("py")

        const_in, kg_in, kv_in, v_in = sem("const_in"), sem("kg_in"), sem("kv_in"), sem("v_in")
        ones_set = sem("ones_set")
        xa_in, xr_in, m_in, x1_out = sem("xa_in"), sem("xr_in"), sem("m_in"), sem("x1_out")
        stats, var_ready, ln_y0, rstd_ready, xn_ready = sem("stats"), sem("var_ready"), sem("ln_y0"), sem("rstd_ready"), sem("xn_ready")
        rstd_step = sem("rstd_step")
        newton, xt_done, xh_done, xl_done = sem("newton"), sem("xt_done"), sem("xh_done"), sem("xl_done")
        q_mm, qh_done, ql_done = sem("q_mm"), sem("qh_done"), sem("ql_done")
        g_mm, max_done, maxt_mm, maxt_done = sem("g_mm"), sem("max_done"), sem("maxt_mm"), sem("maxt_done")
        s_mm, exp_done, el_done, pv_mm = sem("s_mm"), sem("exp_done"), sem("el_done"), sem("pv_mm")
        lnz_done, inv0_done, norm_step, o_done = sem("lnz_done"), sem("inv0_done"), sem("norm_step"), sem("o_done")
        oh_done, ol_done, xb_done, y_mm, x1_done = sem("oh_done"), sem("ol_done"), sem("xb_done"), sem("y_mm"), sem("x1_done")
        st1_done, mv1_done, x1_stats = sem("st1_done"), sem("mv1_done"), sem("x1_stats")
        AHEAD = 2

        x_t = d["x"].rearrange("(n j p) d -> n p j d", p=P, j=TT)
        x1_t = d["x1"].rearrange("(n j p) d -> n p j d", p=P, j=TT)

        def steps(eng, step):
            with eng.Fori(0, B - 1) as b:
                with eng.Fori(0, TPB - 1) as i:
                    step(b * TPB + i, b)
                step(b * TPB + (TPB - 1), b, switch=True)
            with eng.Fori((B - 1) * TPB, TILES - 2) as T:
                step(T, B - 1)
            step(TILES - 2, B - 1, after_next=False)
            step(TILES - 1, B - 1, after_next=False, next_tile=False)

        KG, KV, VV = 2, 7, 2

        with nc.Block() as block:
            @block.sync
            def _(sp):
                def key_slice(part, b):
                    return d[part][:, :, bass.ts(b, KEYS)]

                def load_kg(b):
                    for h in range(2):
                        r = slice(h * DH, (h + 1) * DH)
                        sp.dma_start(kg[r, :, h, :].bitcast(F32), key_slice("k_h", b)[r]).then_inc(kg_in, 16)

                def load_k(b):
                    for h in range(2):
                        r = slice(h * DH, (h + 1) * DH)
                        sp.dma_start(kz_h[r, :, h, :].bitcast(F32), key_slice("k_h", b)[r]).then_inc(kv_in, 16)
                        sp.dma_start(kz_l[r, :, h, :].bitcast(F32), key_slice("k_l", b)[r]).then_inc(kv_in, 16)
                        sp.dma_start(kb[0:DH, :, h, :].bitcast(F32), key_slice("k_h", b)[r]).then_inc(kv_in, 16)
                    sp.dma_start(mb[:, :], t["mask_bias"][:, bass.ts(b, 1)]).then_inc(kv_in, 16)

                def load_v(b):
                    for part, to in (("v_h", v1_h), ("v_l", vz_l)):
                        src = d[part][:, bass.ts(b, 1), :].rearrange("p o (h e) -> p (o h) e", e=DH)
                        sp.dma_start(to[:, :, 0:DH].bitcast(F32), src).then_inc(v_in, 16)

                def load_x(n, to, s):
                    sp.dma_start(to[:, :, :], x_t[n]).then_inc(s, 16)

                load_x(0, xa, xa_in)
                sp.dma_start(ident[:, :], d["ident"]).then_inc(const_in, 16)
                load_kg(0)
                load_k(0)
                load_v(0)
                sp.wait_ge(xn_ready, 2)
                load_x(1, xa, xa_in)
                sp.wait_ge(maxt_done, 1)
                sp.dma_start(q_l[DH:DH + 1, :, :].bitcast(F32), nmax_t[:, :].bitcast(F32)).then_inc(m_in, 16)

                def step(T, b, switch=False, after_next=True, next_tile=True):
                    if switch:
                        sp.wait_ge(g_mm, PAIRS * T + PAIRS)
                        load_kg(b + 1)
                    if after_next:
                        sp.wait_ge(xn_ready, TT * T + 2 * TT)
                        load_x(T + 2, xa, xa_in)
                    sp.wait_ge(x1_out, T * 16 + 16)
                    load_x(T, xr, xr_in)
                    if switch:
                        sp.wait_ge(exp_done, PAIRS * T + PAIRS + AHEAD)
                        load_k(b + 1)
                        sp.wait_ge(pv_mm, PAIRS * T + PAIRS + AHEAD)
                        load_v(b + 1)
                    if next_tile:
                        sp.wait_ge(maxt_done, T + 2)
                        sp.dma_start(q_l[DH:DH + 1, :, :].bitcast(F32), nmax_t[:, :].bitcast(F32)).then_inc(m_in, 16)
                    sp.wait_ge(x1_stats, TT * T + TT)
                    sp.dma_start(x1_t[T], xr[:, :, :]).then_inc(x1_out, 16)

                steps(sp, step)
                sp.wait_ge(x1_out, TILES * 16 + 16)

            @block.tensor
            def _(pe):
                def transposes(n):
                    pe.wait_ge(xn_ready, TT * n + TT)
                    for k in range(2):
                        for c in (2 * k, 2 * k + 1):
                            for j in range(TT):
                                at = (c % 2) * TOK + j * P
                                last = nc.tensor.transpose(pq[k][:, at:at + P], xn[:, j, c * P:(c + 1) * P], ident[:, :])
                        last.then_inc(xt_done, 1)

                def query(n, p):
                    if p == 0:
                        pe.wait_ge(xl_done, 2 * n + 2)
                    if p >= 2:
                        pe.wait_ge(ql_done, PAIRS * n + p - 1)
                    w = slice(p * P, (p + 1) * P)
                    for k in range(DC):
                        last = split_passes(nc, pq[p % 2][:, 0:TOK], t["wq_h"][:, k, w], t["wq_l"][:, k, w],
                                            x_h[:, k, :], x_l[:, k, :], k == 0, k == DC - 1)
                    last.then_inc(q_mm, 1)

                def guard(n, p, batch_keys=None):
                    if batch_keys is not None:
                        pe.wait_ge(kg_in, batch_keys)
                    if p == 0:
                        pe.wait_ge(maxt_done, n)
                    pe.wait_ge(max_done, PAIRS * n + p)
                    pe.wait_ge(qh_done, PAIRS * n + p + 1)
                    for j in range(TT):
                        last = nc.tensor.matmul(pg[:, j * TOK:(j + 1) * TOK], q_h[:, p, j * P:(j + 1) * P],
                                                kg[:, p, :, :].rearrange("p h k -> p (h k)"), start=True, stop=True)
                    last.then_inc(g_mm, 1)

                def max_transpose(n):
                    pe.wait_ge(max_done, PAIRS * n + PAIRS)
                    for j in range(TT):
                        last = nc.tensor.transpose(pg[0:HEADS, j * P:(j + 1) * P], nmax[:, j, :], ident[:, :])
                    last.then_inc(maxt_mm, 1)

                def scores(T, p, b):
                    if p == 0:
                        pe.wait_ge(m_in, 16 * T + 16)
                        pe.wait_ge(kv_in, 16 * KV * b + 16 * KV)
                    pe.wait_ge(exp_done, PAIRS * T + p - 2 + 1 + AHEAD)
                    for h in range(2):
                        out = psc[p % 2][:, h * TOK:(h + 1) * TOK]
                        nc.tensor.matmul(out, kz_h[:, p, h, :], q_h[:, p, :], start=True, stop=False)
                        nc.tensor.matmul(out, kz_l[:, p, h, :], q_h[:, p, :], start=False, stop=False)
                        last = nc.tensor.matmul(out, kb[:, p, h, :], q_l[:, 2 * p + h, :], start=False, stop=True)
                    last.then_inc(s_mm, 1)

                def values(T, p, b):
                    if p == 0:
                        pe.wait_ge(v_in, 16 * VV * b + 16 * VV)
                        pe.wait_ge(x1_done, TT * T + ONE)
                    pe.wait_ge(o_done, PAIRS * T + p - 2 + 1 + AHEAD)
                    pe.wait_ge(el_done, PAIRS * T + p + 1)
                    for h in range(2):
                        out, col = px[p % 2][:, h * TOK:(h + 1) * TOK], slice(h * TOK, (h + 1) * TOK)
                        last = split_passes(nc, out, v1_h[:, 2 * p + h, :], vz_l[:, 2 * p + h, :],
                                            e_h[:, p % 2, col], e_l[:, p % 2, col], True, True)
                    last.then_inc(pv_mm, 1)

                def output(T):
                    banks = (px[0], py)
                    pe.wait_ge(o_done, PAIRS * T + PAIRS - 1 + AHEAD)
                    pe.wait_ge(x1_done, TT * T + ONE)
                    pe.wait_ge(ol_done, PAIRS * T + PAIRS - 1 + AHEAD)
                    for part in (range(PAIRS - 1), (PAIRS - 1,)):
                        for j in range(TT):
                            if j == 0 and part == (PAIRS - 1,):
                                pe.wait_ge(ol_done, PAIRS * T + PAIRS + AHEAD)
                            for c in part:
                                w = slice(j * P, (j + 1) * P)
                                last = split_passes(nc, banks[j][:, :], o_h[:, c, w], o_l[:, c, w],
                                                    t["wo_h"][:, c, :], t["wo_l"][:, c, :], c == 0, c == PAIRS - 1)
                            if part == (PAIRS - 1,):
                                last.then_inc(y_mm, 1)

                pe.wait_ge(const_in, 16)
                pe.wait_ge(ones_set, 3)
                transposes(0)
                for p in range(PAIRS):
                    query(0, p)
                    if p:
                        guard(0, p - 1, 16 * KG if p == 1 else None)
                guard(0, PAIRS - 1)
                pe.wait_ge(ql_done, PAIRS)
                transposes(1)
                max_transpose(0)

                def step(T, b, switch=False, after_next=True, next_tile=True):
                    for p in range(PAIRS):
                        scores(T, p, b)
                        if next_tile:
                            query(T + 1, p)
                            if p:
                                guard(T + 1, p - 1, (b * 16 * KG + 2 * 16 * KG) if switch and p == 1 else None)
                        if p:
                            values(T, p - 1, b)
                    if next_tile:
                        guard(T + 1, PAIRS - 1)
                    values(T, PAIRS - 1, b)
                    if after_next:
                        pe.wait_ge(ql_done, PAIRS * T + 2 * PAIRS)
                        transposes(T + 2)
                    if next_tile:
                        max_transpose(T + 1)
                    output(T)

                steps(pe, step)

            @block.scalar
            def _(act):
                nc.scalar.preload_act_table_set("natural_log_exp_and_others")
                act.sem_inc(exp_done, AHEAD)
                act.sem_inc(inv0_done, ONE)

                def rsqrt_seed(n):
                    act.wait_ge(var_ready, n + 1)
                    nc.scalar.activation(y0[:, :], ve[:, :], ACT.Ln).then_inc(ln_y0, 1)
                    act.wait_ge(ln_y0, 2 * n + 1)
                    nc.scalar.activation(y0[:, :], y0[:, :], ACT.Exp, scale=-0.5).then_inc(ln_y0, 1)

                def normalise(n):
                    act.wait_ge(rstd_ready, n + 1)
                    act.wait_ge(xt_done, 2 * n)
                    for j in range(TT):
                        nc.scalar.activation(xn[:, j, :], xa[:, j, :], ACT.Identity, bias=nmr[:, j:j + 1],
                                             scale=rstd[:, j:j + 1]).then_inc(xn_ready, 1)

                def x_hi(n):
                    for k in range(2):
                        act.wait_ge(xt_done, 2 * n + k + 1)
                        nc.scalar.activation(x_h[:, 2 * k:2 * k + 2, :].rearrange("p c n -> p (c n)"), pq[k][:, :],
                                             ACT.Identity).then_inc(xh_done, 1)

                def q_hi(n, p):
                    act.wait_ge(q_mm, PAIRS * n + p + 1)
                    nc.scalar.activation(q_h[:, p, :], pq[p % 2][:, 0:TOK], ACT.Identity,
                                         bias=t["bq_col"][:, p:p + 1]).then_inc(qh_done, 1)

                def max_hi(n):
                    act.wait_ge(maxt_mm, n + 1)
                    nc.scalar.activation(nmax_t[:, :], pg[0:HEADS, 0:TOK], ACT.Identity).then_inc(maxt_done, 1)

                def exponentials(T, p, b):
                    if p == 0:
                        act.wait_ge(kv_in, 16 * KV * b + 16 * KV)
                    act.wait_ge(s_mm, PAIRS * T + p + 1)
                    act.wait_ge(pv_mm, PAIRS * T + p - 2 + 1 + AHEAD)
                    nc.scalar.activation(e32[:, p % 2, :], psc[p % 2][:, :], ACT.Exp, bias=mb[:, 0:1], scale=SCALE)
                    nc.scalar.activation(e_h[:, p % 2, :], psc[p % 2][:, :], ACT.Exp, bias=mb[:, 0:1],
                                         scale=SCALE).then_inc(exp_done, 1)

                def sum_inverse_seed(T, p):
                    act.wait_ge(inv0_done, PAIRS * T + p + ONE)
                    act.wait_ge(pv_mm, PAIRS * T + p + 1 + AHEAD)
                    nc.scalar.activation(lnz[DH:P, :], px[p % 2][DH:P, :], ACT.Ln).then_inc(lnz_done, 1)
                    act.wait_ge(lnz_done, PAIRS * T + p + 1)
                    act.wait_ge(o_done, PAIRS * T + p - 2 + 1 + AHEAD)
                    nc.scalar.activation(inv0[DH:P, p % 2, :], lnz[DH:P, :], ACT.Exp, scale=-1.0).then_inc(inv0_done, 1)

                def o_hi(T, p):
                    act.wait_ge(o_done, PAIRS * T + p + 1 + AHEAD)
                    nc.scalar.activation(o_h[:, p, :], o32[:, p % 2, :], ACT.Identity).then_inc(oh_done, 1)

                rsqrt_seed(0)
                normalise(0)
                x_hi(0)
                for p in range(PAIRS):
                    q_hi(0, p)
                    if p == 1:
                        rsqrt_seed(1)
                    if p == 3:
                        normalise(1)
                x_hi(1)
                max_hi(0)

                def step(T, b, switch=False, after_next=True, next_tile=True):
                    for p in range(PAIRS):
                        exponentials(T, p, b)
                        if next_tile:
                            q_hi(T + 1, p)
                        if p >= 1:
                            sum_inverse_seed(T, p - 1)
                        if p >= 2:
                            o_hi(T, p - 2)
                        if after_next and p == 3:
                            rsqrt_seed(T + 2)
                        if after_next and p == 5:
                            normalise(T + 2)
                    sum_inverse_seed(T, PAIRS - 1)
                    o_hi(T, PAIRS - 2)
                    if after_next:
                        x_hi(T + 2)
                    if next_tile:
                        max_hi(T + 1)
                    o_hi(T, PAIRS - 1)

                steps(act, step)

            @block.gpsimd
            def _(pool):
                pool.sem_inc(ol_done, AHEAD)

                def e_lo(T, p):
                    pool.wait_ge(exp_done, PAIRS * T + p + 1 + AHEAD)
                    nc.gpsimd.tensor_tensor(e_l[:, p % 2, :], e32[:, p % 2, :], e_h[:, p % 2, :], ALU.subtract).then_inc(el_done, 1)

                def o_lo(T, p):
                    pool.wait_ge(oh_done, PAIRS * T + p + 1)
                    nc.gpsimd.tensor_tensor(o_l[:, p, :], o32[:, p % 2, :], o_h[:, p, :], ALU.subtract).then_inc(ol_done, 1)

                def step(T, b, switch=False, after_next=True, next_tile=True):
                    for p in range(PAIRS):
                        e_lo(T, p)
                        if p >= 2:
                            o_lo(T, p - 2)
                        if p == 3:
                            pool.wait_ge(xr_in, 16 * T + 16)
                            nc.gpsimd.tensor_tensor(xr[:, :, :], xr[:, :, :],
                                                    t["bo_row"][:, :].unsqueeze(1).broadcast_to([P, TT, D]),
                                                    ALU.add).then_inc(xb_done, 1)
                    o_lo(T, PAIRS - 2)
                    o_lo(T, PAIRS - 1)

                steps(pool, step)

            @block.vector
            def _(dve):
                for m in (kz_h, kz_l, kg):
                    nc.vector.memset(m[0:DH, :, 1, :].bitcast(F32), 0.0)
                    nc.vector.memset(m[DH:P, :, 0, :].bitcast(F32), 0.0)
                nc.vector.memset(kb[DH:DH + 1, :, :, :].bitcast(F32), 1.0).then_inc(ones_set, 1)
                nc.vector.memset(v1_h[:, :, DH:P].bitcast(F32), 1.0).then_inc(ones_set, 1)
                nc.vector.memset(vz_l[:, :, DH:P].bitcast(F32), 0.0).then_inc(ones_set, 1)
                dve.sem_inc(pv_mm, AHEAD)
                dve.sem_inc(o_done, AHEAD)
                dve.sem_inc(x1_done, ONE)
                dve.sem_inc(x1_out, 16)


                def statistics(n):
                    dve.wait_ge(xa_in, 16 * n + 16)
                    for j in range(TT):
                        nc.vector.bn_stats(st[:, j, :], xa[:, j, :]).then_inc(stats, 1)
                    dve.drain()
                    for j in range(TT):
                        nc.vector.bn_aggr(mv[:, j, :], st[:, j, :]).then_inc(stats, 1)
                    dve.wait_ge(stats, 2 * TT * n + 2 * TT)
                    nc.vector.tensor_scalar(ve[:, :], mv[:, :, 1], EPS, None, ALU.add).then_inc(var_ready, 1)

                def rstd_newton(n):
                    dve.wait_ge(ln_y0, 2 * n + 2)
                    dve.wait_ge(xn_ready, TT * n)
                    nc.vector.tensor_tensor(ya[:, :], y0[:, :], y0[:, :], ALU.mult).then_inc(newton, 1)
                    dve.wait_ge(newton, 3 * n + 1)
                    nc.vector.tensor_tensor(ya[:, :], ya[:, :], ve[:, :], ALU.mult).then_inc(newton, 1)
                    dve.wait_ge(newton, 3 * n + 2)
                    nc.vector.tensor_scalar(ya[:, :], ya[:, :], -0.5, 1.5, ALU.mult, ALU.add).then_inc(newton, 1)
                    dve.wait_ge(newton, 3 * n + 3)
                    nc.vector.tensor_tensor(rstd[:, :], ya[:, :], y0[:, :], ALU.mult).then_inc(rstd_step, 1)
                    dve.wait_ge(rstd_step, n + 1)
                    nc.vector.scalar_tensor_tensor(nmr[:, :], mv[:, :, 0], -1.0, rstd[:, :], ALU.mult, ALU.mult).then_inc(rstd_ready, 1)

                def x_lo(n):
                    for k in range(2):
                        dve.wait_ge(xh_done, 2 * n + k + 1)
                        c = slice(2 * k, 2 * k + 2)
                        nc.vector.tensor_tensor(x_l[:, c, :].rearrange("p c n -> p (c n)"), pq[k][:, :],
                                                x_h[:, c, :].rearrange("p c n -> p (c n)"), ALU.subtract).then_inc(xl_done, 1)

                def q_lo(n, p):
                    dve.wait_ge(qh_done, PAIRS * n + p + 1)
                    for h in range(2):
                        r = slice(h * DH, (h + 1) * DH)
                        last = nc.vector.scalar_tensor_tensor(q_l[0:DH, 2 * p + h, :], pq[p % 2][r, 0:TOK],
                                                              t["bq_col"][r, p:p + 1], q_h[r, p, :], ALU.add, ALU.subtract)
                    last.then_inc(ql_done, 1)

                def maxima(n, p):
                    dve.wait_ge(g_mm, PAIRS * n + p + 1)
                    nc.vector.tensor_reduce(nmax[:, :, 2 * p:2 * p + 2],
                                            pg[:, :].rearrange("p (j h k) -> p j h k", j=TT, h=2),
                                            axis=AX.X, op=ALU.max, negate=True).then_inc(max_done, 1)

                def divide(T, p):
                    g = PAIRS * T + p
                    dve.wait_ge(inv0_done, g + 1 + ONE)
                    dve.wait_ge(ol_done, g - 2 + 1 + AHEAD)
                    nc.vector.tensor_tensor(res0[DH:P, :], px[p % 2][DH:P, :], inv0[DH:P, p % 2, :], ALU.mult).then_inc(norm_step, 1)
                    dve.wait_ge(norm_step, 2 * g + 1)
                    nc.vector.scalar_tensor_tensor(ninv[:, :], res0[DH:P, :], 2.0, inv0[DH:P, p % 2, :],
                                                   ALU.subtract, ALU.mult).then_inc(norm_step, 1)
                    dve.wait_ge(norm_step, 2 * g + 2)
                    for h in range(2):
                        col = slice(h * TOK, (h + 1) * TOK)
                        last = nc.vector.scalar_tensor_tensor(o32[h * DH:(h + 1) * DH, p % 2, :], px[p % 2][0:DH, col],
                                                              -1.0, ninv[:, col], ALU.mult, ALU.mult)
                    last.then_inc(o_done, 1)

                def residual(T):
                    dve.wait_ge(xb_done, T + 1)
                    for j in range(TT):
                        n = TT * T + j
                        dve.wait_ge(y_mm, n + 1)
                        nc.vector.tensor_tensor(xr[:, j, :], (px[0], py)[j][:, :], xr[:, j, :], ALU.add).then_inc(x1_done, 1)
                        dve.wait_ge(x1_done, n + 1 + ONE)
                        nc.vector.bn_stats(st1[:, :], xr[:, j, :]).then_inc(st1_done, 1)
                        dve.drain()
                        nc.vector.bn_aggr(mv1[:, :], st1[:, :]).then_inc(mv1_done, 1)
                        dve.wait_ge(mv1_done, n + 1)
                        nc.vector.tensor_copy(t["mv_all"][:, bass.ds(n, 1), :], mv1[:, :].unsqueeze(1)).then_inc(x1_stats, 1)

                statistics(0)
                rstd_newton(0)
                x_lo(0)
                statistics(1)
                for p in range(PAIRS):
                    q_lo(0, p)
                    if p == 2:
                        rstd_newton(1)
                    if p:
                        maxima(0, p - 1)
                maxima(0, PAIRS - 1)
                x_lo(1)

                def step(T, b, switch=False, after_next=True, next_tile=True):
                    for p in range(PAIRS):
                        if next_tile:
                            q_lo(T + 1, p)
                            if p:
                                maxima(T + 1, p - 1)
                        if p:
                            divide(T, p - 1)
                        if after_next and p == 2:
                            statistics(T + 2)
                        if after_next and p == 4:
                            rstd_newton(T + 2)
                    if next_tile:
                        maxima(T + 1, PAIRS - 1)
                    divide(T, PAIRS - 1)
                    if after_next:
                        x_lo(T + 2)
                    residual(T)

                steps(dve, step)


def part3(nc, t, d):
    with ExitStack() as ctx:
        def sb(name, shape, dt=F32):
            return ctx.enter_context(nc.sbuf_tensor(name, shape, dt))

        def sem(name):
            return ctx.enter_context(nc.semaphore(name))

        def bank(name):
            return ctx.enter_context(nc.psum_tensor(name, [P, 512], F32))

        W = ("W_k", "W_r", "W_v")
        w_h = {w: sb(f"{w}_h", [P, DC, D], F32R) for w in W}
        w_l = {w: sb(f"{w}_l", [P, DC, D], F32R) for w in W}
        wraw = sb("wraw", [P, DC, D])
        ident = sb("ident3", [P, P])
        mu = {"r": sb("mu_r", [P, DC]), "k": sb("mu_k", [P, DC])}
        NT = TILES * TT
        ve, y0, ya, rstd, nmr = (sb(n, [P, NT]) for n in ("ve3", "y3", "ya3", "rstd3", "nmr3"))
        x1 = sb("x1", [P, 2, T3, D])
        xn = sb("xn3", [P, T3, D])
        xt = sb("xt", [P, DC, 1 + N3])
        dx = sb("dx", [P, DC, N3])
        mix = sb("mix", [P, 2, N3])
        m_h = {"r": sb("mr_h", [P, DC, N3], F32R), "k": sb("mk_h", [P, DC, N3], F32R)}
        m_l = {"r": sb("mr_l", [P, DC, N3], F32R), "k": sb("mk_l", [P, DC, N3], F32R)}
        rl, a32 = sb("rl", [P, 2, N3]), sb("a32", [P, 2, N3])
        a_h, a_l = sb("a_h", [P, DC, N3], F32R), sb("a_l", [P, DC, N3], F32R)
        gate = sb("gate", [P, T3, D])
        res = sb("res", [P, T3, D])
        pt, pk, pr = [bank("pt0"), bank("pt1")], [bank("pk0"), bank("pk1")], [bank(f"pr{i}") for i in range(4)]

        w_in, mu_in, id_in = sem("w_in"), sem("mu_in"), sem("id_in")
        wt_mm, wh_done, wl_done = sem("wt_mm"), sem("wh_done"), sem("wl_done")
        r_step, lnv_done, y0_done, rstd_done = sem("r_step"), sem("lnv_done"), sem("y03_done"), sem("rstd3_done")
        x1_in = [sem("x1_in0"), sem("x1_in1")]
        xn_done, xt_mm, xt_cp, carry, dx_done = sem("xn3_done"), sem("xt_mm"), sem("xt_cp"), sem("carry"), sem("dx_done")
        mix_done, mh_done, ml_done = sem("mix_done"), sem("mh_done"), sem("ml_done")
        k_mm, rl_done, ah_done, a32_done, al_done = sem("k3_mm"), sem("rl_done"), sem("ah_done"), sem("a32_done"), sem("al_done")
        r_mm, gate_done, v_mm, gv_done, res_done, out_st = sem("r3_mm"), sem("gate_done"), sem("v3_mm"), sem("gv_done"), sem("res_done"), sem("out_st")

        x1_t = d["x1"].rearrange("(n j p) d -> n p j d", p=P, j=T3)
        out_t = d["out"].rearrange("(n j p) d -> n p j d", p=P, j=T3)
        LAST = B * TPB3 - 1

        def steps(eng, step):
            with eng.Fori(0, B - 1) as b:
                for i in range(TPB3):
                    step(b * TPB3 + i, i)
            for i in range(TPB3):
                step((B - 1) * TPB3 + i, i)

        with nc.Block() as block:
            @block.sync
            def _(sp):
                sp.dma_start(ident[:, :], d["ident"]).then_inc(id_in, 16)
                for i, w in enumerate(W):
                    if i:
                        sp.wait_ge(wt_mm, DC * i)
                    sp.dma_start(wraw[:, :, :], d[w].rearrange("(c p) n -> p c n", p=P)).then_inc(w_in, 16)
                    if i == 0:
                        sp.dma_start(x1[:, 0, :, :], x1_t[0]).then_inc(x1_in[0], 16)
                        sp.dma_start(mu["r"][:, :], d["mu_r"].rearrange("(c p) -> p c", p=P), allow_slow_non_contiguous=True).then_inc(mu_in, 16)
                        sp.dma_start(mu["k"][:, :], d["mu_k"].rearrange("(c p) -> p c", p=P), allow_slow_non_contiguous=True).then_inc(mu_in, 16)

                def step(n, i):
                    if not (type(n) is int and n == LAST):
                        sp.wait_ge(res_done, n * T3 + ONE)
                        sp.dma_start(x1[:, (i + 1) % 2, :, :], x1_t[n + 1]).then_inc(x1_in[(i + 1) % 2], 16)
                    sp.wait_ge(res_done, n * T3 + T3 + ONE)
                    sp.dma_start(out_t[n], res[:, :, :]).then_inc(out_st, 16)

                steps(sp, step)
                sp.wait_ge(out_st, 16 * (LAST + 1) + 16)

            @block.tensor
            def _(pe):
                pe.wait_ge(id_in, 16)
                for i, w in enumerate(W):
                    pe.wait_ge(w_in, 16 * (i + 1))
                    for c in range(DC):
                        n = DC * i + c
                        if n >= 2:
                            pe.wait_ge(wl_done, n - 1)
                        for o in range(DC):
                            last = nc.tensor.transpose(pt[n % 2][:, o * P:(o + 1) * P], wraw[:, o, c * P:(c + 1) * P], ident[:, :])
                        last.then_inc(wt_mm, 1)
                pe.wait_ge(wl_done, DC * len(W))

                def transposes(n):
                    for c in range(DC):
                        if c < 2:
                            pe.wait_ge(xt_cp, DC * n)
                        else:
                            pe.wait_ge(xt_cp, DC * n + c - 1)
                        for j in range(T3):
                            if c == 0:
                                pe.wait_ge(xn_done, T3 * n + j + 1)
                            last = nc.tensor.transpose(pt[c % 2][:, j * P:(j + 1) * P], xn[:, j, c * P:(c + 1) * P], ident[:, :])
                        last.then_inc(xt_mm, 1)

                transposes(0)

                def step(n, i):
                    for c in range(DC):
                        pe.wait_ge(rl_done, DC * n + c - 2 + 1 + 2)
                        if c == 0:
                            pe.wait_ge(ml_done, 2 * DC * n + DC)
                        for k in range(DC):
                            last = split_passes(nc, pk[c % 2][:, :], w_h["W_k"][:, k, c * P:(c + 1) * P],
                                                w_l["W_k"][:, k, c * P:(c + 1) * P], m_h["k"][:, k, :], m_l["k"][:, k, :],
                                                k == 0, k == DC - 1)
                        last.then_inc(k_mm, 1)
                    for j in range(T3):
                        if j == 0:
                            pe.wait_ge(gv_done, T3 * n + ONE)
                            pe.wait_ge(ml_done, 2 * DC * n + 2 * DC)
                        w = slice(j * P, (j + 1) * P)
                        for k in range(DC):
                            last = split_passes(nc, pr[j][:, :], m_h["r"][:, k, w], m_l["r"][:, k, w],
                                                w_h["W_r"][:, k, :], w_l["W_r"][:, k, :], k == 0, k == DC - 1)
                        last.then_inc(r_mm, 1)
                    if not (type(n) is int and n == LAST):
                        transposes(n + 1)
                    for j in range(T3):
                        pe.wait_ge(gate_done, T3 * n + j + 1)
                        if j == 0:
                            pe.wait_ge(al_done, DC * n + DC + 2)
                        w = slice(j * P, (j + 1) * P)
                        for k in range(DC):
                            last = split_passes(nc, pr[j][:, :], a_h[:, k, w], a_l[:, k, w],
                                                w_h["W_v"][:, k, :], w_l["W_v"][:, k, :], k == 0, k == DC - 1)
                        last.then_inc(v_mm, 1)

                steps(pe, step)

            @block.scalar
            def _(act):
                nc.scalar.preload_act_table_set("natural_log_exp_and_others")
                act.sem_inc(rl_done, 2)
                act.wait_ge(r_step, 1)
                nc.scalar.activation(y0[:, :], ve[:, :], ACT.Ln).then_inc(lnv_done, 1)
                act.wait_ge(lnv_done, 1)
                nc.scalar.activation(y0[:, :], y0[:, :], ACT.Exp, scale=-0.5).then_inc(y0_done, 1)
                for n in range(DC * len(W)):
                    act.wait_ge(wt_mm, n + 1)
                    nc.scalar.activation(w_h[W[n // DC]][:, n % DC, :], pt[n % 2][:, :], ACT.Identity).then_inc(wh_done, 1)

                def normalise(n, buf, loads):
                    act.wait_ge(x1_in[buf], loads)
                    act.wait_ge(xt_mm, DC * n)
                    for j in range(T3):
                        at = bass.ds(T3 * n + j, 1)
                        nc.scalar.activation(xn[:, j, :], x1[:, buf, j, :], ACT.Identity, bias=nmr[:, at],
                                             scale=rstd[:, at]).then_inc(xn_done, 1)

                def xt_copy(n):
                    act.wait_ge(carry, n + 1)
                    for c in range(DC):
                        act.wait_ge(xt_mm, DC * n + c + 1)
                        nc.scalar.activation(xt[:, c, 1:1 + N3], pt[c % 2][:, :], ACT.Identity).then_inc(xt_cp, 1)

                def mix_hi(n, which):
                    name = "kr"[which]
                    for c in range(DC):
                        at = 2 * DC * n + DC * which + c
                        act.wait_ge(mix_done, at + 1)
                        nc.scalar.activation(m_h[name][:, c, :], mix[:, c % 2, :], ACT.Identity).then_inc(mh_done, 1)

                nc.scalar.preload_act_table_set("sigmoid_and_others")
                act.wait_ge(rstd_done, 1)
                normalise(0, 0, 16)
                xt_copy(0)
                mix_hi(0, 0)
                mix_hi(0, 1)

                def step(n, i):
                    more = not (type(n) is int and n == LAST)
                    if more:
                        count = (n + 1 - (i + 1) % 2) * 8 + 16
                        normalise(n + 1, (i + 1) % 2, count)
                    for c in range(DC):
                        act.wait_ge(k_mm, DC * n + c + 1)
                        act.wait_ge(al_done, DC * n + c - 2 + 1 + 2)
                        nc.scalar.activation(rl[:, c % 2, :], pk[c % 2][:, :], ACT.Relu).then_inc(rl_done, 1)
                        act.wait_ge(rl_done, DC * n + c + 1 + 2)
                        nc.scalar.activation(a_h[:, c, :], rl[:, c % 2, :], ACT.Square).then_inc(ah_done, 1)
                    for j in range(T3):
                        act.wait_ge(r_mm, T3 * n + j + 1)
                        nc.scalar.activation(gate[:, j, :], pr[j][:, :], ACT.Sigmoid).then_inc(gate_done, 1)
                    if more:
                        xt_copy(n + 1)
                        mix_hi(n + 1, 0)
                        mix_hi(n + 1, 1)

                steps(act, step)

            @block.gpsimd
            def _(pool):
                def differences(n):
                    pool.wait_ge(ml_done, 2 * DC * n)
                    for c in range(DC):
                        pool.wait_ge(xt_cp, DC * n + c + 1)
                        nc.gpsimd.tensor_tensor(dx[:, c, :], xt[:, c, 1:1 + N3], xt[:, c, 0:N3], ALU.subtract).then_inc(dx_done, 1)

                differences(0)

                def step(n, i):
                    if not (type(n) is int and n == LAST):
                        differences(n + 1)
                    for j in range(T3):
                        pool.wait_ge(gv_done, T3 * n + j + 1 + ONE)
                        nc.gpsimd.tensor_tensor(res[:, j, :], res[:, j, :], x1[:, i % 2, j, :], ALU.add).then_inc(res_done, 1)

                steps(pool, step)

            @block.vector
            def _(dve):
                dve.sem_inc(al_done, 2)
                dve.sem_inc(res_done, ONE)
                dve.sem_inc(gv_done, ONE)
                dve.sem_inc(out_st, 16)
                nc.vector.tensor_scalar(ve[:, :], t["mv_all"][:, :, 1], EPS, None, ALU.add).then_inc(r_step, 1)
                dve.wait_ge(y0_done, 1)
                nc.vector.tensor_tensor(ya[:, :], y0[:, :], y0[:, :], ALU.mult).then_inc(r_step, 1)
                dve.wait_ge(r_step, 2)
                nc.vector.tensor_tensor(ya[:, :], ya[:, :], ve[:, :], ALU.mult).then_inc(r_step, 1)
                dve.wait_ge(r_step, 3)
                nc.vector.tensor_scalar(ya[:, :], ya[:, :], -0.5, 1.5, ALU.mult, ALU.add).then_inc(r_step, 1)
                dve.wait_ge(r_step, 4)
                nc.vector.tensor_tensor(rstd[:, :], ya[:, :], y0[:, :], ALU.mult).then_inc(r_step, 1)
                dve.wait_ge(r_step, 5)
                nc.vector.scalar_tensor_tensor(nmr[:, :], t["mv_all"][:, :, 0], -1.0, rstd[:, :], ALU.mult, ALU.mult).then_inc(rstd_done, 1)
                for n in range(DC * len(W)):
                    dve.wait_ge(wh_done, n + 1)
                    nc.vector.tensor_tensor(w_l[W[n // DC]][:, n % DC, :], pt[n % 2][:, :], w_h[W[n // DC]][:, n % DC, :],
                                            ALU.subtract).then_inc(wl_done, 1)

                def keep_last(n, first_of_batch):
                    dve.wait_ge(dx_done, DC * n)
                    if first_of_batch:
                        nc.vector.memset(xt[:, :, 0:1], 0.0).then_inc(carry, 1)
                    else:
                        nc.vector.tensor_copy(xt[:, :, 0:1], xt[:, :, N3:N3 + 1]).then_inc(carry, 1)

                def mixes(n, which):
                    name = "kr"[which]
                    if which:
                        dve.wait_ge(r_mm, T3 * n)
                    else:
                        dve.wait_ge(k_mm, DC * n)

                    def lo(c):
                        at = 2 * DC * n + DC * which + c
                        dve.wait_ge(mh_done, at + 1)
                        nc.vector.tensor_tensor(m_l[name][:, c, :], mix[:, c % 2, :], m_h[name][:, c, :], ALU.subtract).then_inc(ml_done, 1)

                    for c in range(DC):
                        if which == 0:
                            dve.wait_ge(dx_done, DC * n + c + 1)
                        if c >= 2:
                            lo(c - 2)
                        if not (type(n) is int and n == 0 and which == 0 and c < 2):
                            dve.wait_ge(ml_done, 2 * DC * n + DC * which + c - 1)
                        nc.vector.scalar_tensor_tensor(mix[:, c % 2, :], dx[:, c, :], mu[name][:, c:c + 1], xt[:, c, 0:N3],
                                                       ALU.mult, ALU.add).then_inc(mix_done, 1)
                    lo(DC - 2)
                    lo(DC - 1)

                dve.wait_ge(mu_in, 32)
                keep_last(0, True)
                mixes(0, 0)
                mixes(0, 1)

                def step(n, i):
                    for c in range(DC):
                        dve.wait_ge(rl_done, DC * n + c + 1 + 2)
                        nc.vector.tensor_tensor(a32[:, c % 2, :], rl[:, c % 2, :], rl[:, c % 2, :], ALU.mult).then_inc(a32_done, 1)
                        dve.wait_ge(a32_done, DC * n + c + 1)
                        dve.wait_ge(ah_done, DC * n + c + 1)
                        nc.vector.tensor_tensor(a_l[:, c, :], a32[:, c % 2, :], a_h[:, c, :], ALU.subtract).then_inc(al_done, 1)
                    if not (type(n) is int and n == LAST):
                        keep_last(n + 1, i == TPB3 - 1)
                        mixes(n + 1, 0)
                        mixes(n + 1, 1)
                    for j in range(T3):
                        if j == 0:
                            dve.wait_ge(out_st, 16 * n + 16)
                        dve.wait_ge(v_mm, T3 * n + j + 1)
                        nc.vector.tensor_tensor(res[:, j, :], pr[j][:, :], gate[:, j, :], ALU.mult).then_inc(gv_done, 1)

                steps(dve, step)


def build(nc, x, ctx, mask, Wq, bq, Wk, bk, Wv, bv, Wo, bo, W_r, W_k, W_v, mu_r, mu_k, ident, ramp, ramp_col, out):
    d = dict(ctx=ctx, mask=mask, Wq=Wq, bq=bq, Wk=Wk, bk=bk, Wv=Wv, bv=bv, Wo=Wo, bo=bo, W_r=W_r, W_k=W_k, W_v=W_v,
             mu_r=mu_r, mu_k=mu_k, ident=ident, ramp=ramp, ramp_col=ramp_col,
             x=x.rearrange("b s d -> (b s) d"), out=out.rearrange("b s d -> (b s) d"))
    d["x1"] = nc.dram_tensor("x1_scratch", [B * S, D], F32).ap()
    for n in ("k_h", "k_l"):
        d[n] = nc.dram_tensor(f"{n}_scratch", [P, PAIRS, B * KEYS], F32).ap()
    for n in ("v_h", "v_l"):
        d[n] = nc.dram_tensor(f"{n}_scratch", [P, B, HD], F32).ap()
    with ExitStack() as c:
        def sb(name, shape, dt=F32):
            return c.enter_context(nc.sbuf_tensor(name, shape, dt))
        t = dict(mv_all=sb("mv_all", [P, TILES * TT, 2]))
        with ExitStack() as c2:
            def sb2(name, shape, dt=F32):
                return c2.enter_context(nc.sbuf_tensor(name, shape, dt))
            t.update(wq_h=sb2("wq_h", [P, DC, HD], F32R), wq_l=sb2("wq_l", [P, DC, HD], F32R),
                     wo_h=sb2("wo_h", [P, PAIRS, D], F32R), wo_l=sb2("wo_l", [P, PAIRS, D], F32R),
                     bq_col=sb2("bq_col", [P, PAIRS]), bo_row=sb2("bo_row", [P, D]), mask_bias=sb2("mask_bias", [P, B]))
            part1(nc, t, d)
            part2(nc, t, d)
        part3(nc, t, d)


_INS = ['x', 'ctx_1024', 'mask_BxS2_bf1', 'L0_xattn_Wq', 'L0_xattn_bq', 'L0_xattn_Wk', 'L0_xattn_bk', 'L0_xattn_Wv',
        'L0_xattn_bv', 'L0_xattn_Wo', 'L0_xattn_bo', 'L0_ffn_W_r', 'L0_ffn_W_k', 'L0_ffn_W_v', 'L0_ffn_mu_r', 'L0_ffn_mu_k']


def kernel(**inputs):
    import concourse.bacc as bacc
    from concourse.bass_utils import run_bass_kernel_spmd

    nc = bacc.Bacc("TRN2", target_bir_lowering=False, num_devices=1)
    given = [(n, np.ascontiguousarray(inputs[n])) for n in _INS]
    down = (KEYS - np.arange(KEYS)).astype(np.float32)
    given += [("ident", np.eye(P, dtype=np.float32)), ("ramp", np.tile(down, (P, 1))), ("ramp_col", down[:, None].copy())]
    arrays, args = {}, []
    for name, a in given:
        arrays[f"in_{name}_dram"] = a
        args.append(nc.dram_tensor(f"in_{name}_dram", a.shape, mybir.dt.from_np(a.dtype), kind="ExternalInput").ap())
    args.append(nc.dram_tensor("out_0_dram", (B, S, D), F32, kind="ExternalOutput").ap())
    build(nc, *args)
    r = run_bass_kernel_spmd(nc, [arrays], core_ids=[0])
    return r.results[0]["out_0_dram"]
```

```python
import numpy as np
import concourse.bass as bass
from concourse import mybir
from contextlib import ExitStack

F32, F32R, U8 = mybir.dt.float32, mybir.dt.float32r, mybir.dt.uint8
ALU, ACT, AX = mybir.AluOpType, mybir.ActivationFunctionType, mybir.AxisListType

P = 128
B, S, D = 4, 2048, 512
KEYS, HEADS, DH = 128, 16, 64
HD = HEADS * DH
DC = D // P
PAIRS = HEADS // 2
TOK = 256
TT = TOK // P
TPB = S // TOK
TILES = B * TPB
N3 = 512
T3 = N3 // P
TPB3 = S // N3
SCALE = float(DH) ** -0.5
EPS = 1e-5
BIG = 3e38
ONE = 1


def split_passes(nc, out, w_h, w_l, x_h, x_l, first, last):
    nc.tensor.matmul(out, w_h, x_h, start=first, stop=False)
    nc.tensor.matmul(out, w_h, x_l, start=False, stop=False)
    return nc.tensor.matmul(out, w_l, x_h, start=False, stop=last)


def part1(nc, t, d):
    with ExitStack() as ctx:
        def sb(name, shape, dt=F32):
            return ctx.enter_context(nc.sbuf_tensor(name, shape, dt))

        def sem(name):
            return ctx.enter_context(nc.semaphore(name))

        raw = [sb(f"raw{i}", [P, 2, HD]) for i in range(2)]
        wk_h, wk_l = sb("wk_h", [P, DC, HD], F32R), sb("wk_l", [P, DC, HD], F32R)
        wv_h, wv_l = sb("wv_h", [P, DC, HD], F32R), sb("wv_l", [P, DC, HD], F32R)
        ctxn = sb("ctxn", [P, B, D])
        c_h, c_l = sb("c_h", [P, DC, B * KEYS], F32R), sb("c_l", [P, DC, B * KEYS], F32R)
        kout_h, kout_l = sb("kout_h", [P, 2, B * KEYS], F32R), sb("kout_l", [P, 2, B * KEYS], F32R)
        v32 = sb("v32", [P, 2, 512])
        bv_row = sb("bv_row", [P, HD])
        bk_col = sb("bk_col", [P, PAIRS])
        ident, ramp, ramp_col = sb("ident1", [P, P]), sb("ramp", [P, P]), sb("ramp_col", [P, 1])
        mask8 = sb("mask8", [P, B, KEYS], U8)
        mask = sb("mask", [P, B, KEYS])
        diag = sb("diag", [P, B, KEYS])
        ranked = sb("ranked", [P, B, KEYS])
        sel = sb("sel", [P, B, KEYS])
        best, mcol, nfirst, first = (sb(n, [P, B]) for n in ("best", "mcol", "nfirst", "first_valid"))
        ps = [ctx.enter_context(nc.psum_tensor(f"p1_{i}", [P, 512], F32)) for i in range(4)]

        small_in, mask_in, ctx_in = sem("small_in"), sem("mask_in"), sem("ctx_in")
        raw_in = [sem("raw_in0"), sem("raw_in1")]
        w_hi, w_lo = sem("w_hi"), sem("w_lo")
        dve_step = sem("p1_dve_step")
        sel_ready = sem("sel_ready")
        ctx_t, c_hi, c_lo = sem("ctx_t"), sem("c_hi"), sem("c_lo")
        k_mm, k_hi, k_lo = sem("k_mm"), sem("k_hi"), sem("k_lo")
        v_mm, v_f, v_hi, v_lo = sem("v_mm"), sem("v_f"), sem("v_hi"), sem("v_lo")
        out_h = [sem("kv_out0"), sem("kv_out1")]

        jobs = []
        for w, th, tl in ((d["Wk"], wk_h, wk_l), (d["Wv"], wv_h, wv_l), (d["Wq"], t["wq_h"], t["wq_l"])):
            v = w.rearrange("(c p) n -> p c n", p=P)
            jobs += [(v[:, 2 * i:2 * i + 2, :], th[:, 2 * i:2 * i + 2, :], tl[:, 2 * i:2 * i + 2, :]) for i in range(2)]
        v = d["Wo"].rearrange("(c p) n -> p c n", p=P)
        jobs += [(v[:, 4 * i:4 * i + 4, :], t["wo_h"][:, 4 * i:4 * i + 4, :], t["wo_l"][:, 4 * i:4 * i + 4, :]) for i in range(2)]

        def raw_of(i):
            r = raw[i % 2]
            return r[:, :, :] if i < 6 else r[:, :, :].rearrange("p a (b n) -> p (a b) n", n=D)

        with nc.Block() as block:
            @block.sync
            def _(sp):
                sp.dma_start(mask8[:, :, :], d["mask"].partition_broadcast(P)).then_inc(mask_in, 16)
                sp.dma_start(ident[:, :], d["ident"]).then_inc(mask_in, 16)
                sp.dma_start(ramp[:, :], d["ramp"]).then_inc(mask_in, 16)
                sp.dma_start(ramp_col[:, :], d["ramp_col"]).then_inc(mask_in, 16)
                sp.dma_start(ctxn[:, :, :], d["ctx"].rearrange("b k d -> k b d")).then_inc(ctx_in, 16)
                for i, (src, _, _) in enumerate(jobs):
                    if i >= 2:
                        sp.wait_ge(w_lo, i - 1)
                    sp.dma_start(raw_of(i), src).then_inc(raw_in[i % 2], 16)
                    if i == 1:
                        sp.dma_start(bk_col[:, :], d["bk"].rearrange("(c p) -> p c", p=P), allow_slow_non_contiguous=True).then_inc(small_in, 16)
                        sp.dma_start(t["bq_col"][:, :], d["bq"].rearrange("(c p) -> p c", p=P), allow_slow_non_contiguous=True).then_inc(small_in, 16)
                        sp.dma_start(bv_row[:, :], d["bv"].partition_broadcast(P)).then_inc(small_in, 16)
                        sp.dma_start(t["bo_row"][:, :], d["bo"].partition_broadcast(P)).then_inc(small_in, 16)
                sp.wait_ge(small_in, 64)

            @block.scalar
            def _(act):
                for c in range(DC):
                    act.wait_ge(ctx_t, c + 1)
                    nc.scalar.activation(c_h[:, c, :], ps[c % 2][:, :], ACT.Identity).then_inc(c_hi, 1)
                act.wait_ge(small_in, 64)
                for c in range(PAIRS):
                    act.wait_ge(k_mm, c + 1)
                    if c >= 2:
                        act.wait_ge(out_h[c % 2], 32 * (c // 2))
                    nc.scalar.activation(kout_h[:, c % 2, :], ps[c % 2][:, :], ACT.Identity,
                                         bias=bk_col[:, c:c + 1]).then_inc(k_hi, 1)
                    act.wait_ge(k_lo, c + 1)
                    act.wait_ge(k_hi, c + 1)
                    act.dma_start(d["k_h"][:, c, :], kout_h[:, c % 2, :].bitcast(F32)).then_inc(out_h[c % 2], 16)
                    act.dma_start(d["k_l"][:, c, :], kout_l[:, c % 2, :].bitcast(F32)).then_inc(out_h[c % 2], 16)
                for i in range(2 * B):
                    b, half = i // 2, i % 2
                    act.wait_ge(v_f, i + 1)
                    act.wait_ge(out_h[i % 2], 32 * (PAIRS // 2 + i // 2))
                    nc.scalar.activation(kout_h[:, i % 2, :], v32[:, i % 2, :], ACT.Identity).then_inc(v_hi, 1)
                    act.wait_ge(v_lo, i + 1)
                    act.wait_ge(v_hi, i + 1)
                    act.dma_start(d["v_h"][:, b, half * 512:half * 512 + 512], kout_h[:, i % 2, :].bitcast(F32)).then_inc(out_h[i % 2], 16)
                    act.dma_start(d["v_l"][:, b, half * 512:half * 512 + 512], kout_l[:, i % 2, :].bitcast(F32)).then_inc(out_h[i % 2], 16)
                for i in range(2):
                    act.wait_ge(out_h[i], 32 * (PAIRS // 2 + B))

            @block.gpsimd
            def _(pool):
                for i, (_, th, tl) in enumerate(jobs):
                    pool.wait_ge(w_hi, i + 1)
                    nc.gpsimd.tensor_tensor(tl, raw_of(i), th, ALU.subtract).then_inc(w_lo, 1)

            @block.vector
            def _(dve):
                steps = [0]

                def chained(ins):
                    steps[0] += 1
                    ins.then_inc(dve_step, 1)
                    dve.wait_ge(dve_step, steps[0])

                bcast = lambda x: x.unsqueeze(1).broadcast_to([P, B, KEYS])
                dve.wait_ge(mask_in, 64)
                chained(nc.vector.tensor_copy(mask[:, :, :], mask8[:, :, :]))
                chained(nc.vector.tensor_tensor(diag[:, :, :], mask[:, :, :], bcast(ident[:, :]), ALU.mult))
                chained(nc.vector.tensor_tensor(ranked[:, :, :], mask[:, :, :], bcast(ramp[:, :]), ALU.mult))
                chained(nc.vector.tensor_reduce(best[:, :], ranked[:, :, :], axis=AX.X, op=ALU.max))
                chained(nc.vector.tensor_reduce(mcol[:, :], diag[:, :, :], axis=AX.X, op=ALU.add))
                chained(nc.vector.tensor_scalar(first[:, :], best[:, :], ramp_col[:, 0:1], None, ALU.is_equal))
                chained(nc.vector.tensor_tensor(first[:, :], first[:, :], mcol[:, :], ALU.mult))
                chained(nc.vector.tensor_scalar(nfirst[:, :], first[:, :], -1.0, None, ALU.mult))
                for b in range(B):
                    chained(nc.vector.tensor_scalar(ranked[:, b, :], mask[:, b, :], nfirst[:, b:b + 1], first[:, b:b + 1], ALU.mult, ALU.add))
                nc.vector.tensor_tensor(sel[:, :, :], ranked[:, :, :], diag[:, :, :], ALU.add).then_inc(sel_ready, 1)
                chained(nc.vector.tensor_scalar(mcol[:, :], mcol[:, :], 1.0, BIG, ALU.subtract, ALU.mult))
                chained(nc.vector.tensor_scalar(t["mask_bias"][:, :], mcol[:, :], 10.0, None, ALU.mult))

                def hi(i):
                    dve.wait_ge(raw_in[i % 2], 16 * (i // 2 + 1))
                    nc.vector.tensor_copy(jobs[i][1], raw_of(i)).then_inc(w_hi, 1)

                hi(0)
                hi(1)
                for c in range(DC):
                    dve.wait_ge(c_hi, c + 1)
                    nc.vector.tensor_tensor(c_l[:, c, :], ps[c % 2][:, :], c_h[:, c, :], ALU.subtract).then_inc(c_lo, 1)
                hi(2)
                hi(3)
                dve.wait_ge(small_in, 64)
                for c in range(PAIRS):
                    dve.wait_ge(k_hi, c + 1)
                    nc.vector.scalar_tensor_tensor(kout_l[:, c % 2, :], ps[c % 2][:, :], bk_col[:, c:c + 1],
                                                   kout_h[:, c % 2, :], ALU.add, ALU.subtract).then_inc(k_lo, 1)
                    if c in (3, 5):
                        hi(4 + (c - 3) // 2)
                for i in range(2 * B):
                    dve.wait_ge(v_mm, i + 1)
                    nc.vector.tensor_tensor(v32[:, i % 2, :], ps[i % 2][:, :],
                                            bv_row[:, (i % 2) * 512:(i % 2) * 512 + 512], ALU.add).then_inc(v_f, 1)
                    dve.wait_ge(v_hi, i + 1)
                    nc.vector.tensor_tensor(kout_l[:, i % 2, :], v32[:, i % 2, :], kout_h[:, i % 2, :], ALU.subtract).then_inc(v_lo, 1)
                    if i in (2, 4):
                        hi(6 + (i - 2) // 2)

            @block.tensor
            def _(pe):
                pe.wait_ge(ctx_in, 16)
                pe.wait_ge(sel_ready, 1)
                for c in range(DC):
                    if c >= 2:
                        pe.wait_ge(c_lo, c - 1)
                    for b in range(B):
                        last = nc.tensor.matmul(ps[c % 2][:, b * KEYS:(b + 1) * KEYS], ctxn[:, b, c * P:(c + 1) * P],
                                                sel[:, b, :], start=True, stop=True)
                    last.then_inc(ctx_t, 1)
                pe.wait_ge(c_lo, DC)
                pe.wait_ge(w_lo, 2)
                for c in range(PAIRS):
                    if c >= 2:
                        pe.wait_ge(k_lo, c - 1)
                    for k in range(DC):
                        last = split_passes(nc, ps[c % 2][:, :], wk_h[:, k, c * P:(c + 1) * P], wk_l[:, k, c * P:(c + 1) * P],
                                            c_h[:, k, :], c_l[:, k, :], k == 0, k == DC - 1)
                    last.then_inc(k_mm, 1)
                pe.wait_ge(w_lo, 4)
                for i in range(2 * B):
                    b, n = i // 2, slice((i % 2) * 512, (i % 2) * 512 + 512)
                    if i < 2:
                        pe.wait_ge(k_lo, PAIRS - 1 + i)
                    else:
                        pe.wait_ge(v_f, i - 1)
                    for k in range(DC):
                        key = slice(b * KEYS, (b + 1) * KEYS)
                        last = split_passes(nc, ps[i % 2][:, :], c_h[:, k, key], c_l[:, k, key],
                                            wv_h[:, k, n], wv_l[:, k, n], k == 0, k == DC - 1)
                    last.then_inc(v_mm, 1)


def part2(nc, t, d):
    with ExitStack() as ctx:
        def sb(name, shape, dt=F32):
            return ctx.enter_context(nc.sbuf_tensor(name, shape, dt))

        def sem(name):
            return ctx.enter_context(nc.semaphore(name))

        def bank(name):
            return ctx.enter_context(nc.psum_tensor(name, [P, 512], F32))

        kz_h = sb("kz_h", [P, PAIRS, 2, KEYS], F32R)
        kz_l = sb("kz_l", [P, PAIRS, 2, KEYS], F32R)
        kg = sb("kg", [P, PAIRS, 2, KEYS], F32R)
        kb = sb("kb", [DH + 1, PAIRS, 2, KEYS], F32R)
        v1_h = sb("v1_h", [P, PAIRS, 2, P], F32R)
        vz_l = sb("vz_l", [P, PAIRS, 2, P], F32R)
        ident = sb("ident2", [P, P])
        xa, xn = sb("xa", [P, TT, D]), sb("xn", [P, TT, D])
        x_h, x_l = sb("x_h", [P, 2, DC, TOK], F32R), sb("x_l", [P, 2, DC, TOK], F32R)
        q_h = sb("q_h", [P, PAIRS, TOK], F32R)
        q_l = sb("q_l", [DH + 1, HEADS, TOK], F32R)
        e32, e_h, e_l = sb("e32", [P, 2, 512]), sb("e_h", [P, 2, 512], F32R), sb("e_l", [P, 2, 512], F32R)
        lnz, inv0, res0, ninv = sb("lnz", [P, TOK]), sb("inv0", [P, 2, TOK]), sb("res0", [P, TOK]), sb("ninv", [P, TOK])
        o32 = sb("o32", [P, 2, TOK])
        o_h, o_l = sb("o_h", [P, PAIRS, TOK], F32R), sb("o_l", [P, PAIRS, TOK], F32R)
        nmax, nmax_t = sb("nmax", [P, TT, HEADS]), sb("nmax_t", [PAIRS, 2, TOK], F32R)
        xr = sb("xr", [P, TT, D])
        stage = sb("stage", [P, 2, 512])
        small = sb("small", [P, 15, TT])
        st = small[:, 0:6, :].rearrange("p a b -> p (a b)").rearrange("p (j s) -> p j s", j=TT)
        mv = small[:, 6:8, :]
        ve, y0, ya, rstd, nmr = (small[:, i, :] for i in range(8, 13))
        mb = small[:, 13, :]
        pq, px, py = [bank("pq0"), bank("pq1")], [bank("px0"), bank("px1")], [bank("py0"), bank("py1")]
        psc, pg = bank("psc"), bank("pg")

        const_in, mb_in = sem("const_in"), [sem("mb_in0"), sem("mb_in1")]
        kg_in, k_in, v_in = ([sem(f"{n}{i}") for i in range(2)] for n in ("kg_in", "k_in", "v_in"))
        ones_set = sem("ones_set")
        xa_in, xr_in, m_in, x1_out = sem("xa_in"), sem("xr_in"), sem("m_in"), sem("x1_out")
        stats, var_ready, ln_y0, rstd_ready, xn_ready = sem("stats"), sem("var_ready"), sem("ln_y0"), sem("rstd_ready"), sem("xn_ready")
        rstd_step = sem("rstd_step")
        newton, xt_done, xh_done, xl_done = sem("newton"), sem("xt_done"), sem("xh_done"), sem("xl_done")
        q_mm, qh_done, ql_done = sem("q_mm"), sem("qh_done"), sem("ql_done")
        g_mm, max_done, maxt_mm, maxt_done = sem("g_mm"), sem("max_done"), sem("maxt_mm"), sem("maxt_done")
        s_mm, exp_done, el_done, pv_mm = sem("s_mm"), sem("exp_done"), sem("el_done"), sem("pv_mm")
        lnz_done, inv0_done, norm_step, o_done = sem("lnz_done"), sem("inv0_done"), sem("norm_step"), sem("o_done")
        oh_done, ol_done, xb_done = sem("oh_done"), sem("ol_done"), sem("xb_done")
        y_mm, y_read, x1_done = sem("y_mm"), sem("y_read"), sem("x1_done")
        AHEAD = 2

        x_t = d["x"].rearrange("(n j p) d -> n p j d", p=P, j=TT)
        x1_t = d["x1"].rearrange("(n j p) d -> n p j d", p=P, j=TT)

        def steps(eng, step):
            step(0, 0, 0, first=True, opens=True)
            with eng.Fori(0, B - 1) as b:
                with eng.Fori(0, (TPB - 2) // 2) as i:
                    step(b * TPB + i * 2 + 1, b, 1)
                    step(b * TPB + i * 2 + 2, b, 0)
                step(b * TPB + (TPB - 1), b, 1, switch=True)
                step(b * TPB + TPB, b + 1, 0, opens=True)
            with eng.Fori(0, (TPB - 4) // 2) as i:
                step(i * 2 + (B - 1) * TPB + 1, B - 1, 1)
                step(i * 2 + (B - 1) * TPB + 2, B - 1, 0)
            step(TILES - 3, B - 1, 1, third_next=False)
            step(TILES - 2, B - 1, 0, third_next=False, after_next=False)
            step(TILES - 1, B - 1, 1, third_next=False, after_next=False, next_tile=False)

        def behind(T, p, lag, first):
            if p >= lag:
                return [(T, p - lag)]
            return [] if first else [(T - 1, PAIRS + p - lag)]

        KG, KK, VV = 2, 6, 4
        HALF = [slice(0, PAIRS // 2), slice(PAIRS // 2, PAIRS)]

        with nc.Block() as block:
            @block.sync
            def _(sp):
                def key_slice(part, b, r, half):
                    return d[part][r, HALF[half], bass.ts(b, KEYS)]

                def load_kg(b, half):
                    for h in range(2):
                        r = slice(h * DH, (h + 1) * DH)
                        sp.dma_start(kg[r, HALF[half], h, :].bitcast(F32), key_slice("k_h", b, r, half)).then_inc(kg_in[half], 16)

                def load_k(b, half):
                    for h in range(2):
                        r, p = slice(h * DH, (h + 1) * DH), HALF[half]
                        sp.dma_start(kz_h[r, p, h, :].bitcast(F32), key_slice("k_h", b, r, half)).then_inc(k_in[half], 16)
                        sp.dma_start(kz_l[r, p, h, :].bitcast(F32), key_slice("k_l", b, r, half)).then_inc(k_in[half], 16)
                        sp.dma_start(kb[0:DH, p, h, :].bitcast(F32), key_slice("k_h", b, r, half)).then_inc(k_in[half], 16)

                def load_v(b, half):
                    for part, to in (("v_h", v1_h), ("v_l", vz_l)):
                        src = d[part][:, bass.ts(b, 1), :].rearrange("p o (c h e) -> p (o c) h e", h=2, e=DH)
                        for h in range(2):
                            sp.dma_start(to[:, HALF[half], h, h * DH:(h + 1) * DH].bitcast(F32),
                                         src[:, HALF[half], h, :]).then_inc(v_in[half], 16)

                def load_x(n, to, s):
                    sp.dma_start(to[:, :, :], x_t[n]).then_inc(s, 16)

                def max_row(n, half):
                    sp.wait_ge(maxt_done, 2 * n + half + 1)
                    sp.dma_start(q_l[DH:DH + 1, half * PAIRS:(half + 1) * PAIRS, :].bitcast(F32),
                                 nmax_t[:, half, :].bitcast(F32)).then_inc(m_in, 16)

                load_x(0, xa, xa_in)
                sp.dma_start(ident[:, :], d["ident"]).then_inc(const_in, 16)
                sp.dma_start(mb[:, 0:1], t["mask_bias"][:, 0:1]).then_inc(mb_in[0], 16)
                for half in range(2):
                    load_kg(0, half)
                for half in range(2):
                    load_k(0, half)
                for half in range(2):
                    load_v(0, half)
                sp.wait_ge(xn_ready, TT)
                load_x(1, xa, xa_in)
                sp.wait_ge(xn_ready, 2 * TT)
                load_x(2, xa, xa_in)
                max_row(0, 0)

                def store(R):
                    sp.wait_ge(x1_done, TT * R + TT + ONE)
                    sp.dma_start(x1_t[R], xr[:, :, :]).then_inc(x1_out, 16)

                def step(T, b, odd, switch=False, opens=False, third_next=True, after_next=True, next_tile=True, first=False):
                    if opens:
                        sp.wait_ge(exp_done, PAIRS * T + AHEAD)
                        sp.dma_start(mb[:, 1:2], t["mask_bias"][:, bass.ts(b, 1)]).then_inc(mb_in[1], 16)
                    if switch:
                        sp.wait_ge(g_mm, PAIRS * T + PAIRS // 2)
                        load_kg(b + 1, 0)
                    if not first:
                        sp.wait_ge(x1_out, T * 16)
                        load_x(T - 1, xr, xr_in)
                    max_row(T, 1)
                    if switch:
                        sp.wait_ge(g_mm, PAIRS * T + PAIRS)
                        load_kg(b + 1, 1)
                    if third_next:
                        sp.wait_ge(xn_ready, TT * T + 3 * TT)
                        load_x(T + 3, xa, xa_in)
                    if switch:
                        sp.wait_ge(s_mm, PAIRS * T + PAIRS // 2)
                        load_k(b + 1, 0)
                        sp.dma_start(mb[:, 0:1], t["mask_bias"][:, bass.ts(b + 1, 1)]).then_inc(mb_in[0], 16)
                        sp.wait_ge(pv_mm, PAIRS * T + PAIRS // 2 + AHEAD)
                        load_v(b + 1, 0)
                    if next_tile:
                        max_row(T + 1, 0)
                    if switch:
                        sp.wait_ge(s_mm, PAIRS * T + PAIRS)
                        load_k(b + 1, 1)
                    if not first:
                        store(T - 1)
                    if switch:
                        sp.wait_ge(pv_mm, PAIRS * T + PAIRS + AHEAD)
                        load_v(b + 1, 1)

                steps(sp, step)
                sp.wait_ge(x1_out, TILES * 16)
                load_x(TILES - 1, xr, xr_in)
                store(TILES - 1)
                sp.wait_ge(x1_out, TILES * 16 + 16)

            @block.tensor
            def _(pe):
                def transposes(n, k):
                    if k == 0:
                        pe.wait_ge(xn_ready, TT * n + TT)
                    for c in (2 * k, 2 * k + 1):
                        for j in range(TT):
                            at = (c % 2) * TOK + j * P
                            last = nc.tensor.transpose(pg[:, at:at + P], xn[:, j, c * P:(c + 1) * P], ident[:, :])
                    last.then_inc(xt_done, 1)

                def query(n, p, odd):
                    if p == 0:
                        pe.wait_ge(xl_done, 2 * n + 2)
                    if not (type(n) is int and n == 0 and p < 2):
                        pe.wait_ge(ql_done, PAIRS * n + p - 1)
                    w = slice(p * P, (p + 1) * P)
                    for k in range(DC):
                        last = split_passes(nc, pq[p % 2][:, 0:TOK], t["wq_h"][:, k, w], t["wq_l"][:, k, w],
                                            x_h[:, odd, k, :], x_l[:, odd, k, :], k == 0, k == DC - 1)
                    last.then_inc(q_mm, 1)

                def guard(n, p, batches=None):
                    if batches is not None and p % (PAIRS // 2) == 0:
                        pe.wait_ge(kg_in[p // (PAIRS // 2)], 16 * KG * batches)
                    pe.wait_ge(max_done, PAIRS * n + p)
                    pe.wait_ge(qh_done, PAIRS * n + p + 1)
                    for j in range(TT):
                        last = nc.tensor.matmul(pg[:, j * TOK:(j + 1) * TOK], q_h[:, p, j * P:(j + 1) * P],
                                                kg[:, p, :, :].rearrange("p h k -> p (h k)"), start=True, stop=True)
                    last.then_inc(g_mm, 1)

                def max_transpose(n, half):
                    for j in range(TT):
                        last = nc.tensor.transpose(pg[0:PAIRS, j * P:(j + 1) * P],
                                                   nmax[:, j, half * PAIRS:(half + 1) * PAIRS], ident[:, :])
                    last.then_inc(maxt_mm, 1)

                def scores(T, p, b):
                    if p % (PAIRS // 2) == 0:
                        half = p // (PAIRS // 2)
                        pe.wait_ge(m_in, 32 * T + 16 * half + 16)
                        pe.wait_ge(k_in[half], 16 * KK * b + 16 * KK)
                    pe.wait_ge(exp_done, PAIRS * T + p + AHEAD)
                    for h in range(2):
                        out = psc[:, h * TOK:(h + 1) * TOK]
                        nc.tensor.matmul(out, kz_h[:, p, h, :], q_h[:, p, :], start=True, stop=False)
                        nc.tensor.matmul(out, kz_l[:, p, h, :], q_h[:, p, :], start=False, stop=False)
                        last = nc.tensor.matmul(out, kb[:, p, h, :], q_l[:, 2 * p + h, :], start=False, stop=True)
                    last.then_inc(s_mm, 1)

                def values(T, p, b):
                    if p % (PAIRS // 2) == 0:
                        pe.wait_ge(v_in[p // (PAIRS // 2)], 16 * VV * b + 16 * VV)
                    pe.wait_ge(o_done, PAIRS * T + p - 2 + 1 + AHEAD)
                    pe.wait_ge(el_done, PAIRS * T + p + 1)
                    for h in range(2):
                        out, col = px[p % 2][:, h * TOK:(h + 1) * TOK], slice(h * TOK, (h + 1) * TOK)
                        last = split_passes(nc, out, v1_h[:, p, h, :], vz_l[:, p, h, :],
                                            e_h[:, p % 2, col], e_l[:, p % 2, col], True, True)
                    last.then_inc(pv_mm, 1)

                def output(R, c):
                    if c == 0:
                        pe.wait_ge(y_read, TT * R + ONE)
                    pe.wait_ge(ol_done, PAIRS * R + c + 1 + AHEAD)
                    for j in range(TT):
                        w = slice(j * P, (j + 1) * P)
                        last = split_passes(nc, py[j][:, :], o_h[:, c, w], o_l[:, c, w],
                                            t["wo_h"][:, c, :], t["wo_l"][:, c, :], c == 0, c == PAIRS - 1)
                        if c == PAIRS - 1:
                            last.then_inc(y_mm, 1)

                pe.wait_ge(const_in, 16)
                pe.wait_ge(ones_set, 3)
                def between_maxima(T, p, after_next=True, next_tile=True):
                    if p == 1 and not (type(T) is int and T < 0):
                        pe.wait_ge(max_done, PAIRS * T + PAIRS)
                        max_transpose(T, 1)
                    if p in (4, 6) and after_next:
                        pe.wait_ge(max_done, PAIRS * T + PAIRS + p - 1)
                        transposes(T + 2, p // 2 - 2)
                    if p == 5 and next_tile:
                        pe.wait_ge(max_done, PAIRS * T + PAIRS + p - 1)
                        max_transpose(T + 1, 0)

                def bank_pg_read(T, p, after_next=True, next_tile=True):
                    if p == 1 and not (type(T) is int and T < 0):
                        pe.wait_ge(maxt_done, 2 * T + 2)
                    if p in (4, 6) and after_next:
                        pe.wait_ge(xh_done, 2 * T + 4 + p // 2 - 1)
                    if p == 5 and next_tile:
                        pe.wait_ge(maxt_done, 2 * T + 3)

                transposes(0, 0)
                pe.wait_ge(xh_done, 1)
                transposes(0, 1)
                for p in range(PAIRS):
                    between_maxima(-1, p)
                    query(0, p, 0)
                    if p:
                        bank_pg_read(-1, p)
                        guard(0, p - 1, 1)

                def step(T, b, odd, switch=False, opens=False, third_next=True, after_next=True, next_tile=True, first=False):
                    for p in range(PAIRS):
                        scores(T, p, b)
                        if p == PAIRS - 1 and not first:
                            output(T - 1, p)
                        between_maxima(T, p, after_next, next_tile)
                        if next_tile:
                            query(T + 1, p, 1 - odd)
                        if 0 < p < PAIRS - 1 and not first:
                            output(T - 1, p)
                        bank_pg_read(T, p, after_next, next_tile)
                        if p:
                            if next_tile:
                                guard(T + 1, p - 1, b + 2 if switch else None)
                            values(T, p - 1, b)
                        else:
                            guard(T, PAIRS - 1)
                            if not first:
                                values(T - 1, PAIRS - 1, None)
                                output(T - 1, 0)

                steps(pe, step)
                values(TILES - 1, PAIRS - 1, None)
                for c in range(PAIRS):
                    output(TILES - 1, c)

            @block.scalar
            def _(act):
                nc.scalar.preload_act_table_set("natural_log_exp_and_others")
                act.sem_inc(exp_done, AHEAD)
                act.sem_inc(inv0_done, ONE)

                def rsqrt_seed(n):
                    act.wait_ge(var_ready, n + 1)
                    nc.scalar.activation(y0, ve, ACT.Ln).then_inc(ln_y0, 1)
                    act.wait_ge(ln_y0, 2 * n + 1)
                    nc.scalar.activation(y0, y0, ACT.Exp, scale=-0.5).then_inc(ln_y0, 1)

                def normalise(n, j):
                    if j == 0:
                        act.wait_ge(rstd_ready, n + 1)
                        act.wait_ge(xt_done, 2 * n)
                    nc.scalar.activation(xn[:, j, :], xa[:, j, :], ACT.Identity, bias=nmr[:, j:j + 1],
                                         scale=rstd[:, j:j + 1]).then_inc(xn_ready, 1)

                def x_hi(n, k, odd):
                    if not (type(n) is int and n < 3):
                        act.wait_ge(x1_done, TT * (n - 3) + ONE)
                    if not (type(n) is int and n == 0):
                        act.wait_ge(xl_done, 2 * n + k - 1)
                    act.wait_ge(xt_done, 2 * n + k + 1)
                    nc.scalar.activation(x_h[:, odd, 2 * k:2 * k + 2, :].rearrange("p c n -> p (c n)"), pg[:, :], ACT.Identity)
                    nc.scalar.activation(stage[:, k, :], pg[:, :], ACT.Identity).then_inc(xh_done, 1)

                def q_hi(n, p):
                    act.wait_ge(q_mm, PAIRS * n + p + 1)
                    nc.scalar.activation(q_h[:, p, :], pq[p % 2][:, 0:TOK], ACT.Identity,
                                         bias=t["bq_col"][:, p:p + 1]).then_inc(qh_done, 1)

                def max_hi(n, half):
                    act.wait_ge(maxt_mm, 2 * n + half + 1)
                    nc.scalar.activation(nmax_t[:, half, :], pg[0:PAIRS, 0:TOK], ACT.Identity).then_inc(maxt_done, 1)

                def exponentials(T, p, b, col):
                    if p == 0:
                        act.wait_ge(mb_in[col], 16 * b + 16)
                    act.wait_ge(s_mm, PAIRS * T + p + 1)
                    act.wait_ge(pv_mm, PAIRS * T + p - 2 + 1 + AHEAD)
                    nc.scalar.activation(e32[:, p % 2, :], psc[:, :], ACT.Exp, bias=mb[:, col:col + 1], scale=SCALE)
                    nc.scalar.activation(e_h[:, p % 2, :], psc[:, :], ACT.Exp, bias=mb[:, col:col + 1],
                                         scale=SCALE).then_inc(exp_done, 1)

                def sum_inverse_seed(T, p):
                    act.wait_ge(inv0_done, PAIRS * T + p + ONE)
                    act.wait_ge(pv_mm, PAIRS * T + p + 1 + AHEAD)
                    nc.scalar.activation(lnz[DH:P, :], px[p % 2][DH:P, 0:TOK], ACT.Ln)
                    nc.scalar.activation(lnz[0:DH, :], px[p % 2][0:DH, TOK:2 * TOK], ACT.Ln).then_inc(lnz_done, 1)
                    act.wait_ge(lnz_done, PAIRS * T + p + 1)
                    act.wait_ge(o_done, PAIRS * T + p - 2 + 1 + AHEAD)
                    nc.scalar.activation(inv0[:, p % 2, :], lnz[:, :], ACT.Exp, scale=-1.0).then_inc(inv0_done, 1)

                def o_hi(T, p):
                    act.wait_ge(o_done, PAIRS * T + p + 1 + AHEAD)
                    nc.scalar.activation(o_h[:, p, :], o32[:, p % 2, :], ACT.Identity).then_inc(oh_done, 1)

                def y_copy(R, last=False):
                    act.wait_ge(x1_done, TT * R + ONE)
                    act.wait_ge(xl_done, 2 * TILES if last else 2 * R + 8)
                    for j in range(TT):
                        act.wait_ge(y_mm, TT * R + j + 1)
                        nc.scalar.activation(stage[:, j, :], py[j][:, :], ACT.Identity).then_inc(y_read, 1)

                rsqrt_seed(0)
                normalise(0, 0)
                normalise(0, 1)
                x_hi(0, 0, 0)
                x_hi(0, 1, 0)
                for p in range(PAIRS):
                    if p == 1:
                        rsqrt_seed(1)
                    if p == 2:
                        normalise(1, 0)
                        normalise(1, 1)
                    if p in (4, 6):
                        x_hi(1, p // 2 - 2, 1)
                    if p == 5:
                        max_hi(0, 0)
                    q_hi(0, p)
                rsqrt_seed(2)

                def step(T, b, odd, switch=False, opens=False, third_next=True, after_next=True, next_tile=True, first=False):
                    for p in range(PAIRS):
                        for at in behind(T, p, 2, first):
                            sum_inverse_seed(*at)
                        exponentials(T, p, b, 0 if opens else 1)
                        if p == 1:
                            max_hi(T, 1)
                        if p == 5 and next_tile:
                            max_hi(T + 1, 0)
                        if after_next and p in (4, 6):
                            x_hi(T + 2, p // 2 - 2, odd)
                        if p == PAIRS - 1 and not first:
                            y_copy(T - 1, not after_next)
                        if third_next and p == PAIRS - 1:
                            rsqrt_seed(T + 3)
                        if next_tile:
                            q_hi(T + 1, p)
                        for at in behind(T, p, 2, first):
                            o_hi(*at)
                        if after_next and p in (1, 2):
                            normalise(T + 2, p - 1)

                steps(act, step)
                for p in (PAIRS - 2, PAIRS - 1):
                    sum_inverse_seed(TILES - 1, p)
                    o_hi(TILES - 1, p)
                y_copy(TILES - 1, True)

            @block.gpsimd
            def _(pool):
                pool.sem_inc(ol_done, AHEAD)

                def e_lo(T, p):
                    pool.wait_ge(exp_done, PAIRS * T + p + 1 + AHEAD)
                    nc.gpsimd.tensor_tensor(e_l[:, p % 2, :], e32[:, p % 2, :], e_h[:, p % 2, :], ALU.subtract).then_inc(el_done, 1)

                def o_lo(T, p):
                    pool.wait_ge(oh_done, PAIRS * T + p + 1)
                    nc.gpsimd.tensor_tensor(o_l[:, p, :], o32[:, p % 2, :], o_h[:, p, :], ALU.subtract).then_inc(ol_done, 1)

                def x_lo(n, k, odd):
                    pool.wait_ge(xh_done, 2 * n + k + 1)
                    nc.gpsimd.tensor_tensor(x_l[:, odd, 2 * k:2 * k + 2, :].rearrange("p c n -> p (c n)"), stage[:, k, :],
                                            x_h[:, odd, 2 * k:2 * k + 2, :].rearrange("p c n -> p (c n)"), ALU.subtract).then_inc(xl_done, 1)

                def residual(R):
                    pool.wait_ge(xb_done, R + 1)
                    for j in range(TT):
                        pool.wait_ge(y_read, TT * R + j + 1 + ONE)
                        nc.gpsimd.tensor_tensor(xr[:, j, :], stage[:, j, :], xr[:, j, :], ALU.add).then_inc(x1_done, 1)

                def add_bo(R):
                    pool.wait_ge(xr_in, 16 * R + 16)
                    nc.gpsimd.tensor_tensor(xr[:, :, :], xr[:, :, :], t["bo_row"][:, :].unsqueeze(1).broadcast_to([P, TT, D]),
                                            ALU.add).then_inc(xb_done, 1)

                for n in range(2):
                    for k in range(2):
                        x_lo(n, k, n)

                def step(T, b, odd, switch=False, opens=False, third_next=True, after_next=True, next_tile=True, first=False):
                    for p in range(PAIRS):
                        e_lo(T, p)
                        for at in behind(T, p, 2, first):
                            o_lo(*at)
                        if after_next and p in (4, 6):
                            x_lo(T + 2, (p - 4) // 2, odd)
                        if p == 3 and not first:
                            add_bo(T - 1)
                        if p == PAIRS - 1 and not first:
                            residual(T - 1)

                steps(pool, step)
                for p in (PAIRS - 2, PAIRS - 1):
                    o_lo(TILES - 1, p)
                add_bo(TILES - 1)
                residual(TILES - 1)

            @block.vector
            def _(dve):
                for m in (kz_h, kz_l, kg):
                    nc.vector.memset(m[0:DH, :, 1, :].bitcast(F32), 0.0)
                    nc.vector.memset(m[DH:P, :, 0, :].bitcast(F32), 0.0)
                nc.vector.memset(kb[DH:DH + 1, :, :, :].bitcast(F32), 1.0).then_inc(ones_set, 1)
                for m, value in ((v1_h, 1.0), (vz_l, 0.0)):
                    nc.vector.memset(m[:, :, 0, DH:P].bitcast(F32), value)
                    nc.vector.memset(m[:, :, 1, 0:DH].bitcast(F32), value).then_inc(ones_set, 1)
                dve.sem_inc(pv_mm, AHEAD)
                dve.sem_inc(o_done, AHEAD)
                dve.sem_inc(x1_done, ONE)
                dve.sem_inc(y_read, ONE)
                dve.sem_inc(x1_out, 16)


                def statistics(n):
                    dve.wait_ge(xa_in, 16 * n + 16)
                    for j in range(TT):
                        nc.vector.bn_stats(st[:, j, :], xa[:, j, :]).then_inc(stats, 1)
                    dve.drain()
                    for j in range(TT):
                        nc.vector.bn_aggr(mv[:, j, :], st[:, j, :]).then_inc(stats, 1)
                    dve.wait_ge(stats, 2 * TT * n + 2 * TT)
                    nc.vector.tensor_scalar(ve, mv[:, :, 1], EPS, None, ALU.add).then_inc(var_ready, 1)

                def rstd_newton(n):
                    dve.wait_ge(ln_y0, 2 * n + 2)
                    dve.wait_ge(xn_ready, TT * n)
                    nc.vector.tensor_tensor(ya, y0, y0, ALU.mult).then_inc(newton, 1)
                    dve.wait_ge(newton, 3 * n + 1)
                    nc.vector.tensor_tensor(ya, ya, ve, ALU.mult).then_inc(newton, 1)
                    dve.wait_ge(newton, 3 * n + 2)
                    nc.vector.tensor_scalar(ya, ya, -0.5, 1.5, ALU.mult, ALU.add).then_inc(newton, 1)
                    dve.wait_ge(newton, 3 * n + 3)
                    nc.vector.tensor_tensor(rstd, ya, y0, ALU.mult).then_inc(rstd_step, 1)
                    dve.wait_ge(rstd_step, n + 1)
                    nc.vector.scalar_tensor_tensor(nmr, mv[:, :, 0], -1.0, rstd, ALU.mult, ALU.mult).then_inc(rstd_ready, 1)

                def q_lo(n, p):
                    dve.wait_ge(qh_done, PAIRS * n + p + 1)
                    for h in range(2):
                        r = slice(h * DH, (h + 1) * DH)
                        last = nc.vector.scalar_tensor_tensor(q_l[0:DH, 2 * p + h, :], pq[p % 2][r, 0:TOK],
                                                              t["bq_col"][r, p:p + 1], q_h[r, p, :], ALU.add, ALU.subtract)
                    last.then_inc(ql_done, 1)

                def maxima(n, p):
                    dve.wait_ge(g_mm, PAIRS * n + p + 1)
                    nc.vector.tensor_reduce(nmax[:, :, 2 * p:2 * p + 2],
                                            pg[:, :].rearrange("p (j h k) -> p j h k", j=TT, h=2),
                                            axis=AX.X, op=ALU.max, negate=True).then_inc(max_done, 1)

                def divide(T, p):
                    g = PAIRS * T + p
                    dve.wait_ge(inv0_done, g + 1 + ONE)
                    dve.wait_ge(ol_done, g - 2 + 1 + AHEAD)
                    nc.vector.tensor_tensor(res0[DH:P, :], px[p % 2][DH:P, 0:TOK], inv0[DH:P, p % 2, :], ALU.mult)
                    nc.vector.tensor_tensor(res0[0:DH, :], px[p % 2][0:DH, TOK:2 * TOK], inv0[0:DH, p % 2, :], ALU.mult).then_inc(norm_step, 1)
                    dve.wait_ge(norm_step, 2 * g + 1)
                    nc.vector.scalar_tensor_tensor(ninv[:, :], res0[:, :], 2.0, inv0[:, p % 2, :],
                                                   ALU.subtract, ALU.mult).then_inc(norm_step, 1)
                    dve.wait_ge(norm_step, 2 * g + 2)
                    nc.vector.scalar_tensor_tensor(o32[0:DH, p % 2, :], px[p % 2][0:DH, 0:TOK], -1.0, ninv[DH:P, :],
                                                   ALU.mult, ALU.mult)
                    nc.vector.scalar_tensor_tensor(o32[DH:P, p % 2, :], px[p % 2][DH:P, TOK:2 * TOK], -1.0, ninv[0:DH, :],
                                                   ALU.mult, ALU.mult).then_inc(o_done, 1)

                statistics(0)
                rstd_newton(0)
                statistics(1)
                for p in range(PAIRS):
                    if p == 1:
                        rstd_newton(1)
                    q_lo(0, p)
                    if p:
                        maxima(0, p - 1)
                statistics(2)

                def step(T, b, odd, switch=False, opens=False, third_next=True, after_next=True, next_tile=True, first=False):
                    for p in range(PAIRS):
                        if p == 0:
                            maxima(T, PAIRS - 1)
                        for at in behind(T, p, 2, first):
                            divide(*at)
                        if next_tile:
                            q_lo(T + 1, p)
                        if p and next_tile:
                            maxima(T + 1, p - 1)
                        if third_next and p == 6:
                            statistics(T + 3)
                        if after_next and p == 0:
                            rstd_newton(T + 2)

                steps(dve, step)
                divide(TILES - 1, PAIRS - 2)
                divide(TILES - 1, PAIRS - 1)


def part3(nc, t, d):
    with ExitStack() as ctx:
        def sb(name, shape, dt=F32):
            return ctx.enter_context(nc.sbuf_tensor(name, shape, dt))

        def sem(name):
            return ctx.enter_context(nc.semaphore(name))

        def bank(name):
            return ctx.enter_context(nc.psum_tensor(name, [P, 512], F32))

        W = ("W_k", "W_r", "W_v")
        w_h = {w: sb(f"{w}_h", [P, DC, D], F32R) for w in W}
        w_l = {w: sb(f"{w}_l", [P, DC, D], F32R) for w in W}
        wraw = sb("wraw", [P, 2, DC, D])
        ident = sb("ident3", [P, P])
        mu = {"r": sb("mu_r", [P, DC]), "k": sb("mu_k", [P, DC])}
        st, mv = sb("st3", [P, T3, 6]), sb("mv3", [P, T3, 2])
        ve, y0, ya, rstd, nmr, power = (sb(n, [P, T3]) for n in ("ve3", "y3", "ya3", "rstd3", "nmr3", "power"))
        x1 = sb("x1", [P, TPB3, T3, D])
        xn = sb("xn3", [P, T3, D])
        xt = sb("xt", [P, DC, 1 + N3])
        dx = sb("dx", [P, DC, N3])
        mix = sb("mix", [P, 2, N3])
        m_h = {"r": sb("mr_h", [P, DC, N3], F32R), "k": sb("mk_h", [P, DC, N3], F32R)}
        m_l = {"r": sb("mr_l", [P, DC, N3], F32R), "k": sb("mk_l", [P, DC, N3], F32R)}
        rl, a32 = sb("rl", [P, 2, N3]), sb("a32", [P, 2, N3])
        a_h, a_l = sb("a_h", [P, DC, N3], F32R), sb("a_l", [P, DC, N3], F32R)
        gate = sb("gate", [P, T3, D])
        res = sb("res", [P, T3, D])
        pt, pk, pr = [bank("pt0"), bank("pt1")], [bank("pk0"), bank("pk1")], [bank(f"pr{i}") for i in range(4)]

        wbanks = [pk[0], pk[1]] + pr
        w_in, mu_in, id_in = sem("w_in"), sem("mu_in"), sem("id_in")
        wt_mm, wh_done, wl_done = sem("wt_mm"), sem("wh_done"), sem("wl_done")
        stats, var_ready, y0_done, newton, rstd_done, power_set = (sem(n) for n in (
            "stats3", "var3_ready", "y03_done", "newton3", "rstd3_done", "power_set"))
        x1_in = [sem(f"x1_in{i}") for i in range(TPB3)]
        xn_done, xt_mm, xt_cp, carry, dx_done = sem("xn3_done"), sem("xt_mm"), sem("xt_cp"), sem("carry"), sem("dx_done")
        mix_done, mh_done, ml_done = sem("mix_done"), sem("mh_done"), sem("ml_done")
        k_mm, rl_done, ah_done, a32_done, al_done = sem("k3_mm"), sem("rl_done"), sem("ah_done"), sem("a32_done"), sem("al_done")
        r_mm, gate_done, v_mm, gv_done, res_done, out_st = sem("r3_mm"), sem("gate_done"), sem("v3_mm"), sem("gv_done"), sem("res_done"), sem("out_st")

        x1_t = d["x1"].rearrange("(n j p) d -> n p j d", p=P, j=T3)
        out_t = d["out"].rearrange("(n j p) d -> n p j d", p=P, j=T3)
        LAST = B * TPB3 - 1

        def steps(eng, step):
            with eng.Fori(0, B - 1) as b:
                for i in range(TPB3):
                    step(b * TPB3 + i, i)
            for i in range(TPB3):
                step((B - 1) * TPB3 + i, i)

        with nc.Block() as block:
            @block.sync
            def _(sp):
                sp.dma_start(wraw[:, 0, :, :], d["W_k"].rearrange("(c p) n -> p c n", p=P)).then_inc(w_in, 16)
                sp.dma_start(ident[:, :], d["ident"]).then_inc(id_in, 16)
                sp.dma_start(x1[:, 0, :, :], x1_t[0]).then_inc(x1_in[0], 16)
                sp.dma_start(mu["r"][:, :], d["mu_r"].rearrange("(c p) -> p c", p=P), allow_slow_non_contiguous=True).then_inc(mu_in, 16)
                sp.dma_start(mu["k"][:, :], d["mu_k"].rearrange("(c p) -> p c", p=P), allow_slow_non_contiguous=True).then_inc(mu_in, 16)
                sp.wait_ge(w_in, 16)
                sp.dma_start(wraw[:, 1, :, :], d["W_r"].rearrange("(c p) n -> p c n", p=P)).then_inc(w_in, 16)
                sp.wait_ge(wt_mm, DC)
                sp.wait_ge(w_in, 32)
                sp.dma_start(wraw[:, 0, :, :], d["W_v"].rearrange("(c p) n -> p c n", p=P)).then_inc(w_in, 16)
                for i in (1, 2):
                    sp.dma_start(x1[:, i, :, :], x1_t[i]).then_inc(x1_in[i], 16)

                def step(n, i):
                    if not (type(n) is int and n + 3 > LAST):
                        sp.wait_ge(res_done, n * T3 + ONE)
                        sp.dma_start(x1[:, (i + 3) % TPB3, :, :], x1_t[n + 3]).then_inc(x1_in[(i + 3) % TPB3], 16)
                    sp.wait_ge(res_done, n * T3 + T3 + ONE)
                    sp.dma_start(out_t[n], res[:, :, :]).then_inc(out_st, 16)

                steps(sp, step)
                sp.wait_ge(out_st, 16 * (LAST + 1) + 16)

            @block.tensor
            def _(pe):
                pe.wait_ge(id_in, 16)
                for i, w in enumerate(W):
                    pe.wait_ge(w_in, 16 * (i + 1))
                    for c in range(DC):
                        n = DC * i + c
                        if n >= len(wbanks):
                            pe.wait_ge(wl_done, n - len(wbanks) + 1)
                        for o in range(DC):
                            last = nc.tensor.transpose(wbanks[n % len(wbanks)][:, o * P:(o + 1) * P],
                                                       wraw[:, i % 2, o, c * P:(c + 1) * P], ident[:, :])
                        last.then_inc(wt_mm, 1)

                def transposes(n):
                    for c in range(DC):
                        if c < 2:
                            pe.wait_ge(xt_cp, DC * n)
                        else:
                            pe.wait_ge(xt_cp, DC * n + c - 1)
                        for j in range(T3):
                            if c == 0:
                                pe.wait_ge(xn_done, T3 * n + j + 1)
                            last = nc.tensor.transpose(pt[c % 2][:, j * P:(j + 1) * P], xn[:, j, c * P:(c + 1) * P], ident[:, :])
                        last.then_inc(xt_mm, 1)

                transposes(0)
                pe.wait_ge(wl_done, DC * len(W))

                def step(n, i):
                    for c in range(DC):
                        pe.wait_ge(rl_done, DC * n + c - 2 + 1 + 2)
                        if c == 0:
                            pe.wait_ge(ml_done, 2 * DC * n + DC)
                        for k in range(DC):
                            last = split_passes(nc, pk[c % 2][:, :], w_h["W_k"][:, k, c * P:(c + 1) * P],
                                                w_l["W_k"][:, k, c * P:(c + 1) * P], m_h["k"][:, k, :], m_l["k"][:, k, :],
                                                k == 0, k == DC - 1)
                        last.then_inc(k_mm, 1)
                    for j in range(T3):
                        if j == 0:
                            pe.wait_ge(gv_done, T3 * n + ONE)
                            pe.wait_ge(ml_done, 2 * DC * n + 2 * DC)
                        w = slice(j * P, (j + 1) * P)
                        for k in range(DC):
                            last = split_passes(nc, pr[j][:, :], m_h["r"][:, k, w], m_l["r"][:, k, w],
                                                w_h["W_r"][:, k, :], w_l["W_r"][:, k, :], k == 0, k == DC - 1)
                        last.then_inc(r_mm, 1)
                    if not (type(n) is int and n == LAST):
                        transposes(n + 1)
                    for j in range(T3):
                        pe.wait_ge(gate_done, T3 * n + j + 1)
                        if j == 0:
                            pe.wait_ge(al_done, DC * n + DC + 2)
                        w = slice(j * P, (j + 1) * P)
                        for k in range(DC):
                            last = split_passes(nc, pr[j][:, :], a_h[:, k, w], a_l[:, k, w],
                                                w_h["W_v"][:, k, :], w_l["W_v"][:, k, :], k == 0, k == DC - 1)
                        last.then_inc(v_mm, 1)

                steps(pe, step)

            @block.scalar
            def _(act):
                nc.scalar.preload_act_table_set("sigmoid_and_others")
                act.sem_inc(rl_done, 2)

                def weight_hi(n):
                    act.wait_ge(wt_mm, n + 1)
                    nc.scalar.activation(w_h[W[n // DC]][:, n % DC, :], wbanks[n % len(wbanks)][:, :], ACT.Identity).then_inc(wh_done, 1)

                def normalise(n, buf, j):
                    if j == 0:
                        act.wait_ge(rstd_done, n + 1)
                        act.wait_ge(xt_mm, DC * n)
                    nc.scalar.activation(xn[:, j, :], x1[:, buf, j, :], ACT.Identity, bias=nmr[:, j:j + 1],
                                         scale=rstd[:, j:j + 1]).then_inc(xn_done, 1)

                def xt_copy(n):
                    act.wait_ge(carry, n + 1)
                    for c in range(DC):
                        act.wait_ge(xt_mm, DC * n + c + 1)
                        nc.scalar.activation(xt[:, c, 1:1 + N3], pt[c % 2][:, :], ACT.Identity).then_inc(xt_cp, 1)

                def mix_hi(n, which):
                    name = "kr"[which]
                    for c in range(DC):
                        at = 2 * DC * n + DC * which + c
                        act.wait_ge(mix_done, at + 1)
                        nc.scalar.activation(m_h[name][:, c, :], mix[:, c % 2, :], ACT.Identity).then_inc(mh_done, 1)

                for n in range(DC):
                    weight_hi(n)
                for j in range(T3):
                    normalise(0, 0, j)
                for n in range(DC, DC * len(W)):
                    weight_hi(n)
                xt_copy(0)
                mix_hi(0, 0)
                mix_hi(0, 1)

                def step(n, i):
                    more = not (type(n) is int and n == LAST)
                    for c in range(DC):
                        act.wait_ge(k_mm, DC * n + c + 1)
                        act.wait_ge(al_done, DC * n + c - 2 + 1 + 2)
                        nc.scalar.activation(rl[:, c % 2, :], pk[c % 2][:, :], ACT.Relu).then_inc(rl_done, 1)
                        act.wait_ge(rl_done, DC * n + c + 1 + 2)
                        nc.scalar.activation(a_h[:, c, :], rl[:, c % 2, :], ACT.Square).then_inc(ah_done, 1)
                        if more:
                            normalise(n + 1, (i + 1) % TPB3, c)
                    for j in range(T3):
                        act.wait_ge(r_mm, T3 * n + j + 1)
                        nc.scalar.activation(gate[:, j, :], pr[j][:, :], ACT.Sigmoid).then_inc(gate_done, 1)
                    if more:
                        xt_copy(n + 1)
                        mix_hi(n + 1, 0)
                        mix_hi(n + 1, 1)

                steps(act, step)

            @block.gpsimd
            def _(pool):
                def differences(n):
                    pool.wait_ge(ml_done, 2 * DC * n)
                    for c in range(DC):
                        pool.wait_ge(xt_cp, DC * n + c + 1)
                        nc.gpsimd.tensor_tensor(dx[:, c, :], xt[:, c, 1:1 + N3], xt[:, c, 0:N3], ALU.subtract).then_inc(dx_done, 1)

                def rsqrt_seed(n):
                    pool.wait_ge(var_ready, n + 1)
                    nc.gpsimd.tensor_tensor(y0[:, :], ve[:, :], power[:, :], ALU.pow).then_inc(y0_done, 1)

                nc.gpsimd.memset(power[:, :], -0.5).then_inc(power_set, 1)
                pool.wait_ge(power_set, 1)
                rsqrt_seed(0)
                rsqrt_seed(1)
                differences(0)

                def step(n, i):
                    if not (type(n) is int and n + 2 > LAST):
                        rsqrt_seed(n + 2)
                    if not (type(n) is int and n == LAST):
                        differences(n + 1)
                    for j in range(T3):
                        pool.wait_ge(gv_done, T3 * n + j + 1 + ONE)
                        nc.gpsimd.tensor_tensor(res[:, j, :], res[:, j, :], x1[:, i, j, :], ALU.add).then_inc(res_done, 1)

                steps(pool, step)

            @block.vector
            def _(dve):
                dve.sem_inc(al_done, 2)
                dve.sem_inc(res_done, ONE)
                dve.sem_inc(gv_done, ONE)
                dve.sem_inc(out_st, 16)

                def statistics(n, buf):
                    loads = (n - buf) * (16 // TPB3) + 16
                    dve.wait_ge(x1_in[buf], loads)
                    for j in range(T3):
                        nc.vector.bn_stats(st[:, j, :], x1[:, buf, j, :]).then_inc(stats, 1)
                    dve.drain()
                    for j in range(T3):
                        nc.vector.bn_aggr(mv[:, j, :], st[:, j, :]).then_inc(stats, 1)
                    dve.wait_ge(stats, 2 * T3 * n + 2 * T3)
                    nc.vector.tensor_scalar(ve[:, :], mv[:, :, 1], EPS, None, ALU.add).then_inc(var_ready, 1)

                def rstd_newton(n):
                    dve.wait_ge(y0_done, n + 1)
                    nc.vector.tensor_tensor(ya[:, :], y0[:, :], y0[:, :], ALU.mult).then_inc(newton, 1)
                    dve.wait_ge(newton, 4 * n + 1)
                    nc.vector.tensor_tensor(ya[:, :], ya[:, :], ve[:, :], ALU.mult).then_inc(newton, 1)
                    dve.wait_ge(newton, 4 * n + 2)
                    nc.vector.tensor_scalar(ya[:, :], ya[:, :], -0.5, 1.5, ALU.mult, ALU.add).then_inc(newton, 1)
                    dve.wait_ge(newton, 4 * n + 3)
                    nc.vector.tensor_tensor(rstd[:, :], ya[:, :], y0[:, :], ALU.mult).then_inc(newton, 1)
                    dve.wait_ge(newton, 4 * n + 4)
                    nc.vector.scalar_tensor_tensor(nmr[:, :], mv[:, :, 0], -1.0, rstd[:, :], ALU.mult, ALU.mult).then_inc(rstd_done, 1)

                statistics(0, 0)
                for n in range(DC * len(W)):
                    if n == DC:
                        rstd_newton(0)
                    dve.wait_ge(wh_done, n + 1)
                    nc.vector.tensor_tensor(w_l[W[n // DC]][:, n % DC, :], wbanks[n % len(wbanks)][:, :], w_h[W[n // DC]][:, n % DC, :],
                                            ALU.subtract).then_inc(wl_done, 1)

                def keep_last(n, first_of_batch):
                    dve.wait_ge(dx_done, DC * n)
                    if first_of_batch:
                        nc.vector.memset(xt[:, :, 0:1], 0.0).then_inc(carry, 1)
                    else:
                        nc.vector.tensor_copy(xt[:, :, 0:1], xt[:, :, N3:N3 + 1]).then_inc(carry, 1)

                def mixes(n, which):
                    name = "kr"[which]
                    if which:
                        dve.wait_ge(r_mm, T3 * n)
                    else:
                        dve.wait_ge(k_mm, DC * n)

                    def lo(c):
                        at = 2 * DC * n + DC * which + c
                        dve.wait_ge(mh_done, at + 1)
                        nc.vector.tensor_tensor(m_l[name][:, c, :], mix[:, c % 2, :], m_h[name][:, c, :], ALU.subtract).then_inc(ml_done, 1)

                    for c in range(DC):
                        if which == 0:
                            dve.wait_ge(dx_done, DC * n + c + 1)
                        if c >= 2:
                            lo(c - 2)
                        if not (type(n) is int and n == 0 and which == 0 and c < 2):
                            dve.wait_ge(ml_done, 2 * DC * n + DC * which + c - 1)
                        nc.vector.scalar_tensor_tensor(mix[:, c % 2, :], dx[:, c, :], mu[name][:, c:c + 1], xt[:, c, 0:N3],
                                                       ALU.mult, ALU.add).then_inc(mix_done, 1)
                    lo(DC - 2)
                    lo(DC - 1)

                dve.wait_ge(xn_done, T3)
                statistics(1, 1)
                rstd_newton(1)
                dve.wait_ge(mu_in, 32)
                keep_last(0, True)
                mixes(0, 0)
                mixes(0, 1)

                def step(n, i):
                    for c in range(DC):
                        dve.wait_ge(rl_done, DC * n + c + 1 + 2)
                        nc.vector.tensor_tensor(a32[:, c % 2, :], rl[:, c % 2, :], rl[:, c % 2, :], ALU.mult).then_inc(a32_done, 1)
                        dve.wait_ge(a32_done, DC * n + c + 1)
                        dve.wait_ge(ah_done, DC * n + c + 1)
                        nc.vector.tensor_tensor(a_l[:, c, :], a32[:, c % 2, :], a_h[:, c, :], ALU.subtract).then_inc(al_done, 1)
                    if not (type(n) is int and n + 2 > LAST):
                        dve.wait_ge(xn_done, T3 * n + 2 * T3)
                        statistics(n + 2, (i + 2) % TPB3)
                        rstd_newton(n + 2)
                    if not (type(n) is int and n == LAST):
                        keep_last(n + 1, i == TPB3 - 1)
                        mixes(n + 1, 0)
                        mixes(n + 1, 1)
                    for j in range(T3):
                        if j == 0:
                            dve.wait_ge(out_st, 16 * n + 16)
                        dve.wait_ge(v_mm, T3 * n + j + 1)
                        nc.vector.tensor_tensor(res[:, j, :], pr[j][:, :], gate[:, j, :], ALU.mult).then_inc(gv_done, 1)

                steps(dve, step)


def build(nc, x, ctx, mask, Wq, bq, Wk, bk, Wv, bv, Wo, bo, W_r, W_k, W_v, mu_r, mu_k, ident, ramp, ramp_col, out):
    d = dict(ctx=ctx, mask=mask, Wq=Wq, bq=bq, Wk=Wk, bk=bk, Wv=Wv, bv=bv, Wo=Wo, bo=bo, W_r=W_r, W_k=W_k, W_v=W_v,
             mu_r=mu_r, mu_k=mu_k, ident=ident, ramp=ramp, ramp_col=ramp_col,
             x=x.rearrange("b s d -> (b s) d"), out=out.rearrange("b s d -> (b s) d"))
    d["x1"] = nc.dram_tensor("x1_scratch", [B * S, D], F32).ap()
    for n in ("k_h", "k_l"):
        d[n] = nc.dram_tensor(f"{n}_scratch", [P, PAIRS, B * KEYS], F32).ap()
    for n in ("v_h", "v_l"):
        d[n] = nc.dram_tensor(f"{n}_scratch", [P, B, HD], F32).ap()
    with ExitStack() as c:
        def sb(name, shape, dt=F32):
            return c.enter_context(nc.sbuf_tensor(name, shape, dt))
        t = {}
        with ExitStack() as c2:
            def sb2(name, shape, dt=F32):
                return c2.enter_context(nc.sbuf_tensor(name, shape, dt))
            t.update(wq_h=sb2("wq_h", [P, DC, HD], F32R), wq_l=sb2("wq_l", [P, DC, HD], F32R),
                     wo_h=sb2("wo_h", [P, PAIRS, D], F32R), wo_l=sb2("wo_l", [P, PAIRS, D], F32R),
                     bq_col=sb2("bq_col", [P, PAIRS]), bo_row=sb2("bo_row", [P, D]), mask_bias=sb2("mask_bias", [P, B]))
            part1(nc, t, d)
            part2(nc, t, d)
        part3(nc, t, d)


_INS = ['x', 'ctx_1024', 'mask_BxS2_bf1', 'L0_xattn_Wq', 'L0_xattn_bq', 'L0_xattn_Wk', 'L0_xattn_bk', 'L0_xattn_Wv',
        'L0_xattn_bv', 'L0_xattn_Wo', 'L0_xattn_bo', 'L0_ffn_W_r', 'L0_ffn_W_k', 'L0_ffn_W_v', 'L0_ffn_mu_r', 'L0_ffn_mu_k']


def kernel(**inputs):
    import concourse.bacc as bacc
    from concourse.bass_utils import run_bass_kernel_spmd

    nc = bacc.Bacc("TRN2", target_bir_lowering=False, num_devices=1)
    given = [(n, np.ascontiguousarray(inputs[n])) for n in _INS]
    down = (KEYS - np.arange(KEYS)).astype(np.float32)
    given += [("ident", np.eye(P, dtype=np.float32)), ("ramp", np.tile(down, (P, 1))), ("ramp_col", down[:, None].copy())]
    arrays, args = {}, []
    for name, a in given:
        arrays[f"in_{name}_dram"] = a
        args.append(nc.dram_tensor(f"in_{name}_dram", a.shape, mybir.dt.from_np(a.dtype), kind="ExternalInput").ap())
    args.append(nc.dram_tensor("out_0_dram", (B, S, D), F32, kind="ExternalOutput").ap())
    build(nc, *args)
    r = run_bass_kernel_spmd(nc, [arrays], core_ids=[0])
    return r.results[0]["out_0_dram"]
```

```python
import numpy as np
import concourse.bass as bass
from concourse import mybir
from contextlib import ExitStack

F32, F32R, U8 = mybir.dt.float32, mybir.dt.float32r, mybir.dt.uint8
ALU, ACT, AX = mybir.AluOpType, mybir.ActivationFunctionType, mybir.AxisListType

P = 128
B, S, D = 4, 2048, 512
KEYS, HEADS, DH = 128, 16, 64
HD = HEADS * DH
DC = D // P
PAIRS = HEADS // 2
TOK = 256
TT = TOK // P
TPB = S // TOK
TILES = B * TPB
N3 = 512
T3 = N3 // P
TPB3 = S // N3
SCALE = float(DH) ** -0.5
EPS = 1e-5
BIG = 3e38
ONE = 1


def split_passes(nc, out, w_h, w_l, x_h, x_l, first, last):
    nc.tensor.matmul(out, w_h, x_h, start=first, stop=False)
    nc.tensor.matmul(out, w_h, x_l, start=False, stop=False)
    return nc.tensor.matmul(out, w_l, x_h, start=False, stop=last)


def norm_stages(nc, t):
    xa, xn, xa_in, xt_done = t["xa"], t["xn"], t["xa_in"], t["xt_done"]
    stats, var_ready, ln_y0, newton = t["stats"], t["var_ready"], t["ln_y0"], t["newton"]
    rstd_step, rstd_ready, xn_ready = t["rstd_step"], t["rstd_ready"], t["xn_ready"]
    small = t["small"]
    st = small[:, 0:6, :].rearrange("p a b -> p (a b)").rearrange("p (j s) -> p j s", j=TT)
    mv = small[:, 6:8, :]
    ve, y0, ya, rstd, nmr = (small[:, i, :] for i in range(8, 13))

    def statistics(dve, n):
        dve.wait_ge(xa_in, 16 * n + 16)
        for j in range(TT):
            nc.vector.bn_stats(st[:, j, :], xa[:, j, :]).then_inc(stats, 1)
        dve.drain()
        for j in range(TT):
            nc.vector.bn_aggr(mv[:, j, :], st[:, j, :]).then_inc(stats, 1)
        dve.wait_ge(stats, 2 * TT * n + 2 * TT)
        nc.vector.tensor_scalar(ve, mv[:, :, 1], EPS, None, ALU.add).then_inc(var_ready, 1)

    def rsqrt_seed(act, n):
        act.wait_ge(var_ready, n + 1)
        nc.scalar.activation(y0, ve, ACT.Ln).then_inc(ln_y0, 1)
        act.wait_ge(ln_y0, 2 * n + 1)
        nc.scalar.activation(y0, y0, ACT.Exp, scale=-0.5).then_inc(ln_y0, 1)

    def rstd_newton(dve, n):
        dve.wait_ge(ln_y0, 2 * n + 2)
        dve.wait_ge(xn_ready, TT * n)
        nc.vector.tensor_tensor(ya, y0, y0, ALU.mult).then_inc(newton, 1)
        dve.wait_ge(newton, 3 * n + 1)
        nc.vector.tensor_tensor(ya, ya, ve, ALU.mult).then_inc(newton, 1)
        dve.wait_ge(newton, 3 * n + 2)
        nc.vector.tensor_scalar(ya, ya, -0.5, 1.5, ALU.mult, ALU.add).then_inc(newton, 1)
        dve.wait_ge(newton, 3 * n + 3)
        nc.vector.tensor_tensor(rstd, ya, y0, ALU.mult).then_inc(rstd_step, 1)
        dve.wait_ge(rstd_step, n + 1)
        nc.vector.scalar_tensor_tensor(nmr, mv[:, :, 0], -1.0, rstd, ALU.mult, ALU.mult).then_inc(rstd_ready, 1)

    def normalise(act, n, j):
        if j == 0:
            act.wait_ge(rstd_ready, n + 1)
            act.wait_ge(xt_done, 2 * n)
        nc.scalar.activation(xn[:, j, :], xa[:, j, :], ACT.Identity, bias=nmr[:, j:j + 1],
                             scale=rstd[:, j:j + 1]).then_inc(xn_ready, 1)

    return statistics, rsqrt_seed, rstd_newton, normalise


def part1(nc, t, d):
    with ExitStack() as ctx:
        def sb(name, shape, dt=F32):
            return ctx.enter_context(nc.sbuf_tensor(name, shape, dt))

        def sem(name):
            return ctx.enter_context(nc.semaphore(name))

        raw = [t["wraw"][:, i, :].rearrange("p (c n) -> p c n", n=512) for i in range(3)]
        wk_h, wk_l = sb("wk_h", [P, DC, HD], F32R), sb("wk_l", [P, DC, HD], F32R)
        wv_h, wv_l = sb("wv_h", [P, DC, HD], F32R), sb("wv_l", [P, DC, HD], F32R)
        ctxn = sb("ctxn", [P, B, D])
        c_h, c_l = sb("c_h", [P, DC, B * KEYS], F32R), sb("c_l", [P, DC, B * KEYS], F32R)
        kout_h, kout_l = sb("kout_h", [P, 4, B * KEYS], F32R), sb("kout_l", [P, 4, B * KEYS], F32R)
        v32 = sb("v32", [P, 2, 512])
        bv_row = ctxn[:, 0:2, :].rearrange("p b n -> p (b n)")
        bk_col = sb("bk_col", [P, PAIRS])
        ramp, ramp_col = sb("ramp", [P, P]), sb("ramp_col", [P, 1])
        ident = t["ident"]
        mask8 = sb("mask8", [P, B, KEYS], U8)
        mask = kout_h[:, 3, :].bitcast(F32).rearrange("p (b k) -> p b k", b=B)
        sel = kout_l[:, 3, :].bitcast(F32).rearrange("p (b k) -> p b k", b=B)
        diag, ranked = (v32[:, i, :].rearrange("p (b k) -> p b k", b=B) for i in range(2))
        of_batch = sb("of_batch", [P, 3, B])
        best, mcol, first = (of_batch[:, i, :] for i in range(3))
        ps = [ctx.enter_context(nc.psum_tensor(f"p1_{i}", [P, 512], F32)) for i in range(8)]

        bv_in, filled, fill_out = sem("bv_in"), sem("filled"), sem("fill_out")
        small_in, mask_in, ctx_in = sem("small_in"), sem("mask_in"), sem("ctx_in")
        raw_in = [sem(f"raw_in{i}") for i in range(3)]
        w_hi, wlo_pool, wlo_dve = sem("w_hi"), sem("wlo_pool"), sem("wlo_dve")
        dve_step = sem("p1_dve_step")
        sel_ready = sem("sel_ready")
        ctx_t, c_hi, c_lo = sem("ctx_t"), sem("c_hi"), sem("c_lo")
        k_mm, k_hi, k_lo = sem("k_mm"), sem("k_hi"), sem("k_lo")
        v_mm, v_f, v_hi, v_lo = sem("v_mm"), sem("v_f"), sem("v_hi"), sem("v_lo")
        kv_out = [sem(f"kv_out{i}") for i in range(4)]
        statistics, rsqrt_seed, rstd_newton, normalise = norm_stages(nc, t)

        jobs = []
        for w, th, tl in ((d["Wk"], wk_h, wk_l), (d["Wv"], wv_h, wv_l), (d["Wq"], t["wq_h"], t["wq_l"])):
            v = w.rearrange("(c p) n -> p c n", p=P)
            for i in range(2):
                n = slice(512 * i, 512 * i + 512)
                jobs.append((v[:, :, n], th[:, :, n], tl[:, :, n]))
        v = d["Wo"].rearrange("(c p) n -> p c n", p=P)
        jobs += [(v[:, 4 * i:4 * i + 4, :], t["wo_h"][:, 4 * i:4 * i + 4, :], t["wo_l"][:, 4 * i:4 * i + 4, :]) for i in range(2)]

        def raw_ready(eng, i):
            eng.wait_ge(raw_in[i % 3], 16 * (i // 3 + 1))

        with nc.Block() as block:
            @block.sync
            def _(sp):
                sp.dma_start(mask8[:, :, :], d["mask"].partition_broadcast(P)).then_inc(mask_in, 16)
                sp.dma_start(ident[:, :], d["ident"]).then_inc(mask_in, 16)
                sp.dma_start(ramp[:, :], d["ramp"]).then_inc(mask_in, 16)
                sp.dma_start(ramp_col[:, :], d["ramp_col"]).then_inc(mask_in, 16)
                sp.dma_start(ctxn[:, :, :], d["ctx"].rearrange("b k d -> k b d")).then_inc(ctx_in, 16)
                sp.wait_ge(filled, 2)
                for i, m in enumerate((kout_h, kout_l)):
                    sp.dma_start(d["fill"][i:i + 1, :], m[0:1, 0:2, :].bitcast(F32).rearrange("p a n -> p (a n)")).then_inc(fill_out, 16)
                x_t = d["x"].rearrange("(n j p) d -> n p j d", p=P, j=TT)
                for i, (src, _, _) in enumerate(jobs):
                    if i >= 3:
                        sp.wait_ge(wlo_pool, i - 2)
                        sp.wait_ge(wlo_dve, i - 2)
                    sp.dma_start(raw[i % 3], src).then_inc(raw_in[i % 3], 16)
                    if i == 1:
                        sp.dma_start(bk_col[:, :], d["bk"].rearrange("(c p) -> p c", p=P), allow_slow_non_contiguous=True).then_inc(small_in, 16)
                        sp.dma_start(t["bq_col"][:, :], d["bq"].rearrange("(c p) -> p c", p=P), allow_slow_non_contiguous=True).then_inc(small_in, 16)
                        sp.dma_start(t["bo_row"][:, :], d["bo"].partition_broadcast(P)).then_inc(small_in, 16)
                    if i == 4:
                        sp.wait_ge(ctx_t, DC)
                        sp.dma_start(bv_row, d["bv"].partition_broadcast(P)).then_inc(bv_in, 16)
                    if i == 2:
                        sp.dma_start(t["xa"], x_t[0]).then_inc(t["xa_in"], 16)
                sp.wait_ge(t["xn_ready"], TT)
                sp.dma_start(t["xa"], x_t[1]).then_inc(t["xa_in"], 16)
                sp.wait_ge(small_in, 48)

            @block.scalar
            def _(act):
                nc.scalar.preload_act_table_set("natural_log_exp_and_others")

                def weight_hi(i):
                    raw_ready(act, i)
                    nc.scalar.activation(jobs[i][1], raw[i % 3], ACT.Identity).then_inc(w_hi, 1)

                def store(to_h, to_l, i, hi, lo):
                    act.wait_ge(lo, i + 1)
                    act.wait_ge(hi, i + 1)
                    act.dma_start(to_h, kout_h[:, i % 4, :].bitcast(F32)).then_inc(kv_out[i % 4], 16)
                    act.dma_start(to_l, kout_l[:, i % 4, :].bitcast(F32)).then_inc(kv_out[i % 4], 16)

                def store_keys(c):
                    store(d["k_h"][:, c, :], d["k_l"][:, c, :], c, k_hi, k_lo)

                def store_values(i):
                    b, n = i % B, slice(i // B * 512, i // B * 512 + 512)
                    store(d["v_h"][:, b, n], d["v_l"][:, b, n], i, v_hi, v_lo)

                weight_hi(0)
                for c in range(DC):
                    act.wait_ge(ctx_t, c + 1)
                    nc.scalar.activation(c_h[:, c, :], ps[4 + c][:, :], ACT.Identity).then_inc(c_hi, 1)
                weight_hi(1)
                rsqrt_seed(act, 0)
                weight_hi(2)
                for j in range(TT):
                    normalise(act, 0, j)
                act.wait_ge(small_in, 48)
                act.wait_ge(fill_out, 32)
                for c in range(PAIRS):
                    act.wait_ge(k_mm, c + 1)
                    if c >= 4:
                        act.wait_ge(kv_out[c % 4], 32)
                    nc.scalar.activation(kout_h[:, c % 4, :], ps[c % 4][:, :], ACT.Identity,
                                         bias=bk_col[:, c:c + 1]).then_inc(k_hi, 1)
                    if c:
                        store_keys(c - 1)
                    if c in (1, 4, 6):
                        weight_hi({1: 3, 4: 4, 6: 5}[c])
                store_keys(PAIRS - 1)
                for i in range(2 * B):
                    act.wait_ge(v_f, i + 1)
                    act.wait_ge(kv_out[i % 4], 32 * (PAIRS // 4 + i // 4))
                    nc.scalar.activation(kout_h[:, i % 4, :], v32[:, i % 2, :], ACT.Identity).then_inc(v_hi, 1)
                    if i:
                        store_values(i - 1)
                    if i in (1, 3):
                        weight_hi(6 + i // 2)
                store_values(2 * B - 1)
                for i in range(4):
                    act.wait_ge(kv_out[i], 32 * (PAIRS + 2 * B) // 4)

            @block.gpsimd
            def _(pool):
                nc.gpsimd.memset(kout_h[:, 0:2, :].bitcast(F32), 0.0).then_inc(filled, 1)
                nc.gpsimd.memset(kout_l[:, 0:2, :].bitcast(F32), 1.0).then_inc(filled, 1)
                for i, (_, th, tl) in enumerate(jobs):
                    pool.wait_ge(w_hi, i + 1)
                    nc.gpsimd.tensor_tensor(tl[:, 0:2, :], raw[i % 3][:, 0:2, :], th[:, 0:2, :], ALU.subtract).then_inc(wlo_pool, 1)

            @block.vector
            def _(dve):
                steps = [0]

                def chained(ins):
                    steps[0] += 1
                    ins.then_inc(dve_step, 1)
                    dve.wait_ge(dve_step, steps[0])

                bcast = lambda x: x.unsqueeze(1).broadcast_to([P, B, KEYS])
                dve.wait_ge(mask_in, 64)
                chained(nc.vector.tensor_copy(mask[:, :, :], mask8[:, :, :]))
                chained(nc.vector.tensor_tensor(diag[:, :, :], mask[:, :, :], bcast(ident[:, :]), ALU.mult))
                chained(nc.vector.tensor_tensor(ranked[:, :, :], mask[:, :, :], bcast(ramp[:, :]), ALU.mult))
                chained(nc.vector.tensor_reduce(best[:, :], ranked[:, :, :], axis=AX.X, op=ALU.max))
                chained(nc.vector.tensor_reduce(mcol[:, :], diag[:, :, :], axis=AX.X, op=ALU.add))
                chained(nc.vector.tensor_scalar(first[:, :], best[:, :], ramp_col[:, 0:1], None, ALU.is_equal))
                chained(nc.vector.tensor_tensor(first[:, :], first[:, :], mcol[:, :], ALU.mult))
                for b in range(B):
                    last = nc.vector.tensor_scalar(ranked[:, b, :], mask[:, b, :], 1.0, first[:, b:b + 1], ALU.subtract, ALU.mult)
                chained(last)
                nc.vector.tensor_tensor(sel[:, :, :], diag[:, :, :], ranked[:, :, :], ALU.subtract).then_inc(sel_ready, 1)

                def weight_lo(i):
                    dve.wait_ge(w_hi, i + 1)
                    nc.vector.tensor_tensor(jobs[i][2][:, 2:4, :], raw[i % 3][:, 2:4, :], jobs[i][1][:, 2:4, :],
                                            ALU.subtract).then_inc(wlo_dve, 1)

                weight_lo(0)
                for c in range(DC):
                    dve.wait_ge(c_hi, c + 1)
                    nc.vector.tensor_tensor(c_l[:, c, :], ps[4 + c][:, :], c_h[:, c, :], ALU.subtract).then_inc(c_lo, 1)
                statistics(dve, 0)
                weight_lo(1)
                rstd_newton(dve, 0)
                chained(nc.vector.tensor_scalar(t["mask_bias"][:, :], mcol[:, :], 1.0, BIG, ALU.subtract, ALU.mult))
                weight_lo(2)
                dve.wait_ge(small_in, 48)
                dve.wait_ge(fill_out, 32)
                for c in range(PAIRS):
                    dve.wait_ge(k_hi, c + 1)
                    if c >= 4:
                        dve.wait_ge(kv_out[c % 4], 32)
                    nc.vector.scalar_tensor_tensor(kout_l[:, c % 4, :], ps[c % 4][:, :], bk_col[:, c:c + 1],
                                                   kout_h[:, c % 4, :], ALU.add, ALU.subtract).then_inc(k_lo, 1)
                    if c in (2, 5, 7):
                        weight_lo(3 + c // 3)

                def value_lo(i):
                    dve.wait_ge(v_hi, i + 1)
                    nc.vector.tensor_tensor(kout_l[:, i % 4, :], v32[:, i % 2, :], kout_h[:, i % 4, :], ALU.subtract).then_inc(v_lo, 1)

                dve.wait_ge(bv_in, 16)
                for i in range(2 * B):
                    half = i // B
                    dve.wait_ge(v_mm, i + 1)
                    if i >= 2:
                        dve.wait_ge(v_lo, i - 1)
                    nc.vector.tensor_tensor(v32[:, i % 2, :], ps[i % 4][:, :], bv_row[:, half * 512:half * 512 + 512], ALU.add).then_inc(v_f, 1)
                    if i:
                        value_lo(i - 1)
                    if i in (2, 4):
                        weight_lo(5 + i // 2)
                value_lo(2 * B - 1)

            @block.tensor
            def _(pe):
                pe.wait_ge(ctx_in, 16)
                pe.wait_ge(sel_ready, 1)
                for c in range(DC):
                    for b in range(B):
                        last = nc.tensor.matmul(ps[4 + c][:, b * KEYS:(b + 1) * KEYS], ctxn[:, b, c * P:(c + 1) * P],
                                                sel[:, b, :], start=True, stop=True)
                    last.then_inc(ctx_t, 1)
                for c in range(PAIRS):
                    if c % 4 == 0:
                        pe.wait_ge(wlo_pool, 1 + c // 4)
                        pe.wait_ge(wlo_dve, 1 + c // 4)
                    if c >= 4:
                        pe.wait_ge(k_lo, c - 3)
                    for k in range(DC):
                        if c == 0:
                            pe.wait_ge(c_lo, k + 1)
                        last = split_passes(nc, ps[c % 4][:, :], wk_h[:, k, c * P:(c + 1) * P], wk_l[:, k, c * P:(c + 1) * P],
                                            c_h[:, k, :], c_l[:, k, :], k == 0, k == DC - 1)
                    last.then_inc(k_mm, 1)
                for i in range(2 * B):
                    half, b = i // B, i % B
                    n, key = slice(half * 512, half * 512 + 512), slice(b * KEYS, (b + 1) * KEYS)
                    if b == 0:
                        pe.wait_ge(wlo_pool, 3 + half)
                        pe.wait_ge(wlo_dve, 3 + half)
                    if i < 4:
                        pe.wait_ge(k_lo, PAIRS - 3 + i)
                    else:
                        pe.wait_ge(v_f, i - 3)
                    for k in range(DC):
                        last = split_passes(nc, ps[i % 4][:, :], c_h[:, k, key], c_l[:, k, key],
                                            wv_h[:, k, n], wv_l[:, k, n], k == 0, k == DC - 1)
                    last.then_inc(v_mm, 1)


def part2(nc, t, d):
    with ExitStack() as ctx:
        def sb(name, shape, dt=F32):
            return ctx.enter_context(nc.sbuf_tensor(name, shape, dt))

        def sem(name):
            return ctx.enter_context(nc.semaphore(name))

        def bank(name):
            return ctx.enter_context(nc.psum_tensor(name, [P, 512], F32))

        def in_wraw(name, third, shape):
            return nc.alloc_sbuf_tensor_at(name, shape, F32R, offset=t["wraw_at"] + third * 4 * DC * D)

        kz_h = sb("kz_h", [P, PAIRS, 2, KEYS], F32R)
        kz_l = sb("kz_l", [P, PAIRS, 2, KEYS], F32R)
        kg = in_wraw("kg", 0, [P, PAIRS, 2, KEYS])
        kb = sb("kb", [DH + 1, PAIRS, 2, KEYS], F32R)
        v1_h = sb("v1_h", [P, PAIRS, 2, P], F32R)
        vz_l = sb("vz_l", [P, PAIRS, 2, P], F32R)
        ident = t["ident"]
        xa, xn, xa_in, xn_ready, xt_done = t["xa"], t["xn"], t["xa_in"], t["xn_ready"], t["xt_done"]
        x_h, x_l = in_wraw("x_h", 1, [P, 2, DC, TOK]), in_wraw("x_l", 2, [P, 2, DC, TOK])
        q_h = sb("q_h", [P, PAIRS, TOK], F32R)
        q_l = sb("q_l", [DH + 1, HEADS, TOK], F32R)
        e32, e_h, e_l = sb("e32", [P, 2, 512]), sb("e_h", [P, 2, 512], F32R), sb("e_l", [P, 2, 512], F32R)
        lnz, inv0, res0, ninv = sb("lnz", [P, TOK]), sb("inv0", [P, 2, TOK]), sb("res0", [P, TOK]), sb("ninv", [P, TOK])
        o32 = sb("o32", [P, 2, TOK])
        o_h, o_l = sb("o_h", [P, PAIRS, TOK], F32R), sb("o_l", [P, PAIRS, TOK], F32R)
        nmax, nmax_t = sb("nmax", [P, TT, HEADS]), sb("nmax_t", [PAIRS, 2, TOK], F32R)
        xr = sb("xr", [P, TT, D])
        stage = sb("stage", [P, 2, 512])
        mb = t["small"][:, 13, :]
        statistics, rsqrt_seed, rstd_newton, normalise = norm_stages(nc, t)
        pq, px, py = [bank("pq0"), bank("pq1")], [bank("px0"), bank("px1")], [bank("py0"), bank("py1")]
        psc, pg = bank("psc"), bank("pg")

        mb_in, next_in = [sem("mb_in0"), sem("mb_in1")], sem("next_in")
        kg_in, k_in, v_in = ([sem(f"{n}{i}") for i in range(2)] for n in ("kg_in", "k_in", "v_in"))
        const_in, kg_set, v_set = sem("const_in"), sem("kg_set"), sem("v_set")
        xr_in, m_in, x1_out = sem("xr_in"), sem("m_in"), sem("x1_out")
        xh_done, xl_done = sem("xh_done"), sem("xl_done")
        q_mm, qh_done, ql_done = sem("q_mm"), sem("qh_done"), sem("ql_done")
        g_mm, max_done, maxt_mm, maxt_done = sem("g_mm"), sem("max_done"), sem("maxt_mm"), sem("maxt_done")
        s_mm, exp_done, el_done, pv_mm = sem("s_mm"), sem("exp_done"), sem("el_done"), sem("pv_mm")
        lnz_done, inv0_done, norm_step, o_done = sem("lnz_done"), sem("inv0_done"), sem("norm_step"), sem("o_done")
        oh_done, ol_done, xb_done = sem("oh_done"), sem("ol_done"), sem("xb_done")
        y_mm, y_read, x1_done = sem("y_mm"), sem("y_read"), sem("x1_done")
        AHEAD = 2

        x_t = d["x"].rearrange("(n j p) d -> n p j d", p=P, j=TT)
        x1_t = d["x1"].rearrange("(n j p) d -> n p j d", p=P, j=TT)

        def steps(eng, step):
            step(0, 0, 0, first=True, opens=True)
            with eng.Fori(0, B - 1) as b:
                with eng.Fori(0, (TPB - 2) // 2) as i:
                    step(b * TPB + i * 2 + 1, b, 1)
                    step(b * TPB + i * 2 + 2, b, 0)
                step(b * TPB + (TPB - 1), b, 1, switch=True)
                step(b * TPB + TPB, b + 1, 0, opens=True)
            with eng.Fori(0, (TPB - 4) // 2) as i:
                step(i * 2 + (B - 1) * TPB + 1, B - 1, 1)
                step(i * 2 + (B - 1) * TPB + 2, B - 1, 0)
            step(TILES - 3, B - 1, 1, third_next=False)
            step(TILES - 2, B - 1, 0, third_next=False, after_next=False)
            step(TILES - 1, B - 1, 1, third_next=False, after_next=False, next_tile=False)

        def behind(T, p, lag, first):
            if p >= lag:
                return [(T, p - lag)]
            return [] if first else [(T - 1, PAIRS + p - lag)]

        KG, KK, VV = 2, 6, 4
        HALF = [slice(0, PAIRS // 2), slice(PAIRS // 2, PAIRS)]

        with nc.Block() as block:
            @block.sync
            def _(sp):
                def key_slice(part, b, r, half):
                    return d[part][r, HALF[half], bass.ts(b, KEYS)]

                def load_kg(b, half):
                    for h in range(2):
                        r = slice(h * DH, (h + 1) * DH)
                        sp.dma_start(kg[r, HALF[half], h, :].bitcast(F32), key_slice("k_h", b, r, half)).then_inc(kg_in[half], 16)

                def load_k(b, half):
                    for h in range(2):
                        r, p = slice(h * DH, (h + 1) * DH), HALF[half]
                        sp.dma_start(kz_h[r, p, h, :].bitcast(F32), key_slice("k_h", b, r, half)).then_inc(k_in[half], 16)
                        sp.dma_start(kz_l[r, p, h, :].bitcast(F32), key_slice("k_l", b, r, half)).then_inc(k_in[half], 16)
                        sp.dma_start(kb[0:DH, p, h, :].bitcast(F32), key_slice("k_h", b, r, half)).then_inc(k_in[half], 16)

                def load_v(b, half):
                    for part, to in (("v_h", v1_h), ("v_l", vz_l)):
                        src = d[part][:, bass.ts(b, 1), :].rearrange("p o (c h e) -> p (o c) h e", h=2, e=DH)
                        for h in range(2):
                            sp.dma_start(to[:, HALF[half], h, h * DH:(h + 1) * DH].bitcast(F32),
                                         src[:, HALF[half], h, :]).then_inc(v_in[half], 16)

                def load_x(n, to, s):
                    sp.dma_start(to[:, :, :], x_t[n]).then_inc(s, 16)

                def max_row(n, half):
                    sp.wait_ge(maxt_done, 2 * n + half + 1)
                    sp.dma_start(q_l[DH:DH + 1, half * PAIRS:(half + 1) * PAIRS, :].bitcast(F32),
                                 nmax_t[:, half, :].bitcast(F32)).then_inc(m_in, 16)

                sp.dma_start(mb[:, 0:1], t["mask_bias"][:, 0:1]).then_inc(mb_in[0], 16)
                for half in range(2):
                    load_kg(0, half)
                for m in (kz_h, kz_l):
                    for h in range(2):
                        sp.dma_start(m[(1 - h) * DH:(2 - h) * DH, :, h, :].bitcast(F32),
                                     d["fill"][0].partition_broadcast(DH).rearrange("p (c k) -> p c k", c=PAIRS)).then_inc(const_in, 16)
                for half in HALF:
                    sp.dma_start(kb[DH:DH + 1, half, :, :].bitcast(F32),
                                 d["fill"][1:2, :].rearrange("o (c h k) -> o c h k", c=PAIRS // 2, h=2)).then_inc(const_in, 16)
                for half in range(2):
                    load_k(0, half)
                for half in range(2):
                    load_v(0, half)
                sp.wait_ge(xn_ready, 2 * TT)
                load_x(2, xa, xa_in)
                max_row(0, 0)

                def store(R):
                    sp.wait_ge(x1_done, TT * R + TT + ONE)
                    sp.dma_start(x1_t[R], xr[:, :, :]).then_inc(x1_out, 16)

                def step(T, b, odd, switch=False, opens=False, third_next=True, after_next=True, next_tile=True, first=False):
                    if opens:
                        sp.wait_ge(exp_done, PAIRS * T + AHEAD)
                        sp.dma_start(mb[:, 1:2], t["mask_bias"][:, bass.ts(b, 1)]).then_inc(mb_in[1], 16)
                    if switch:
                        sp.wait_ge(g_mm, PAIRS * T + PAIRS // 2)
                        load_kg(b + 1, 0)
                    if not first:
                        sp.wait_ge(x1_out, T * 16)
                        load_x(T - 1, xr, xr_in)
                    max_row(T, 1)
                    if switch:
                        sp.wait_ge(g_mm, PAIRS * T + PAIRS)
                        load_kg(b + 1, 1)
                    if third_next:
                        sp.wait_ge(xn_ready, TT * T + 3 * TT)
                        load_x(T + 3, xa, xa_in)
                    if not next_tile:
                        sp.wait_ge(g_mm, PAIRS * TILES)
                        sp.wait_ge(q_mm, PAIRS * TILES)
                        sp.wait_ge(xt_done, 2 * TILES)
                        x1_first = d["x1"].rearrange("(n j p) d -> n p j d", p=P, j=T3)[0]
                        sp.dma_start(t["rows"][:, :, :], x1_first).then_inc(next_in, 16)
                        for i, w in enumerate(("W_k", "W_r", "W_v")):
                            sp.dma_start(t["wraw"][:, i, :].rearrange("p (c n) -> p c n", c=DC),
                                         d[w].rearrange("(c p) n -> p c n", p=P)).then_inc(next_in, 16)
                    if switch:
                        sp.wait_ge(s_mm, PAIRS * T + PAIRS // 2)
                        load_k(b + 1, 0)
                        sp.dma_start(mb[:, 0:1], t["mask_bias"][:, bass.ts(b + 1, 1)]).then_inc(mb_in[0], 16)
                        sp.wait_ge(pv_mm, PAIRS * T + PAIRS // 2 + AHEAD)
                        load_v(b + 1, 0)
                    if next_tile:
                        max_row(T + 1, 0)
                    if switch:
                        sp.wait_ge(s_mm, PAIRS * T + PAIRS)
                        load_k(b + 1, 1)
                    if not first:
                        store(T - 1)
                    if switch:
                        sp.wait_ge(pv_mm, PAIRS * T + PAIRS + AHEAD)
                        load_v(b + 1, 1)

                steps(sp, step)
                sp.wait_ge(x1_out, TILES * 16)
                load_x(TILES - 1, xr, xr_in)
                for j in range(TT):
                    sp.wait_ge(x1_done, TT * (TILES - 1) + j + 1 + ONE)
                    sp.dma_start(x1_t[TILES - 1][:, j, :], xr[:, j, :]).then_inc(x1_out, 16)
                sp.wait_ge(x1_out, TILES * 16 + 32)
                sp.wait_ge(next_in, 64)

            @block.tensor
            def _(pe):
                def transposes(n, k, bank=pg):
                    if k == 0:
                        pe.wait_ge(xn_ready, TT * n + TT)
                    for c in (2 * k, 2 * k + 1):
                        for j in range(TT):
                            at = (c % 2) * TOK + j * P
                            last = nc.tensor.transpose(bank[:, at:at + P], xn[:, j, c * P:(c + 1) * P], ident[:, :])
                    last.then_inc(xt_done, 1)

                def query(n, p, odd):
                    if not (type(n) is int and n == 0 and p < 2):
                        pe.wait_ge(ql_done, PAIRS * n + p - 1)
                    w = slice(p * P, (p + 1) * P)
                    for k in range(DC):
                        if p == 0 and k % 2 == 0:
                            pe.wait_ge(xl_done, 2 * n + k // 2 + 1)
                        last = split_passes(nc, pq[p % 2][:, 0:TOK], t["wq_h"][:, k, w], t["wq_l"][:, k, w],
                                            x_h[:, odd, k, :], x_l[:, odd, k, :], k == 0, k == DC - 1)
                    last.then_inc(q_mm, 1)

                def guard(n, p, batches=None):
                    if batches is not None and p % (PAIRS // 2) == 0:
                        pe.wait_ge(kg_in[p // (PAIRS // 2)], 16 * KG * batches)
                    pe.wait_ge(max_done, PAIRS * n + p)
                    pe.wait_ge(qh_done, PAIRS * n + p + 1)
                    for j in range(TT):
                        last = nc.tensor.matmul(pg[:, j * TOK:(j + 1) * TOK], q_h[:, p, j * P:(j + 1) * P],
                                                kg[:, p, :, :].rearrange("p h k -> p (h k)"), start=True, stop=True)
                    last.then_inc(g_mm, 1)

                def max_transpose(n, half, bank=pg):
                    for j in range(TT):
                        last = nc.tensor.transpose(bank[0:PAIRS, j * P:(j + 1) * P],
                                                   nmax[:, j, half * PAIRS:(half + 1) * PAIRS], ident[:, :])
                    last.then_inc(maxt_mm, 1)

                def scores(T, p, b):
                    if p % (PAIRS // 2) == 0:
                        half = p // (PAIRS // 2)
                        pe.wait_ge(m_in, 32 * T + 16 * half + 16)
                        pe.wait_ge(k_in[half], 16 * KK * b + 16 * KK)
                    pe.wait_ge(exp_done, PAIRS * T + p + AHEAD)
                    for h in range(2):
                        out = psc[:, h * TOK:(h + 1) * TOK]
                        nc.tensor.matmul(out, kz_h[:, p, h, :], q_h[:, p, :], start=True, stop=False)
                        nc.tensor.matmul(out, kz_l[:, p, h, :], q_h[:, p, :], start=False, stop=False)
                        last = nc.tensor.matmul(out, kb[:, p, h, :], q_l[:, 2 * p + h, :], start=False, stop=True)
                    last.then_inc(s_mm, 1)

                def values(T, p, b):
                    if p % (PAIRS // 2) == 0:
                        pe.wait_ge(v_in[p // (PAIRS // 2)], 16 * VV * b + 16 * VV)
                    pe.wait_ge(o_done, PAIRS * T + p - 2 + 1 + AHEAD)
                    pe.wait_ge(el_done, PAIRS * T + p + 1)
                    for h in range(2):
                        out, col = px[p % 2][:, h * TOK:(h + 1) * TOK], slice(h * TOK, (h + 1) * TOK)
                        last = split_passes(nc, out, v1_h[:, p, h, :], vz_l[:, p, h, :],
                                            e_h[:, p % 2, col], e_l[:, p % 2, col], True, True)
                    last.then_inc(pv_mm, 1)

                def output(R, c):
                    if c == 0:
                        pe.wait_ge(y_read, TT * R + ONE)
                    pe.wait_ge(ol_done, PAIRS * R + c + 1 + AHEAD)
                    for j in range(TT):
                        w = slice(j * P, (j + 1) * P)
                        last = split_passes(nc, py[j][:, :], o_h[:, c, w], o_l[:, c, w],
                                            t["wo_h"][:, c, :], t["wo_l"][:, c, :], c == 0, c == PAIRS - 1)
                        if c == PAIRS - 1:
                            last.then_inc(y_mm, 1)

                def between_maxima(T, p, after_next=True, next_tile=True):
                    if p == 1:
                        pe.wait_ge(max_done, PAIRS * T + PAIRS)
                        max_transpose(T, 1)
                    if p in (4, 6) and after_next:
                        pe.wait_ge(max_done, PAIRS * T + PAIRS + p - 1)
                        transposes(T + 2, p // 2 - 2)
                    if p == 5 and next_tile:
                        pe.wait_ge(max_done, PAIRS * T + PAIRS + p - 1)
                        max_transpose(T + 1, 0)

                def bank_pg_read(T, p, after_next=True, next_tile=True):
                    if p == 1:
                        pe.wait_ge(maxt_done, 2 * T + 2)
                    if p in (4, 6) and after_next:
                        pe.wait_ge(xh_done, 2 * T + 4 + p // 2 - 1)
                    if p == 5 and next_tile:
                        pe.wait_ge(maxt_done, 2 * T + 3)

                for k in range(2):
                    transposes(0, k, py[k])
                for p in range(PAIRS):
                    query(0, p, 0)
                    if p == 3:
                        for k in range(2):
                            transposes(1, k, px[k])
                    if p == 1:
                        pe.wait_ge(kg_set, 1)
                    if p:
                        guard(0, p - 1, 1)
                pe.wait_ge(max_done, PAIRS // 2)
                max_transpose(0, 0, psc)

                pe.wait_ge(const_in, 96)
                pe.wait_ge(v_set, 2)

                def step(T, b, odd, switch=False, opens=False, third_next=True, after_next=True, next_tile=True, first=False):
                    for p in range(PAIRS):
                        scores(T, p, b)
                        if p == PAIRS - 1 and not first:
                            output(T - 1, p)
                        between_maxima(T, p, after_next, next_tile)
                        if next_tile:
                            query(T + 1, p, 1 - odd)
                        if 0 < p < PAIRS - 1 and not first:
                            output(T - 1, p)
                        bank_pg_read(T, p, after_next, next_tile)
                        if p:
                            if next_tile:
                                guard(T + 1, p - 1, b + 2 if switch else None)
                            values(T, p - 1, b)
                        else:
                            guard(T, PAIRS - 1)
                            if not first:
                                values(T - 1, PAIRS - 1, None)
                                output(T - 1, 0)

                steps(pe, step)
                values(TILES - 1, PAIRS - 1, None)
                for c in range(PAIRS):
                    output(TILES - 1, c)

            @block.scalar
            def _(act):
                nc.scalar.preload_act_table_set("natural_log_exp_and_others")
                act.sem_inc(exp_done, AHEAD)
                act.sem_inc(inv0_done, ONE)

                def x_hi(n, k, odd, bank=pg):
                    if not (type(n) is int and n < 3):
                        act.wait_ge(x1_done, TT * (n - 3) + ONE)
                    if not (type(n) is int and n == 0):
                        act.wait_ge(xl_done, 2 * n + k - 1)
                    act.wait_ge(xt_done, 2 * n + k + 1)
                    nc.scalar.activation(x_h[:, odd, 2 * k:2 * k + 2, :].rearrange("p c n -> p (c n)"), bank[:, :], ACT.Identity)
                    nc.scalar.activation(stage[:, k, :], bank[:, :], ACT.Identity).then_inc(xh_done, 1)

                def q_hi(n, p):
                    act.wait_ge(q_mm, PAIRS * n + p + 1)
                    nc.scalar.activation(q_h[:, p, :], pq[p % 2][:, 0:TOK], ACT.Identity,
                                         bias=t["bq_col"][:, p:p + 1]).then_inc(qh_done, 1)

                def max_hi(n, half, bank=pg):
                    act.wait_ge(maxt_mm, 2 * n + half + 1)
                    nc.scalar.activation(nmax_t[:, half, :], bank[0:PAIRS, 0:TOK], ACT.Identity).then_inc(maxt_done, 1)

                def exponentials(T, p, b, col):
                    if p == 0:
                        act.wait_ge(mb_in[col], 16 * b + 16)
                    act.wait_ge(s_mm, PAIRS * T + p + 1)
                    act.wait_ge(pv_mm, PAIRS * T + p - 2 + 1 + AHEAD)
                    nc.scalar.activation(e32[:, p % 2, :], psc[:, :], ACT.Exp, bias=mb[:, col:col + 1], scale=SCALE)
                    nc.scalar.activation(e_h[:, p % 2, :], psc[:, :], ACT.Exp, bias=mb[:, col:col + 1],
                                         scale=SCALE).then_inc(exp_done, 1)

                def sum_inverse_seed(T, p):
                    act.wait_ge(inv0_done, PAIRS * T + p + ONE)
                    act.wait_ge(pv_mm, PAIRS * T + p + 1 + AHEAD)
                    nc.scalar.activation(lnz[DH:P, :], px[p % 2][DH:P, 0:TOK], ACT.Ln)
                    nc.scalar.activation(lnz[0:DH, :], px[p % 2][0:DH, TOK:2 * TOK], ACT.Ln).then_inc(lnz_done, 1)
                    act.wait_ge(lnz_done, PAIRS * T + p + 1)
                    act.wait_ge(o_done, PAIRS * T + p - 2 + 1 + AHEAD)
                    nc.scalar.activation(inv0[:, p % 2, :], lnz[:, :], ACT.Exp, scale=-1.0).then_inc(inv0_done, 1)

                def o_hi(T, p):
                    act.wait_ge(o_done, PAIRS * T + p + 1 + AHEAD)
                    nc.scalar.activation(o_h[:, p, :], o32[:, p % 2, :], ACT.Identity).then_inc(oh_done, 1)

                def y_copy(R, last=False):
                    act.wait_ge(x1_done, TT * R + ONE)
                    act.wait_ge(xl_done, 2 * TILES if last else 2 * R + 8)
                    for j in range(TT):
                        act.wait_ge(y_mm, TT * R + j + 1)
                        nc.scalar.activation(stage[:, j, :], py[j][:, :], ACT.Identity).then_inc(y_read, 1)

                for k in range(2):
                    x_hi(0, k, 0, py[k])
                for p in range(PAIRS):
                    q_hi(0, p)
                    if p == 0:
                        rsqrt_seed(act, 1)
                    if p == 1:
                        normalise(act, 1, 0)
                        normalise(act, 1, 1)
                    if p in (4, 5):
                        x_hi(1, p - 4, 1, px[p - 4])
                max_hi(0, 0, psc)
                rsqrt_seed(act, 2)

                def step(T, b, odd, switch=False, opens=False, third_next=True, after_next=True, next_tile=True, first=False):
                    for p in range(PAIRS):
                        for at in behind(T, p, 2, first):
                            sum_inverse_seed(*at)
                        exponentials(T, p, b, 0 if opens else 1)
                        if p == 1:
                            max_hi(T, 1)
                        if p == 5 and next_tile:
                            max_hi(T + 1, 0)
                        if after_next and p in (4, 6):
                            x_hi(T + 2, p // 2 - 2, odd)
                        if p == PAIRS - 1 and not first:
                            y_copy(T - 1, not after_next)
                        if third_next and p == PAIRS - 1:
                            rsqrt_seed(act, T + 3)
                        if next_tile:
                            q_hi(T + 1, p)
                        for at in behind(T, p, 3, first):
                            o_hi(*at)
                        if after_next and p in (1, 2):
                            normalise(act, T + 2, p - 1)

                steps(act, step)
                for p in (PAIRS - 2, PAIRS - 1):
                    sum_inverse_seed(TILES - 1, p)
                    o_hi(TILES - 1, p - 1)
                o_hi(TILES - 1, PAIRS - 1)
                nc.scalar.preload_act_table_set("sigmoid_and_others")

            @block.gpsimd
            def _(pool):
                pool.sem_inc(ol_done, AHEAD)

                def e_lo(T, p):
                    pool.wait_ge(exp_done, PAIRS * T + p + 1 + AHEAD)
                    nc.gpsimd.tensor_tensor(e_l[:, p % 2, :], e32[:, p % 2, :], e_h[:, p % 2, :], ALU.subtract).then_inc(el_done, 1)

                def o_lo(T, p):
                    pool.wait_ge(oh_done, PAIRS * T + p + 1)
                    nc.gpsimd.tensor_tensor(o_l[:, p, :], o32[:, p % 2, :], o_h[:, p, :], ALU.subtract).then_inc(ol_done, 1)

                def x_lo(n, k, odd):
                    pool.wait_ge(xh_done, 2 * n + k + 1)
                    nc.gpsimd.tensor_tensor(x_l[:, odd, 2 * k:2 * k + 2, :].rearrange("p c n -> p (c n)"), stage[:, k, :],
                                            x_h[:, odd, 2 * k:2 * k + 2, :].rearrange("p c n -> p (c n)"), ALU.subtract).then_inc(xl_done, 1)

                def residual(R):
                    pool.wait_ge(xb_done, R + 1)
                    for j in range(TT):
                        pool.wait_ge(y_read, TT * R + j + 1 + ONE)
                        nc.gpsimd.tensor_tensor(xr[:, j, :], stage[:, j, :], xr[:, j, :], ALU.add).then_inc(x1_done, 1)

                def add_bo(R):
                    pool.wait_ge(xr_in, 16 * R + 16)
                    nc.gpsimd.tensor_tensor(xr[:, :, :], xr[:, :, :], t["bo_row"][:, :].unsqueeze(1).broadcast_to([P, TT, D]),
                                            ALU.add).then_inc(xb_done, 1)

                x_lo(0, 0, 0)
                x_lo(0, 1, 0)
                for m, value in ((v1_h, 1.0), (vz_l, 0.0)):
                    nc.gpsimd.memset(m[:, :, 0, DH:P].bitcast(F32), value)
                    nc.gpsimd.memset(m[:, :, 1, 0:DH].bitcast(F32), value).then_inc(v_set, 1)
                x_lo(1, 0, 1)
                x_lo(1, 1, 1)

                def step(T, b, odd, switch=False, opens=False, third_next=True, after_next=True, next_tile=True, first=False):
                    for p in range(PAIRS):
                        e_lo(T, p)
                        for at in behind(T, p, 3, first):
                            o_lo(*at)
                        if after_next and p in (4, 6):
                            x_lo(T + 2, (p - 4) // 2, odd)
                        if p == 3 and not first:
                            add_bo(T - 1)
                        if p == PAIRS - 1 and not first:
                            residual(T - 1)

                steps(pool, step)
                for p in range(PAIRS - 3, PAIRS):
                    o_lo(TILES - 1, p)
                add_bo(TILES - 1)

            @block.vector
            def _(dve):
                nc.vector.memset(kg[0:DH, :, 1, :].bitcast(F32), 0.0)
                nc.vector.memset(kg[DH:P, :, 0, :].bitcast(F32), 0.0).then_inc(kg_set, 1)
                dve.sem_inc(pv_mm, AHEAD)
                dve.sem_inc(o_done, AHEAD)
                dve.sem_inc(x1_done, ONE)
                dve.sem_inc(y_read, ONE)
                dve.sem_inc(x1_out, 16)


                def q_lo(n, p):
                    dve.wait_ge(qh_done, PAIRS * n + p + 1)
                    for h in range(2):
                        r = slice(h * DH, (h + 1) * DH)
                        last = nc.vector.scalar_tensor_tensor(q_l[0:DH, 2 * p + h, :], pq[p % 2][r, 0:TOK],
                                                              t["bq_col"][r, p:p + 1], q_h[r, p, :], ALU.add, ALU.subtract)
                    last.then_inc(ql_done, 1)

                def maxima(n, p):
                    dve.wait_ge(g_mm, PAIRS * n + p + 1)
                    nc.vector.tensor_reduce(nmax[:, :, 2 * p:2 * p + 2],
                                            pg[:, :].rearrange("p (j h k) -> p j h k", j=TT, h=2),
                                            axis=AX.X, op=ALU.max, negate=True).then_inc(max_done, 1)

                def divide(T, p):
                    g = PAIRS * T + p
                    dve.wait_ge(inv0_done, g + 1 + ONE)
                    dve.wait_ge(ol_done, g - 2 + 1 + AHEAD)
                    nc.vector.tensor_tensor(res0[DH:P, :], px[p % 2][DH:P, 0:TOK], inv0[DH:P, p % 2, :], ALU.mult)
                    nc.vector.tensor_tensor(res0[0:DH, :], px[p % 2][0:DH, TOK:2 * TOK], inv0[0:DH, p % 2, :], ALU.mult).then_inc(norm_step, 1)
                    dve.wait_ge(norm_step, 2 * g + 1)
                    nc.vector.scalar_tensor_tensor(ninv[:, :], res0[:, :], 2.0, inv0[:, p % 2, :],
                                                   ALU.subtract, ALU.mult).then_inc(norm_step, 1)
                    dve.wait_ge(norm_step, 2 * g + 2)
                    nc.vector.scalar_tensor_tensor(o32[0:DH, p % 2, :], px[p % 2][0:DH, 0:TOK], -1.0, ninv[DH:P, :],
                                                   ALU.mult, ALU.mult)
                    nc.vector.scalar_tensor_tensor(o32[DH:P, p % 2, :], px[p % 2][DH:P, TOK:2 * TOK], -1.0, ninv[0:DH, :],
                                                   ALU.mult, ALU.mult).then_inc(o_done, 1)

                statistics(dve, 1)
                for p in range(PAIRS):
                    if p == 1:
                        rstd_newton(dve, 1)
                    q_lo(0, p)
                    if p:
                        maxima(0, p - 1)
                statistics(dve, 2)

                def step(T, b, odd, switch=False, opens=False, third_next=True, after_next=True, next_tile=True, first=False):
                    for p in range(PAIRS):
                        if p == 0:
                            maxima(T, PAIRS - 1)
                        for at in behind(T, p, 2, first):
                            divide(*at)
                        if next_tile:
                            q_lo(T + 1, p)
                        if p and next_tile:
                            maxima(T + 1, p - 1)
                        if third_next and p == 6:
                            statistics(dve, T + 3)
                        if after_next and p == 0:
                            rstd_newton(dve, T + 2)

                steps(dve, step)
                divide(TILES - 1, PAIRS - 2)
                divide(TILES - 1, PAIRS - 1)
                dve.wait_ge(xb_done, TILES)
                for j in range(TT):
                    dve.wait_ge(y_mm, TT * (TILES - 1) + j + 1)
                    nc.vector.tensor_tensor(xr[:, j, :], py[j][:, :], xr[:, j, :], ALU.add).then_inc(x1_done, 1)


def part3(nc, t, d):
    with ExitStack() as ctx:
        def sb(name, shape, dt=F32):
            return ctx.enter_context(nc.sbuf_tensor(name, shape, dt))

        def sem(name):
            return ctx.enter_context(nc.semaphore(name))

        def bank(name):
            return ctx.enter_context(nc.psum_tensor(name, [P, 512], F32))

        W = ("W_k", "W_r", "W_v")
        w_h = {w: sb(f"{w}_h", [P, DC, D], F32R) for w in W}
        w_l = {w: sb(f"{w}_l", [P, DC, D], F32R) for w in W}
        wraw = t["wraw"][:, :, :].rearrange("p w (c n) -> p w c n", c=DC)
        ident = t["ident"]
        mu = {"r": sb("mu_r", [P, DC]), "k": sb("mu_k", [P, DC])}
        st, mv = sb("st3", [P, T3, 6]), sb("mv3", [P, T3, 2])
        ve, y0, ya, rstd, nmr, power = (sb(n, [P, T3]) for n in ("ve3", "y3", "ya3", "rstd3", "nmr3", "power"))
        x1 = [t["rows"]] + [sb(f"x1_{i}", [P, T3, D]) for i in range(1, TPB3)]
        xn = sb("xn3", [P, T3, D])
        xt = sb("xt", [P, DC, 1 + N3])
        dx = sb("dx", [P, DC, N3])
        mix = sb("mix", [P, 2, N3])
        m_h = {"r": sb("mr_h", [P, DC, N3], F32R), "k": sb("mk_h", [P, DC, N3], F32R)}
        m_l = {"r": sb("mr_l", [P, DC, N3], F32R), "k": sb("mk_l", [P, DC, N3], F32R)}
        rl, a32 = sb("rl", [P, 2, N3]), sb("a32", [P, 2, N3])
        a_h, a_l = sb("a_h", [P, DC, N3], F32R), sb("a_l", [P, DC, N3], F32R)
        gate = sb("gate", [P, T3, D])
        res = sb("res", [P, T3, D])
        pt, pk, pr = [bank("pt0"), bank("pt1")], [bank("pk0"), bank("pk1")], [bank(f"pr{i}") for i in range(4)]

        wbanks = pk + pr + pr + pk
        mu_in = sem("mu_in")
        wt_mm, wh_done, wl_done = sem("wt_mm"), sem("wh_done"), sem("wl_done")
        stats, var_ready, y0_done, newton, rstd_done, power_set = (sem(n) for n in (
            "stats3", "var3_ready", "y03_done", "newton3", "rstd3_done", "power_set"))
        x1_in = [sem(f"x1_in{i}") for i in range(TPB3)]
        xn_done, xt_mm, xt_cp, carry, dx_done = sem("xn3_done"), sem("xt_mm"), sem("xt_cp"), sem("carry"), sem("dx_done")
        mix_done, mh_done, ml_done = sem("mix_done"), sem("mh_done"), sem("ml_done")
        k_mm, rl_done, ah_done, a32_done, al_done = sem("k3_mm"), sem("rl_done"), sem("ah_done"), sem("a32_done"), sem("al_done")
        r_mm, gate_done, v_mm, gv_done, res_done, out_st = sem("r3_mm"), sem("gate_done"), sem("v3_mm"), sem("gv_done"), sem("res_done"), sem("out_st")

        x1_t = d["x1"].rearrange("(n j p) d -> n p j d", p=P, j=T3)
        out_t = d["out"].rearrange("(n j p) d -> n p j d", p=P, j=T3)
        LAST = B * TPB3 - 1

        def steps(eng, step):
            with eng.Fori(0, B - 1) as b:
                for i in range(TPB3):
                    step(b * TPB3 + i, i)
            for i in range(TPB3):
                step((B - 1) * TPB3 + i, i)

        with nc.Block() as block:
            @block.sync
            def _(sp):
                sp.dma_start(mu["r"][:, :], d["mu_r"].rearrange("(c p) -> p c", p=P), allow_slow_non_contiguous=True).then_inc(mu_in, 16)
                sp.dma_start(mu["k"][:, :], d["mu_k"].rearrange("(c p) -> p c", p=P), allow_slow_non_contiguous=True).then_inc(mu_in, 16)
                for i in (1, 2):
                    sp.dma_start(x1[i][:, :, :], x1_t[i]).then_inc(x1_in[i], 16)

                def step(n, i):
                    if not (type(n) is int and n + 3 > LAST):
                        sp.wait_ge(res_done, n * T3 + ONE)
                        sp.dma_start(x1[(i + 3) % TPB3][:, :, :], x1_t[n + 3]).then_inc(x1_in[(i + 3) % TPB3], 16)
                    if type(n) is int and n == LAST:
                        for j in range(T3):
                            sp.wait_ge(res_done, n * T3 + j + 1 + ONE)
                            sp.dma_start(out_t[n][:, j, :], res[:, j, :]).then_inc(out_st, 16)
                    else:
                        sp.wait_ge(res_done, n * T3 + T3 + ONE)
                        sp.dma_start(out_t[n], res[:, :, :]).then_inc(out_st, 16)

                steps(sp, step)
                sp.wait_ge(out_st, 16 * (LAST + T3) + 16)

            @block.tensor
            def _(pe):
                def weight(n):
                    if n >= 10:
                        pe.wait_ge(wl_done, n - 9)
                    elif n >= 6:
                        pe.wait_ge(wl_done, n - 3)
                    for o in range(DC):
                        last = nc.tensor.transpose(wbanks[n][:, o * P:(o + 1) * P],
                                                   wraw[:, n // DC, o, (n % DC) * P:(n % DC + 1) * P], ident[:, :])
                    last.then_inc(wt_mm, 1)

                def transposes(n):
                    for c in range(DC):
                        if c < 2:
                            pe.wait_ge(xt_cp, DC * n)
                        else:
                            pe.wait_ge(xt_cp, DC * n + c - 1)
                        for j in range(T3):
                            if c == 0:
                                pe.wait_ge(xn_done, T3 * n + j + 1)
                            last = nc.tensor.transpose(pt[c % 2][:, j * P:(j + 1) * P], xn[:, j, c * P:(c + 1) * P], ident[:, :])
                        last.then_inc(xt_mm, 1)

                for n in range(DC * len(W)):
                    weight(n)
                transposes(0)
                pe.wait_ge(wl_done, DC * len(W))

                def step(n, i):
                    for c in range(DC):
                        pe.wait_ge(rl_done, DC * n + c - 2 + 1 + 2)
                        for k in range(DC):
                            if c == 0:
                                pe.wait_ge(ml_done, 2 * DC * n + k + 1)
                            last = split_passes(nc, pk[c % 2][:, :], w_h["W_k"][:, k, c * P:(c + 1) * P],
                                                w_l["W_k"][:, k, c * P:(c + 1) * P], m_h["k"][:, k, :], m_l["k"][:, k, :],
                                                k == 0, k == DC - 1)
                        last.then_inc(k_mm, 1)
                    for j in range(T3):
                        if j == 0:
                            pe.wait_ge(gv_done, T3 * n + ONE)
                            pe.wait_ge(ml_done, 2 * DC * n + 2 * DC)
                        w = slice(j * P, (j + 1) * P)
                        for k in range(DC):
                            last = split_passes(nc, pr[j][:, :], m_h["r"][:, k, w], m_l["r"][:, k, w],
                                                w_h["W_r"][:, k, :], w_l["W_r"][:, k, :], k == 0, k == DC - 1)
                        last.then_inc(r_mm, 1)
                    if not (type(n) is int and n == LAST):
                        transposes(n + 1)
                    for j in range(T3):
                        pe.wait_ge(gate_done, T3 * n + j + 1)
                        if j == 0:
                            pe.wait_ge(al_done, DC * n + DC + 2)
                        w = slice(j * P, (j + 1) * P)
                        for k in range(DC):
                            last = split_passes(nc, pr[j][:, :], a_h[:, k, w], a_l[:, k, w],
                                                w_h["W_v"][:, k, :], w_l["W_v"][:, k, :], k == 0, k == DC - 1)
                        last.then_inc(v_mm, 1)

                steps(pe, step)

            @block.scalar
            def _(act):
                act.sem_inc(rl_done, 2)

                def weight_hi(n):
                    act.wait_ge(wt_mm, n + 1)
                    nc.scalar.activation(w_h[W[n // DC]][:, n % DC, :], wbanks[n][:, :], ACT.Identity).then_inc(wh_done, 1)

                def normalise(n, buf, j):
                    if j == 0:
                        act.wait_ge(rstd_done, n + 1)
                        act.wait_ge(xt_mm, DC * n)
                    nc.scalar.activation(xn[:, j, :], x1[buf][:, j, :], ACT.Identity, bias=nmr[:, j:j + 1],
                                         scale=rstd[:, j:j + 1]).then_inc(xn_done, 1)

                def xt_copy(n):
                    act.wait_ge(carry, n + 1)
                    for c in range(DC):
                        act.wait_ge(xt_mm, DC * n + c + 1)
                        nc.scalar.activation(xt[:, c, 1:1 + N3], pt[c % 2][:, :], ACT.Identity).then_inc(xt_cp, 1)

                def mix_hi(n, which):
                    name = "kr"[which]
                    for c in range(DC):
                        at = 2 * DC * n + DC * which + c
                        act.wait_ge(mix_done, at + 1)
                        nc.scalar.activation(m_h[name][:, c, :], mix[:, c % 2, :], ACT.Identity).then_inc(mh_done, 1)

                for n in range(5):
                    weight_hi(n)
                for j in range(T3):
                    normalise(0, 0, j)
                for n in range(5, DC * len(W)):
                    weight_hi(n)
                xt_copy(0)
                mix_hi(0, 0)
                mix_hi(0, 1)

                def step(n, i):
                    more = not (type(n) is int and n == LAST)
                    for c in range(DC):
                        act.wait_ge(k_mm, DC * n + c + 1)
                        act.wait_ge(al_done, DC * n + c - 2 + 1 + 2)
                        nc.scalar.activation(rl[:, c % 2, :], pk[c % 2][:, :], ACT.Relu).then_inc(rl_done, 1)
                        act.wait_ge(rl_done, DC * n + c + 1 + 2)
                        nc.scalar.activation(a_h[:, c, :], rl[:, c % 2, :], ACT.Square).then_inc(ah_done, 1)
                        if more:
                            normalise(n + 1, (i + 1) % TPB3, c)
                    for j in range(T3):
                        act.wait_ge(r_mm, T3 * n + j + 1)
                        nc.scalar.activation(gate[:, j, :], pr[j][:, :], ACT.Sigmoid).then_inc(gate_done, 1)
                    if more:
                        xt_copy(n + 1)
                        mix_hi(n + 1, 0)
                        mix_hi(n + 1, 1)

                steps(act, step)

            @block.gpsimd
            def _(pool):
                def differences(n):
                    pool.wait_ge(ml_done, 2 * DC * n)
                    for c in range(DC):
                        pool.wait_ge(xt_cp, DC * n + c + 1)
                        nc.gpsimd.tensor_tensor(dx[:, c, :], xt[:, c, 1:1 + N3], xt[:, c, 0:N3], ALU.subtract).then_inc(dx_done, 1)

                def rsqrt_seed(n):
                    pool.wait_ge(var_ready, n + 1)
                    nc.gpsimd.tensor_tensor(y0[:, :], ve[:, :], power[:, :], ALU.pow).then_inc(y0_done, 1)

                nc.gpsimd.memset(power[:, :], -0.5).then_inc(power_set, 1)
                pool.wait_ge(power_set, 1)
                rsqrt_seed(0)
                differences(0)
                rsqrt_seed(1)

                def step(n, i):
                    if not (type(n) is int and n + 2 > LAST):
                        rsqrt_seed(n + 2)
                    if not (type(n) is int and n == LAST):
                        differences(n + 1)
                    last = type(n) is int and n == LAST
                    for j in range(T3 - 1 if last else T3):
                        pool.wait_ge(gv_done, T3 * n + j + 1 + ONE)
                        nc.gpsimd.tensor_tensor(res[:, j, :], res[:, j, :], x1[i][:, j, :], ALU.add).then_inc(res_done, 1)

                steps(pool, step)

            @block.vector
            def _(dve):
                dve.sem_inc(al_done, 2)
                dve.sem_inc(res_done, ONE)
                dve.sem_inc(gv_done, ONE)
                dve.sem_inc(out_st, 16)
                dve.sem_inc(x1_in[0], 16)

                def statistics(n, buf):
                    loads = (n - buf) * (16 // TPB3) + 16
                    dve.wait_ge(x1_in[buf], loads)
                    for j in range(T3):
                        nc.vector.bn_stats(st[:, j, :], x1[buf][:, j, :]).then_inc(stats, 1)
                    dve.drain()
                    for j in range(T3):
                        nc.vector.bn_aggr(mv[:, j, :], st[:, j, :]).then_inc(stats, 1)
                    dve.wait_ge(stats, 2 * T3 * n + 2 * T3)
                    nc.vector.tensor_scalar(ve[:, :], mv[:, :, 1], EPS, None, ALU.add).then_inc(var_ready, 1)

                def rstd_newton(n):
                    dve.wait_ge(y0_done, n + 1)
                    nc.vector.tensor_tensor(ya[:, :], y0[:, :], y0[:, :], ALU.mult).then_inc(newton, 1)
                    dve.wait_ge(newton, 4 * n + 1)
                    nc.vector.tensor_tensor(ya[:, :], ya[:, :], ve[:, :], ALU.mult).then_inc(newton, 1)
                    dve.wait_ge(newton, 4 * n + 2)
                    nc.vector.tensor_scalar(ya[:, :], ya[:, :], -0.5, 1.5, ALU.mult, ALU.add).then_inc(newton, 1)
                    dve.wait_ge(newton, 4 * n + 3)
                    nc.vector.tensor_tensor(rstd[:, :], ya[:, :], y0[:, :], ALU.mult).then_inc(newton, 1)
                    dve.wait_ge(newton, 4 * n + 4)
                    nc.vector.scalar_tensor_tensor(nmr[:, :], mv[:, :, 0], -1.0, rstd[:, :], ALU.mult, ALU.mult).then_inc(rstd_done, 1)

                def weight_lo(n):
                    dve.wait_ge(wh_done, n + 1)
                    nc.vector.tensor_tensor(w_l[W[n // DC]][:, n % DC, :], wbanks[n][:, :], w_h[W[n // DC]][:, n % DC, :],
                                            ALU.subtract).then_inc(wl_done, 1)

                statistics(0, 0)
                weight_lo(0)
                rstd_newton(0)
                for n in range(1, DC * len(W)):
                    weight_lo(n)

                def keep_last(n, first_of_batch):
                    dve.wait_ge(dx_done, DC * n)
                    if first_of_batch:
                        nc.vector.memset(xt[:, :, 0:1], 0.0).then_inc(carry, 1)
                    else:
                        nc.vector.tensor_copy(xt[:, :, 0:1], xt[:, :, N3:N3 + 1]).then_inc(carry, 1)

                def mixes(n, which):
                    name = "kr"[which]
                    if which:
                        dve.wait_ge(r_mm, T3 * n)
                    else:
                        dve.wait_ge(k_mm, DC * n)

                    def lo(c):
                        at = 2 * DC * n + DC * which + c
                        dve.wait_ge(mh_done, at + 1)
                        nc.vector.tensor_tensor(m_l[name][:, c, :], mix[:, c % 2, :], m_h[name][:, c, :], ALU.subtract).then_inc(ml_done, 1)

                    for c in range(DC):
                        if which == 0:
                            dve.wait_ge(dx_done, DC * n + c + 1)
                        if c >= 2:
                            lo(c - 2)
                        if not (type(n) is int and n == 0 and which == 0 and c < 2):
                            dve.wait_ge(ml_done, 2 * DC * n + DC * which + c - 1)
                        nc.vector.scalar_tensor_tensor(mix[:, c % 2, :], dx[:, c, :], mu[name][:, c:c + 1], xt[:, c, 0:N3],
                                                       ALU.mult, ALU.add).then_inc(mix_done, 1)
                    lo(DC - 2)
                    lo(DC - 1)

                dve.wait_ge(mu_in, 32)
                keep_last(0, True)
                dve.wait_ge(xn_done, T3)
                statistics(1, 1)
                mixes(0, 0)
                mixes(0, 1)
                rstd_newton(1)

                def step(n, i):
                    for c in range(DC):
                        dve.wait_ge(rl_done, DC * n + c + 1 + 2)
                        nc.vector.tensor_tensor(a32[:, c % 2, :], rl[:, c % 2, :], rl[:, c % 2, :], ALU.mult).then_inc(a32_done, 1)
                        dve.wait_ge(a32_done, DC * n + c + 1)
                        dve.wait_ge(ah_done, DC * n + c + 1)
                        nc.vector.tensor_tensor(a_l[:, c, :], a32[:, c % 2, :], a_h[:, c, :], ALU.subtract).then_inc(al_done, 1)
                    if not (type(n) is int and n + 2 > LAST):
                        dve.wait_ge(xn_done, T3 * n + 2 * T3)
                        statistics(n + 2, (i + 2) % TPB3)
                        rstd_newton(n + 2)
                    if not (type(n) is int and n == LAST):
                        keep_last(n + 1, i == TPB3 - 1)
                        mixes(n + 1, 0)
                        mixes(n + 1, 1)
                    for j in range(T3):
                        if j == 0:
                            dve.wait_ge(out_st, 16 * n + 16)
                        dve.wait_ge(v_mm, T3 * n + j + 1)
                        nc.vector.tensor_tensor(res[:, j, :], pr[j][:, :], gate[:, j, :], ALU.mult).then_inc(gv_done, 1)

                steps(dve, step)
                dve.wait_ge(gv_done, T3 * (LAST + 1) + ONE)
                dve.wait_ge(res_done, T3 * (LAST + 1) - 1 + ONE)
                nc.vector.tensor_tensor(res[:, T3 - 1, :], res[:, T3 - 1, :], x1[TPB3 - 1][:, T3 - 1, :], ALU.add).then_inc(res_done, 1)


def build(nc, x, ctx, mask, Wq, bq, Wk, bk, Wv, bv, Wo, bo, W_r, W_k, W_v, mu_r, mu_k, ident, ramp, ramp_col, out):
    d = dict(ctx=ctx, mask=mask, Wq=Wq, bq=bq, Wk=Wk, bk=bk, Wv=Wv, bv=bv, Wo=Wo, bo=bo, W_r=W_r, W_k=W_k, W_v=W_v,
             mu_r=mu_r, mu_k=mu_k, ident=ident, ramp=ramp, ramp_col=ramp_col,
             x=x.rearrange("b s d -> (b s) d"), out=out.rearrange("b s d -> (b s) d"))
    d["x1"] = nc.dram_tensor("x1_scratch", [B * S, D], F32).ap()
    d["fill"] = nc.dram_tensor("fill_scratch", [2, 2 * 512], F32).ap()
    for n in ("k_h", "k_l"):
        d[n] = nc.dram_tensor(f"{n}_scratch", [P, PAIRS, B * KEYS], F32).ap()
    for n in ("v_h", "v_l"):
        d[n] = nc.dram_tensor(f"{n}_scratch", [P, B, HD], F32).ap()
    with ExitStack() as c:
        def sb(name, shape, dt=F32):
            return c.enter_context(nc.sbuf_tensor(name, shape, dt))
        t = dict(ident=sb("ident", [P, P]), rows=sb("rows", [P, T3, D]), 
                 small=sb("small", [P, 14, TT]))
        t["wraw_at"] = -(-nc.sbuf_base // 32) * 32
        t["wraw"] = sb("wraw", [P, 3, DC * D])
        t["xa"], t["xn"] = t["rows"][:, 0:TT, :], t["rows"][:, TT:2 * TT, :]
        for n in ("xa_in", "xt_done", "stats", "var_ready", "ln_y0", "newton", "rstd_step", "rstd_ready", "xn_ready"):
            t[n] = c.enter_context(nc.semaphore(n))
        with ExitStack() as c2:
            def sb2(name, shape, dt=F32):
                return c2.enter_context(nc.sbuf_tensor(name, shape, dt))
            t.update(wq_h=sb2("wq_h", [P, DC, HD], F32R), wq_l=sb2("wq_l", [P, DC, HD], F32R),
                     wo_h=sb2("wo_h", [P, PAIRS, D], F32R), wo_l=sb2("wo_l", [P, PAIRS, D], F32R),
                     bq_col=sb2("bq_col", [P, PAIRS]), bo_row=sb2("bo_row", [P, D]), mask_bias=sb2("mask_bias", [P, B]))
            part1(nc, t, d)
            part2(nc, t, d)
        part3(nc, t, d)


_INS = ['x', 'ctx_1024', 'mask_BxS2_bf1', 'L0_xattn_Wq', 'L0_xattn_bq', 'L0_xattn_Wk', 'L0_xattn_bk', 'L0_xattn_Wv',
        'L0_xattn_bv', 'L0_xattn_Wo', 'L0_xattn_bo', 'L0_ffn_W_r', 'L0_ffn_W_k', 'L0_ffn_W_v', 'L0_ffn_mu_r', 'L0_ffn_mu_k']


def kernel(**inputs):
    import concourse.bacc as bacc
    from concourse.bass_utils import run_bass_kernel_spmd

    nc = bacc.Bacc("TRN2", target_bir_lowering=False, num_devices=1)
    given = [(n, np.ascontiguousarray(inputs[n])) for n in _INS]
    down = (KEYS - np.arange(KEYS)).astype(np.float32)
    given += [("ident", np.eye(P, dtype=np.float32)), ("ramp", np.tile(down, (P, 1))), ("ramp_col", down[:, None].copy())]
    arrays, args = {}, []
    for name, a in given:
        arrays[f"in_{name}_dram"] = a
        args.append(nc.dram_tensor(f"in_{name}_dram", a.shape, mybir.dt.from_np(a.dtype), kind="ExternalInput").ap())
    args.append(nc.dram_tensor("out_0_dram", (B, S, D), F32, kind="ExternalOutput").ap())
    build(nc, *args)
    r = run_bass_kernel_spmd(nc, [arrays], core_ids=[0])
    return r.results[0]["out_0_dram"]
```
